# Optimizing a Trainium2 kernel written in Bass

```python
import numpy as np
import jax
import jax.numpy as jnp

def _softmax(x, axis=-1):
    return jax.nn.softmax(x, axis=axis)

def _gelu(x):
    return jax.nn.gelu(x, approximate=True)

def _silu(x):
    return jax.nn.silu(x)

def _sigmoid(x):
    return jax.nn.sigmoid(x)

def _layernorm(x, axis=-1, eps=1e-05):
    m = jnp.mean(x, axis=axis, keepdims=True)
    v = jnp.var(x, axis=axis, keepdims=True)
    return (x - m) / jnp.sqrt(v + eps)

def _scatter_add(tgt, idx, src, axis=0):
    return tgt.at[idx].add(src)

def _segment_sum(src, seg, n):
    return jax.ops.segment_sum(src, seg, n)
kernel_name = 'mk_xattn_seq_d4_seqx_r4_c736e4'

def setup_inputs(seed: int=0):
    np.random.seed(seed)
    _w = jnp.asarray

    def _rec_inputs():
        import jax
        import jax.numpy as jnp
        _rk = jax.random.key(seed)
        x = 7.22e-05 + 1 * jax.random.normal(jax.random.fold_in(_rk, 1), (8, 512, 256), jnp.float32)
        _lenS = 512 - jax.random.randint(jax.random.fold_in(_rk, 7), (8,), 0, max(1, 512 // 4) + 1, jnp.int32)
        _lenS2 = 512 - jax.random.randint(jax.random.fold_in(_rk, 8), (8,), 0, max(1, 512 // 4) + 1, jnp.int32)
        _ctx_1024P = jax.random.normal(jax.random.fold_in(_rk, 11), (8, 16, 256), jnp.float32)
        _ctx_1024c = jax.random.dirichlet(jax.random.fold_in(_rk, 511), 0.3 * jnp.ones((16,), jnp.float32), (8, 512))
        _ctx_1024t = jnp.einsum('bsk,bkd->bsd', _ctx_1024c, _ctx_1024P)
        _ctx_1024t = _ctx_1024t * jax.lax.rsqrt(jnp.mean(jnp.square(_ctx_1024t)) + 1e-12) * 0.953939
        ctx_1024 = -0.000431507 + 0.999848 * (_ctx_1024t + 0.3 * jax.random.normal(jax.random.fold_in(_rk, 611), (8, 512, 256), jnp.float32))
        _validS = jnp.arange(512)[None, :] < _lenS[:, None]
        _validS2 = jnp.arange(512)[None, :] < _lenS2[:, None]
        _causal = jnp.tril(jnp.ones((512, 512), dtype=bool))
        mask_SxS_fc0 = jnp.where(jnp.broadcast_to(_causal[:, :], (512, 512)), 0.0, -1000000000.0).astype(jnp.float32)
        return (x, ctx_1024, mask_SxS_fc0)
    x, ctx_1024, mask_SxS_fc0 = _rec_inputs()

    def _L0_xattn_setup():
        import jax, jax.numpy as jnp
        import numpy as np
        B, S, E, H, T, R = (8, 256, 256, 16, 196, 4)
        HD = E // H
        EPS = 1e-05

        def _ln(x, g, b):
            mu = jnp.mean(x, axis=-1, keepdims=True)
            var = jnp.mean(jnp.square(x - mu), axis=-1, keepdims=True)
            return (x - mu) * jax.lax.rsqrt(var + EPS) * g + b

        def _lin(x, w, b):
            return jnp.einsum('bse,oe->bso', x, w) + b

        def _heads(t):
            b, s, _ = t.shape
            return t.reshape(b, s, H, HD).transpose(0, 2, 1, 3)

        def _attend(q, k, v, causal):
            scale = HD ** (-0.5)
            scores = jnp.einsum('bhqd,bhkd->bhqk', q, k) * scale
            if causal:
                sq, sk = (scores.shape[-2], scores.shape[-1])
                mask = jnp.tril(jnp.ones((sq, sk), bool))
                scores = jnp.where(mask, scores, -jnp.inf)
            w = jax.nn.softmax(scores, axis=-1)
            out = jnp.einsum('bhqk,bhkd->bhqd', w, v)
            b, h, s, d = out.shape
            return out.transpose(0, 2, 1, 3).reshape(b, s, h * d)
        key = jax.random.key(seed)
        ks = jax.random.split(key, 12)
        w = lambda k, shape: jax.random.normal(k, shape, jnp.float32) * 0.02
        return {'x': jax.random.normal(ks[0], (B, S, E), jnp.float32), 'enc_out': jax.random.normal(ks[1], (B, T, E), jnp.float32), 'ln1_g': jnp.ones(E), 'ln1_b': jnp.zeros(E), 'attn_qkv_w': w(ks[2], (3 * E, E)), 'attn_qkv_b': jnp.zeros(3 * E), 'attn_proj_w': w(ks[3], (E, E)), 'attn_proj_b': jnp.zeros(E), 'ln2_g': jnp.ones(E), 'ln2_b': jnp.zeros(E), 'q_w': w(ks[4], (E, E)), 'q_b': jnp.zeros(E), 'k_w': w(ks[5], (E, E)), 'k_b': jnp.zeros(E), 'v_w': w(ks[6], (E, E)), 'v_b': jnp.zeros(E), 'ca_proj_w': w(ks[7], (E, E)), 'ca_proj_b': jnp.zeros(E), 'ln3_g': jnp.ones(E), 'ln3_b': jnp.zeros(E), 'fc_w': w(ks[8], (R * E, E)), 'fc_b': jnp.zeros(R * E), 'proj_w': w(ks[9], (E, R * E)), 'proj_b': jnp.zeros(E)}
    _L0_xattn_all = _L0_xattn_setup()
    _L0_xattn_in = {k: v for k, v in _L0_xattn_all.items() if k in ('ln1_g', 'ln1_b', 'attn_qkv_w', 'attn_qkv_b', 'attn_proj_w', 'attn_proj_b', 'ln2_g', 'ln2_b', 'q_w', 'q_b', 'k_w', 'k_b', 'v_w', 'v_b', 'ca_proj_w', 'ca_proj_b', 'ln3_g', 'ln3_b', 'fc_w', 'fc_b', 'proj_w', 'proj_b')}
    del _L0_xattn_all

    def _L1_xattn_setup():
        import jax, jax.numpy as jnp
        import numpy as np
        D_MODEL = 256
        NUM_HEADS = 16
        HEAD_DIM = D_MODEL // NUM_HEADS
        SCALE = HEAD_DIM ** (-0.5)
        LN_EPS = 1e-05
        Q_EPS = 1e-05

        def bit_quant(W):
            gamma = jnp.mean(jnp.abs(W))
            Wq = jnp.clip(jnp.round(W / (gamma + Q_EPS)), -1.0, 1.0) * gamma
            return W + jax.lax.stop_gradient(Wq - W)

        def layer_norm(x, gamma, beta):
            mu = jnp.mean(x, axis=-1, keepdims=True)
            var = jnp.mean(jnp.square(x - mu), axis=-1, keepdims=True)
            return (x - mu) * jax.lax.rsqrt(var + LN_EPS) * gamma + beta
        key = jax.random.key(seed)
        ks = jax.random.split(key, 8)
        B, T, T_ctx, C = (4, 256, 512, D_MODEL)
        w_std = C ** (-0.5)
        return {'x': jax.random.normal(ks[0], (B, T, C), jnp.float32), 'context': jax.random.normal(ks[1], (B, T_ctx, C), jnp.float32), 'Wq': jax.random.normal(ks[2], (C, C), jnp.float32) * w_std, 'bq': jnp.zeros((C,), jnp.float32), 'Wk': jax.random.normal(ks[3], (C, C), jnp.float32) * w_std, 'bk': jnp.zeros((C,), jnp.float32), 'Wv': jax.random.normal(ks[4], (C, C), jnp.float32) * w_std, 'bv': jnp.zeros((C,), jnp.float32), 'Wo': jax.random.normal(ks[5], (C, C), jnp.float32) * w_std, 'bo': jnp.zeros((C,), jnp.float32), 'ln_gamma': jnp.ones((C,), jnp.float32), 'ln_beta': jnp.zeros((C,), jnp.float32)}
    _L1_xattn_all = _L1_xattn_setup()
    _L1_xattn_in = {k: v for k, v in _L1_xattn_all.items() if k in ('Wq', 'bq', 'Wk', 'bk', 'Wv', 'bv', 'Wo', 'bo', 'ln_gamma', 'ln_beta')}
    del _L1_xattn_all

    def _L2_xattn_setup():
        import jax, jax.numpy as jnp
        import numpy as np
        B, QL, KVL = (4, 256, 375)
        D, H, MLP = (256, 16, 1024)
        DH = D // H
        EPS = 1e-05
        NEG = -1000000000.0

        def layernorm(x, w, b):
            m = jnp.mean(x, axis=-1, keepdims=True)
            v = jnp.mean((x - m) ** 2, axis=-1, keepdims=True)
            return (x - m) / jnp.sqrt(v + EPS) * w + b

        def gelu_exact(x):
            return x * 0.5 * (1.0 + jax.lax.erf(x * np.float32(0.7071067811865476)))

        def mha(xq, xkv, qw, qb, kw, vw, vb, ow, ob, mask=None):
            nb, ql = (xq.shape[0], xq.shape[1])
            kl = xkv.shape[1]
            q = xq @ qw.T + qb
            k = xkv @ kw.T
            v = xkv @ vw.T + vb
            scale = np.float32(DH ** (-0.25))
            q = q.reshape(nb, ql, H, DH) * scale
            k = k.reshape(nb, kl, H, DH) * scale
            v = v.reshape(nb, kl, H, DH)
            logits = jnp.einsum('bqhd,bkhd->bhqk', q, k)
            if mask is not None:
                logits = logits + mask[:ql, :kl]
            p = jax.nn.softmax(logits, axis=-1)
            o = jnp.einsum('bhqk,bkhd->bqhd', p, v).reshape(nb, ql, H * DH)
            return o @ ow.T + ob
        key = jax.random.key(seed)
        ks = jax.random.split(key, 20)
        s = 0.02
        inp = {'x': jax.random.normal(ks[0], (B, QL, D), jnp.float32), 'xa': jax.random.normal(ks[1], (B, KVL, D), jnp.float32), 'mask': jnp.where(jnp.tril(jnp.ones((QL, QL), bool)), 0.0, NEG).astype(jnp.float32), 'attn_ln_w': jnp.ones((D,), jnp.float32), 'attn_ln_b': jnp.zeros((D,), jnp.float32), 'q_w': jax.random.normal(ks[2], (D, D), jnp.float32) * s, 'q_b': jnp.zeros((D,), jnp.float32), 'k_w': jax.random.normal(ks[3], (D, D), jnp.float32) * s, 'v_w': jax.random.normal(ks[4], (D, D), jnp.float32) * s, 'v_b': jnp.zeros((D,), jnp.float32), 'o_w': jax.random.normal(ks[5], (D, D), jnp.float32) * s, 'o_b': jnp.zeros((D,), jnp.float32), 'cross_ln_w': jnp.ones((D,), jnp.float32), 'cross_ln_b': jnp.zeros((D,), jnp.float32), 'cq_w': jax.random.normal(ks[6], (D, D), jnp.float32) * s, 'cq_b': jnp.zeros((D,), jnp.float32), 'ck_w': jax.random.normal(ks[7], (D, D), jnp.float32) * s, 'cv_w': jax.random.normal(ks[8], (D, D), jnp.float32) * s, 'cv_b': jnp.zeros((D,), jnp.float32), 'co_w': jax.random.normal(ks[9], (D, D), jnp.float32) * s, 'co_b': jnp.zeros((D,), jnp.float32), 'mlp_ln_w': jnp.ones((D,), jnp.float32), 'mlp_ln_b': jnp.zeros((D,), jnp.float32), 'fc1_w': jax.random.normal(ks[10], (MLP, D), jnp.float32) * s, 'fc1_b': jnp.zeros((MLP,), jnp.float32), 'fc2_w': jax.random.normal(ks[11], (D, MLP), jnp.float32) * s, 'fc2_b': jnp.zeros((D,), jnp.float32)}
        return inp
    _L2_xattn_all = _L2_xattn_setup()
    _L2_xattn_in = {k: v for k, v in _L2_xattn_all.items() if k in ('attn_ln_w', 'attn_ln_b', 'q_w', 'q_b', 'k_w', 'v_w', 'v_b', 'o_w', 'o_b', 'cross_ln_w', 'cross_ln_b', 'cq_w', 'cq_b', 'ck_w', 'cv_w', 'cv_b', 'co_w', 'co_b', 'mlp_ln_w', 'mlp_ln_b', 'fc1_w', 'fc1_b', 'fc2_w', 'fc2_b')}
    del _L2_xattn_all

    def _L3_xattn_setup():
        import jax, jax.numpy as jnp
        import numpy as np
        B, T, E = (4, 512, 256)
        H, HS = (16, 64)
        EPS = 1e-05

        def _layernorm(x, g, b):
            mu = jnp.mean(x, axis=-1, keepdims=True)
            var = jnp.mean(jnp.square(x - mu), axis=-1, keepdims=True)
            return (x - mu) * jax.lax.rsqrt(var + EPS) * g + b
        key = jax.random.key(seed)
        ks = jax.random.split(key, 8)
        q = jax.random.normal(ks[0], (B, T, E), dtype=jnp.float32)
        s_in = 1.0 / np.sqrt(E)
        s_o = 1.0 / np.sqrt(H * HS)
        return {'q': q, 'kv': q, 'ln_g': jnp.ones((E,), jnp.float32), 'ln_b': jnp.zeros((E,), jnp.float32), 'wq': jax.random.uniform(ks[1], (E, H * HS), jnp.float32, -s_in, s_in), 'bq': jax.random.uniform(ks[2], (H * HS,), jnp.float32, -s_in, s_in), 'wkv': jax.random.uniform(ks[3], (E, 2 * H * HS), jnp.float32, -s_in, s_in), 'bkv': jax.random.uniform(ks[4], (2 * H * HS,), jnp.float32, -s_in, s_in), 'wo': jax.random.uniform(ks[5], (H * HS, E), jnp.float32, -s_o, s_o), 'bo': jax.random.uniform(ks[6], (E,), jnp.float32, -s_o, s_o)}
    _L3_xattn_all = _L3_xattn_setup()
    _L3_xattn_in = {k: v for k, v in _L3_xattn_all.items() if k in ('ln_g', 'ln_b', 'wq', 'bq', 'wkv', 'bkv', 'wo', 'bo')}
    del _L3_xattn_all
    return {'x': x, 'ctx_1024': ctx_1024, 'mask_SxS_fc0': mask_SxS_fc0, 'L0_xattn_ln1_g': _L0_xattn_in['ln1_g'], 'L0_xattn_ln1_b': _L0_xattn_in['ln1_b'], 'L0_xattn_attn_qkv_w': _L0_xattn_in['attn_qkv_w'], 'L0_xattn_attn_qkv_b': _L0_xattn_in['attn_qkv_b'], 'L0_xattn_attn_proj_w': _L0_xattn_in['attn_proj_w'], 'L0_xattn_attn_proj_b': _L0_xattn_in['attn_proj_b'], 'L0_xattn_ln2_g': _L0_xattn_in['ln2_g'], 'L0_xattn_ln2_b': _L0_xattn_in['ln2_b'], 'L0_xattn_q_w': _L0_xattn_in['q_w'], 'L0_xattn_q_b': _L0_xattn_in['q_b'], 'L0_xattn_k_w': _L0_xattn_in['k_w'], 'L0_xattn_k_b': _L0_xattn_in['k_b'], 'L0_xattn_v_w': _L0_xattn_in['v_w'], 'L0_xattn_v_b': _L0_xattn_in['v_b'], 'L0_xattn_ca_proj_w': _L0_xattn_in['ca_proj_w'], 'L0_xattn_ca_proj_b': _L0_xattn_in['ca_proj_b'], 'L0_xattn_ln3_g': _L0_xattn_in['ln3_g'], 'L0_xattn_ln3_b': _L0_xattn_in['ln3_b'], 'L0_xattn_fc_w': _L0_xattn_in['fc_w'], 'L0_xattn_fc_b': _L0_xattn_in['fc_b'], 'L0_xattn_proj_w': _L0_xattn_in['proj_w'], 'L0_xattn_proj_b': _L0_xattn_in['proj_b'], 'L1_xattn_Wq': _L1_xattn_in['Wq'], 'L1_xattn_bq': _L1_xattn_in['bq'], 'L1_xattn_Wk': _L1_xattn_in['Wk'], 'L1_xattn_bk': _L1_xattn_in['bk'], 'L1_xattn_Wv': _L1_xattn_in['Wv'], 'L1_xattn_bv': _L1_xattn_in['bv'], 'L1_xattn_Wo': _L1_xattn_in['Wo'], 'L1_xattn_bo': _L1_xattn_in['bo'], 'L1_xattn_ln_gamma': _L1_xattn_in['ln_gamma'], 'L1_xattn_ln_beta': _L1_xattn_in['ln_beta'], 'L2_xattn_attn_ln_w': _L2_xattn_in['attn_ln_w'], 'L2_xattn_attn_ln_b': _L2_xattn_in['attn_ln_b'], 'L2_xattn_q_w': _L2_xattn_in['q_w'], 'L2_xattn_q_b': _L2_xattn_in['q_b'], 'L2_xattn_k_w': _L2_xattn_in['k_w'], 'L2_xattn_v_w': _L2_xattn_in['v_w'], 'L2_xattn_v_b': _L2_xattn_in['v_b'], 'L2_xattn_o_w': _L2_xattn_in['o_w'], 'L2_xattn_o_b': _L2_xattn_in['o_b'], 'L2_xattn_cross_ln_w': _L2_xattn_in['cross_ln_w'], 'L2_xattn_cross_ln_b': _L2_xattn_in['cross_ln_b'], 'L2_xattn_cq_w': _L2_xattn_in['cq_w'], 'L2_xattn_cq_b': _L2_xattn_in['cq_b'], 'L2_xattn_ck_w': _L2_xattn_in['ck_w'], 'L2_xattn_cv_w': _L2_xattn_in['cv_w'], 'L2_xattn_cv_b': _L2_xattn_in['cv_b'], 'L2_xattn_co_w': _L2_xattn_in['co_w'], 'L2_xattn_co_b': _L2_xattn_in['co_b'], 'L2_xattn_mlp_ln_w': _L2_xattn_in['mlp_ln_w'], 'L2_xattn_mlp_ln_b': _L2_xattn_in['mlp_ln_b'], 'L2_xattn_fc1_w': _L2_xattn_in['fc1_w'], 'L2_xattn_fc1_b': _L2_xattn_in['fc1_b'], 'L2_xattn_fc2_w': _L2_xattn_in['fc2_w'], 'L2_xattn_fc2_b': _L2_xattn_in['fc2_b'], 'L3_xattn_ln_g': _L3_xattn_in['ln_g'], 'L3_xattn_ln_b': _L3_xattn_in['ln_b'], 'L3_xattn_wq': _L3_xattn_in['wq'], 'L3_xattn_bq': _L3_xattn_in['bq'], 'L3_xattn_wkv': _L3_xattn_in['wkv'], 'L3_xattn_bkv': _L3_xattn_in['bkv'], 'L3_xattn_wo': _L3_xattn_in['wo'], 'L3_xattn_bo': _L3_xattn_in['bo']}

def reference(x, ctx_1024, mask_SxS_fc0, L0_xattn_ln1_g, L0_xattn_ln1_b, L0_xattn_attn_qkv_w, L0_xattn_attn_qkv_b, L0_xattn_attn_proj_w, L0_xattn_attn_proj_b, L0_xattn_ln2_g, L0_xattn_ln2_b, L0_xattn_q_w, L0_xattn_q_b, L0_xattn_k_w, L0_xattn_k_b, L0_xattn_v_w, L0_xattn_v_b, L0_xattn_ca_proj_w, L0_xattn_ca_proj_b, L0_xattn_ln3_g, L0_xattn_ln3_b, L0_xattn_fc_w, L0_xattn_fc_b, L0_xattn_proj_w, L0_xattn_proj_b, L1_xattn_Wq, L1_xattn_bq, L1_xattn_Wk, L1_xattn_bk, L1_xattn_Wv, L1_xattn_bv, L1_xattn_Wo, L1_xattn_bo, L1_xattn_ln_gamma, L1_xattn_ln_beta, L2_xattn_attn_ln_w, L2_xattn_attn_ln_b, L2_xattn_q_w, L2_xattn_q_b, L2_xattn_k_w, L2_xattn_v_w, L2_xattn_v_b, L2_xattn_o_w, L2_xattn_o_b, L2_xattn_cross_ln_w, L2_xattn_cross_ln_b, L2_xattn_cq_w, L2_xattn_cq_b, L2_xattn_ck_w, L2_xattn_cv_w, L2_xattn_cv_b, L2_xattn_co_w, L2_xattn_co_b, L2_xattn_mlp_ln_w, L2_xattn_mlp_ln_b, L2_xattn_fc1_w, L2_xattn_fc1_b, L2_xattn_fc2_w, L2_xattn_fc2_b, L3_xattn_ln_g, L3_xattn_ln_b, L3_xattn_wq, L3_xattn_bq, L3_xattn_wkv, L3_xattn_bkv, L3_xattn_wo, L3_xattn_bo):
    import jax
    import jax.numpy as jnp

    def _L0_xattn_ref(x, enc_out, ln1_g, ln1_b, attn_qkv_w, attn_qkv_b, attn_proj_w, attn_proj_b, ln2_g, ln2_b, q_w, q_b, k_w, k_b, v_w, v_b, ca_proj_w, ca_proj_b, ln3_g, ln3_b, fc_w, fc_b, proj_w, proj_b):
        import jax, jax.numpy as jnp
        import numpy as np
        B, S, E, H, T, R = (8, 256, 256, 16, 196, 4)
        HD = E // H
        EPS = 1e-05

        def _ln(x, g, b):
            mu = jnp.mean(x, axis=-1, keepdims=True)
            var = jnp.mean(jnp.square(x - mu), axis=-1, keepdims=True)
            return (x - mu) * jax.lax.rsqrt(var + EPS) * g + b

        def _lin(x, w, b):
            return jnp.einsum('bse,oe->bso', x, w) + b

        def _heads(t):
            b, s, _ = t.shape
            return t.reshape(b, s, H, HD).transpose(0, 2, 1, 3)

        def _attend(q, k, v, causal):
            scale = HD ** (-0.5)
            scores = jnp.einsum('bhqd,bhkd->bhqk', q, k) * scale
            if causal:
                sq, sk = (scores.shape[-2], scores.shape[-1])
                mask = jnp.tril(jnp.ones((sq, sk), bool))
                scores = jnp.where(mask, scores, -jnp.inf)
            w = jax.nn.softmax(scores, axis=-1)
            out = jnp.einsum('bhqk,bhkd->bhqd', w, v)
            b, h, s, d = out.shape
            return out.transpose(0, 2, 1, 3).reshape(b, s, h * d)
        h = _ln(x, ln1_g, ln1_b)
        qkv = _lin(h, attn_qkv_w, attn_qkv_b)
        q, k, v = jnp.split(qkv, 3, axis=-1)
        a = _attend(_heads(q), _heads(k), _heads(v), causal=True)
        x = x + _lin(a, attn_proj_w, attn_proj_b)
        h = _ln(x, ln2_g, ln2_b)
        q = _heads(_lin(h, q_w, q_b))
        k = _heads(_lin(enc_out, k_w, k_b))
        v = _heads(_lin(enc_out, v_w, v_b))
        a = _attend(q, k, v, causal=False)
        x = x + _lin(a, ca_proj_w, ca_proj_b)
        h = _ln(x, ln3_g, ln3_b)
        h = jax.nn.gelu(_lin(h, fc_w, fc_b), approximate=False)
        x = x + _lin(h, proj_w, proj_b)
        return x

    def _L1_xattn_ref(x, context, Wq, bq, Wk, bk, Wv, bv, Wo, bo, ln_gamma, ln_beta):
        import jax, jax.numpy as jnp
        import numpy as np
        D_MODEL = 256
        NUM_HEADS = 16
        HEAD_DIM = D_MODEL // NUM_HEADS
        SCALE = HEAD_DIM ** (-0.5)
        LN_EPS = 1e-05
        Q_EPS = 1e-05

        def bit_quant(W):
            gamma = jnp.mean(jnp.abs(W))
            Wq = jnp.clip(jnp.round(W / (gamma + Q_EPS)), -1.0, 1.0) * gamma
            return W + jax.lax.stop_gradient(Wq - W)

        def layer_norm(x, gamma, beta):
            mu = jnp.mean(x, axis=-1, keepdims=True)
            var = jnp.mean(jnp.square(x - mu), axis=-1, keepdims=True)
            return (x - mu) * jax.lax.rsqrt(var + LN_EPS) * gamma + beta
        B, T, C = x.shape
        T_ctx = context.shape[1]
        residual = x
        xn = layer_norm(x, ln_gamma, ln_beta)
        q = xn @ bit_quant(Wq).T + bq
        k = context @ bit_quant(Wk).T + bk
        v = context @ bit_quant(Wv).T + bv
        q = q.reshape(B, T, NUM_HEADS, HEAD_DIM)
        k = k.reshape(B, T_ctx, NUM_HEADS, HEAD_DIM)
        v = v.reshape(B, T_ctx, NUM_HEADS, HEAD_DIM)
        scores = jnp.einsum('bqhd,bkhd->bhqk', q, k) * SCALE
        probs = jax.nn.softmax(scores, axis=-1)
        out = jnp.einsum('bhqk,bkhd->bqhd', probs, v).reshape(B, T, C)
        return residual + (out @ bit_quant(Wo).T + bo)

    def _L2_xattn_ref(x, xa, mask, attn_ln_w, attn_ln_b, q_w, q_b, k_w, v_w, v_b, o_w, o_b, cross_ln_w, cross_ln_b, cq_w, cq_b, ck_w, cv_w, cv_b, co_w, co_b, mlp_ln_w, mlp_ln_b, fc1_w, fc1_b, fc2_w, fc2_b):
        import jax, jax.numpy as jnp
        import numpy as np
        B, QL, KVL = (4, 256, 375)
        D, H, MLP = (256, 16, 1024)
        DH = D // H
        EPS = 1e-05
        NEG = -1000000000.0

        def layernorm(x, w, b):
            m = jnp.mean(x, axis=-1, keepdims=True)
            v = jnp.mean((x - m) ** 2, axis=-1, keepdims=True)
            return (x - m) / jnp.sqrt(v + EPS) * w + b

        def gelu_exact(x):
            return x * 0.5 * (1.0 + jax.lax.erf(x * np.float32(0.7071067811865476)))

        def mha(xq, xkv, qw, qb, kw, vw, vb, ow, ob, mask=None):
            nb, ql = (xq.shape[0], xq.shape[1])
            kl = xkv.shape[1]
            q = xq @ qw.T + qb
            k = xkv @ kw.T
            v = xkv @ vw.T + vb
            scale = np.float32(DH ** (-0.25))
            q = q.reshape(nb, ql, H, DH) * scale
            k = k.reshape(nb, kl, H, DH) * scale
            v = v.reshape(nb, kl, H, DH)
            logits = jnp.einsum('bqhd,bkhd->bhqk', q, k)
            if mask is not None:
                logits = logits + mask[:ql, :kl]
            p = jax.nn.softmax(logits, axis=-1)
            o = jnp.einsum('bhqk,bkhd->bqhd', p, v).reshape(nb, ql, H * DH)
            return o @ ow.T + ob
        h = layernorm(x, attn_ln_w, attn_ln_b)
        x = x + mha(h, h, q_w, q_b, k_w, v_w, v_b, o_w, o_b, mask=mask)
        h = layernorm(x, cross_ln_w, cross_ln_b)
        x = x + mha(h, xa, cq_w, cq_b, ck_w, cv_w, cv_b, co_w, co_b, mask=None)
        h = layernorm(x, mlp_ln_w, mlp_ln_b)
        h = gelu_exact(h @ fc1_w.T + fc1_b)
        x = x + (h @ fc2_w.T + fc2_b)
        return x

    def _L3_xattn_ref(q, kv, ln_g, ln_b, wq, bq, wkv, bkv, wo, bo):
        import jax, jax.numpy as jnp
        import numpy as np
        B, T, E = (4, 512, 256)
        H, HS = (16, 64)
        EPS = 1e-05

        def _layernorm(x, g, b):
            mu = jnp.mean(x, axis=-1, keepdims=True)
            var = jnp.mean(jnp.square(x - mu), axis=-1, keepdims=True)
            return (x - mu) * jax.lax.rsqrt(var + EPS) * g + b
        oq = q
        qn = _layernorm(q, ln_g, ln_b)
        kvn = _layernorm(kv, ln_g, ln_b)
        b, qT, _ = q.shape
        kvT = kv.shape[1]
        qp = (qn @ wq + bq).reshape(b, qT, H, HS).transpose(0, 2, 1, 3)
        kvp = kvn @ wkv + bkv
        kp, vp = jnp.split(kvp, 2, axis=-1)
        kp = kp.reshape(b, kvT, H, HS).transpose(0, 2, 1, 3)
        vp = vp.reshape(b, kvT, H, HS).transpose(0, 2, 1, 3)
        attn = jnp.einsum('bhqd,bhkd->bhqk', qp, kp) / jnp.sqrt(jnp.float32(HS))
        causal = jnp.tril(jnp.ones((qT, kvT), dtype=bool))
        attn = jnp.where(causal, attn, -jnp.inf)
        attn = jax.nn.softmax(attn, axis=-1)
        ctx = jnp.einsum('bhqk,bhkd->bhqd', attn, vp)
        ctx = ctx.transpose(0, 2, 1, 3).reshape(b, qT, H * HS)
        out = ctx @ wo + bo + oq
        return out
    x = _L0_xattn_ref(x, ctx_1024, L0_xattn_ln1_g, L0_xattn_ln1_b, L0_xattn_attn_qkv_w, L0_xattn_attn_qkv_b, L0_xattn_attn_proj_w, L0_xattn_attn_proj_b, L0_xattn_ln2_g, L0_xattn_ln2_b, L0_xattn_q_w, L0_xattn_q_b, L0_xattn_k_w, L0_xattn_k_b, L0_xattn_v_w, L0_xattn_v_b, L0_xattn_ca_proj_w, L0_xattn_ca_proj_b, L0_xattn_ln3_g, L0_xattn_ln3_b, L0_xattn_fc_w, L0_xattn_fc_b, L0_xattn_proj_w, L0_xattn_proj_b)
    x = _L1_xattn_ref(x, ctx_1024, L1_xattn_Wq, L1_xattn_bq, L1_xattn_Wk, L1_xattn_bk, L1_xattn_Wv, L1_xattn_bv, L1_xattn_Wo, L1_xattn_bo, L1_xattn_ln_gamma, L1_xattn_ln_beta)
    x = _L2_xattn_ref(x, ctx_1024, mask_SxS_fc0, L2_xattn_attn_ln_w, L2_xattn_attn_ln_b, L2_xattn_q_w, L2_xattn_q_b, L2_xattn_k_w, L2_xattn_v_w, L2_xattn_v_b, L2_xattn_o_w, L2_xattn_o_b, L2_xattn_cross_ln_w, L2_xattn_cross_ln_b, L2_xattn_cq_w, L2_xattn_cq_b, L2_xattn_ck_w, L2_xattn_cv_w, L2_xattn_cv_b, L2_xattn_co_w, L2_xattn_co_b, L2_xattn_mlp_ln_w, L2_xattn_mlp_ln_b, L2_xattn_fc1_w, L2_xattn_fc1_b, L2_xattn_fc2_w, L2_xattn_fc2_b)
    x = _L3_xattn_ref(x, ctx_1024, L3_xattn_ln_g, L3_xattn_ln_b, L3_xattn_wq, L3_xattn_bq, L3_xattn_wkv, L3_xattn_bkv, L3_xattn_wo, L3_xattn_bo)
    return x

_drawn_inputs = setup_inputs


def setup_inputs(seed=0):
    import zlib

    import numpy as np

    out = dict(_drawn_inputs(seed))
    spreads = {'L0_xattn_ln1_g': (1.0, 0.6),
     'L0_xattn_ln1_b': (0.0, 0.8),
     'L0_xattn_attn_qkv_b': (0.0, 0.276),
     'L0_xattn_attn_proj_b': (0.0, 0.1),
     'L0_xattn_ln2_g': (1.0, 0.6),
     'L0_xattn_ln2_b': (0.0, 0.8),
     'L0_xattn_q_b': (0.0, 0.8),
     'L0_xattn_k_b': (0.0, 2.0),
     'L0_xattn_v_b': (0.0, 0.28),
     'L0_xattn_ca_proj_b': (0.0, 0.1),
     'L0_xattn_ln3_g': (1.0, 0.6),
     'L0_xattn_ln3_b': (0.0, 0.708),
     'L0_xattn_fc_b': (0.0, 0.1),
     'L0_xattn_proj_b': (0.0, 0.1),
     'L1_xattn_bq': (0.0, 0.8),
     'L1_xattn_bk': (0.0, 2.0),
     'L1_xattn_bv': (0.0, 0.1),
     'L1_xattn_bo': (0.0, 0.1),
     'L1_xattn_ln_gamma': (1.0, 0.6),
     'L1_xattn_ln_beta': (0.0, 2.0),
     'L2_xattn_attn_ln_w': (1.0, 0.6),
     'L2_xattn_attn_ln_b': (0.0, 0.8),
     'L2_xattn_q_b': (0.0, 0.8),
     'L2_xattn_v_b': (0.0, 0.295),
     'L2_xattn_o_b': (0.0, 0.1),
     'L2_xattn_cross_ln_w': (1.0, 0.6),
     'L2_xattn_cross_ln_b': (0.0, 0.8),
     'L2_xattn_cq_b': (0.0, 0.8),
     'L2_xattn_cv_b': (0.0, 0.273),
     'L2_xattn_co_b': (0.0, 0.1),
     'L2_xattn_mlp_ln_w': (1.0, 0.6),
     'L2_xattn_mlp_ln_b': (0.0, 0.792),
     'L2_xattn_fc1_b': (0.0, 0.268),
     'L2_xattn_fc2_b': (0.0, 0.1),
     'L3_xattn_ln_g': (1.0, 0.557),
     'L3_xattn_ln_b': (0.0, 0.278)}
    factors = {'mask_SxS_fc0': 5.655,
     'L0_xattn_attn_qkv_w': 3.847,
     'L0_xattn_q_w': 8.0,
     'L0_xattn_k_w': 8.0,
     'L2_xattn_q_w': 8.0,
     'L2_xattn_k_w': 8.0,
     'L2_xattn_cq_w': 8.0,
     'L2_xattn_ck_w': 8.0,
     'L3_xattn_bq': 48.726,
     'L3_xattn_bkv': 3.096,
     'L3_xattn_bo': 3.316,
     'L3_xattn_wq': 3.041}
    for name, (base, spread) in spreads.items():
        noise = np.random.default_rng([zlib.crc32(name.encode()), seed]).standard_normal(out[name].shape)
        drawn = base * np.exp(spread * noise) if base else spread * noise
        out[name] = jnp.asarray(drawn.astype(out[name].dtype))
    for name, factor in factors.items():
        out[name] = (out[name] * factor).astype(out[name].dtype)
    return out
```

```python
from contextlib import ExitStack

import numpy as np

import concourse.bass as bass
from concourse import mybir

F32 = mybir.dt.float32
F32R = mybir.dt.float32r
BF16 = mybir.dt.bfloat16
ALU = mybir.AluOpType
ACT = mybir.ActivationFunctionType
AX = mybir.AxisListType

P = 128
NB = 8
S = 512
E = 256
NT = S // P
NC = E // P
H = 16
HD = E // H
HS = 64
F = 4 * E
NF = F // P
EPS = 1e-5
NEG = -1e30

SELF0, CROSS0, MLP0, CROSS1, SELF2, CROSS2, MLP2, SELF3 = range(8)
ATTN = {SELF0: (False, True, False), CROSS0: (True, False, False), CROSS1: (True, False, False),
        SELF2: (False, False, True), CROSS2: (True, False, False)}
ATTN_NO = {s: n for n, s in enumerate(ATTN)}
CROSS_NO = {CROSS0: 0, CROSS1: 1, CROSS2: 2}
MLP_NO = {MLP0: 0, MLP2: 1}

UNITS = 2 * NB
G = 4
ROWS = 3 * HD + 2
R3 = H // 4
UNITS3 = R3 * NB

C_G, C_B = 0, 16
C_Q, C_K = 32, 42
C_Q3, C_K3 = 52, 60
C_V, C_F = 68, 76
N_COLS = 92
R_V, R_O = 0, 5
N_ROWS = 13
C_ID, C_MQ, C_MK = 0, P, 2 * P

BASE = 1
WCOLS = 4096


def program(nc, x_in, ctx_in, ctx_rows_in, masks_in, shapes_in, cols_in, rows_in, wts, out):
    es = ExitStack()
    with es:
        def sb(name, shape, dt=F32):
            return es.enter_context(nc.sbuf_tensor(name, shape, dt))

        def pb(name):
            return es.enter_context(nc.psum_tensor(name, [P, 512], F32))

        def sem(name):
            return es.enter_context(nc.semaphore(name))

        X = sb("X", [P, NB * NT, E])
        W = [sb("W_even", [P, WCOLS]), sb("W_odd", [P, WCOLS])]
        stk = sb("stk", [P, 32, S], F32R)
        misc = sb("misc", [P, 8, 512])
        V = sb("V", [P, 2, NT * H * 32])
        Pr = sb("Pr", [P, 2, G, S])
        sums = sb("sums", [P, 2, S])
        XH = sb("XH", [P, NT, E])
        hT = sb("hT", [P, NC, S])
        qk32 = sb("qk32", [P, S])
        hi = sb("hi", [P, 2, S], F32R)
        lo = sb("lo", [P, 2, S], F32R)
        mrows = sb("mrows", [P, S])
        cols = sb("cols", [P, N_COLS])
        brow = sb("brow", [P, 2, 2, E])
        ident = sb("ident", [P, P])
        shpb = sb("shpb", [P, 3 * P], BF16)
        st6 = sb("st6", [P, NT, 6])
        mv = sb("mv", [P, NT, 2])
        rstd = sb("rstd", [P, 2, NT])
        mhalf = sb("mhalf", [P, NT])
        mx = sb("mx", [P, 2, 2, NT, G])
        mhl = sb("mhl", [P, 2, 2, NT, 2 * G], F32R)
        qabs = sb("qabs", [P, 4])
        qst = sb("qst", [P, 16])
        ctxT = misc[:, 0:4, :].rearrange("p (a c) n -> p a c n", a=2)
        ovs = misc[:, 4:6, :]
        raw = misc[:, 6:8, :]
        AT3 = misc
        Vh = V[:, :, :].rearrange("p a (t h c) -> p a t h c", t=NT, h=H)
        Vf = V[:, :, :].rearrange("p a n -> p (a n)")
        v3_n = 2 * NT * G * HS
        V3 = Vf[:, 0:v3_n].rearrange("p (a t h c) -> p a t h c", a=2, t=NT, h=G)
        cT = Vf[:, v3_n:v3_n + NC * S].rearrange("p (c n) -> p c n", c=NC)
        ones3 = Vf[:, v3_n + NC * S:v3_n + NC * S + HS]
        h1T = V[:, :, :].rearrange("p a (b n) -> p (a b) n", n=S)
        ones = XH[:, 0, 0:P]
        shp = XH[:, 0:2, :].rearrange("p a n -> p (a n)")[:, 0:3 * P]
        identb = shpb[:, C_ID:C_ID + P]
        mask_q = W[0][:, 2048:4096].rearrange("p (t n) -> p t n", t=NT)
        mask_k = W[1][:, 2048:4096].rearrange("p (t n) -> p t n", t=NT)

        MX = [pb("MX0"), pb("MX1")]
        ST = [pb("ST0"), pb("ST1")]
        OV = [pb("OV0"), pb("OV1")]
        LA = pb("LA")
        LB = pb("LB")
        LBt = LB[:, :].rearrange("p (t n) -> p t n", t=2)
        LAt = LA[:, :].rearrange("p (t n) -> p t n", t=2)
        FR = [MX[0], MX[1], ST[0], ST[1]]

        x_loaded, consts_in = sem("x_loaded"), sem("consts_in")
        w_in = [sem(f"w_in{s}") for s in range(8)]
        w3_late = sem("w3_late")
        masks_loaded = sem("masks_loaded")
        ctx_rows_loaded = sem("ctx_rows_loaded")
        ctx_in_sem = [sem("ctx_even"), sem("ctx_odd")]
        brow_in = [sem("brow_even"), sem("brow_odd")]
        shapes_done, pool_ready = sem("shapes_done"), sem("pool_ready")
        quant = sem("quant")
        quant_pe = sem("quant_pe")
        ln_stats, ln_mv, ln_pool, xh_ready = sem("ln_stats"), sem("ln_mv"), sem("ln_pool"), sem("xh_ready")
        la_full, la_free = sem("la_full"), sem("la_free")
        split_hi, split_done = sem("split_hi"), sem("split_done")
        stack_in = [sem("stack_in0"), sem("stack_in1")]
        mx_full, mx_red = sem("mx_full"), sem("mx_red")
        max_hi, max_split = sem("max_hi"), sem("max_split")
        mt_full, mt_evac = sem("mt_full"), sem("mt_evac")
        mrow_in = [sem("mrow_in0"), sem("mrow_in1")]
        st_full, st_masked, ex_done = sem("st_full"), sem("st_masked"), sem("ex_done")
        pv_done, ov_evac = sem("pv_done"), sem("ov_evac")
        ov_moved = [sem("ov_moved0"), sem("ov_moved1")]
        recip_done, at_mul, at_ready = sem("recip_done"), sem("at_mul"), sem("at_ready")
        op_full, op_evac, x_done = sem("op_full"), sem("op_evac"), sem("x_done")
        v_ones = sem("v_ones")
        fc_full, gelu_done, pr_full, pr_evac, ml_full, ml_evac = (
            sem("fc_full"), sem("gelu_done"), sem("pr_full"), sem("pr_evac"), sem("ml_full"), sem("ml_evac"))
        la3_full, la3_free = sem("la3_full"), sem("la3_free")
        split3_hi, split3_done = sem("split3_hi"), sem("split3_done")
        stack3_in = [sem("stack3_in0"), sem("stack3_in1")]
        mx3_full, mx3_red = sem("mx3_full"), sem("mx3_red")
        max3_hi, max3_split = sem("max3_hi"), sem("max3_split")
        mt3_full, mt3_evac, mrow3_in = sem("mt3_full"), sem("mt3_evac"), sem("mrow3_in")
        st3_full, ex3_done, pv3_done = sem("st3_full"), sem("ex3_done"), sem("pv3_done")
        rc3_done, nm3_done, at3_ready = sem("rc3_done"), sem("nm3_done"), sem("at3_ready")
        op3_full, op3_evac = sem("op3_full"), sem("op3_evac")
        stack3_ones = sem("stack3_ones")
        stored = sem("stored")
        pool_init, ones_set = sem("pool_init"), sem("ones_set")

        def wait(eng, s, v):
            if not isinstance(v, int) or v > 0:
                eng.wait_ge(s, v)

        QUANT_STEPS = 18

        def waits(eng, *pairs, apart=False):
            pairs = [(s, v if isinstance(v, int) else eng.to_reg(v)) for s, v in pairs]
            if apart and any(not isinstance(v, int) for _, v in pairs):
                eng.wait_ge(pool_ready, 1)
            for s, v in pairs:
                wait(eng, s, v)

        def brow_count(s):
            return 16 * sum(2 if x in ATTN_NO else 1 for x in range(s % 2, s + 1, 2))

        def addmask_of(s):
            return ATTN[s][2]

        def xt(b, t, n=1):
            return X[:, bass.ds(NT * b + t, n), :]

        def wq(s, m):
            return W[s % 2][:, 512 * m:512 * m + 512].rearrange("p (c o) -> p c o", c=NC)

        def stages(u):
            return dict(a=u < UNITS - 2, m=-1 <= u < UNITS - 1, b=0 <= u < UNITS, tail=u >= 1, op=u >= 2)

        def run_slots(eng, slot):
            for u in range(-2, 2):
                slot(u, u % 4, u // 2, (u // 2 + 1) // 2, stages(u))
            with eng.Fori(0, 3) as k:
                for n in range(4):
                    slot(4 * k + (2 + n), (2 + n) % 4, 2 * k + (1 + n // 2), k + 1, stages(2 + n))
            for u in range(UNITS - 2, UNITS + 1):
                slot(u, u % 4, u // 2, (u // 2 + 1) // 2, stages(u))

        J_T, J_K, J_Q, J_V, JOBS = 0, (2, 6), (3, 7), 4, 8

        def stages3(v):
            return dict(a=v < UNITS3 - 2, v=-1 <= v < UNITS3 - 1, m=-1 <= v < UNITS3 - 1, b=0 <= v < UNITS3,
                        tail=v >= 1, op=v >= 1, ln=v < UNITS3 - R3)

        def run_slots3(eng, slot):
            for v in range(-2, 1):
                slot(v, v % R3, v // R3, stages3(v))
            with eng.Fori(0, NB - 1) as k:
                for n in range(R3):
                    slot(R3 * k + (1 + n), (1 + n) % R3, k + (1 + n) // R3, stages3(1 + n))
            for v in range(UNITS3 - R3 + 1, UNITS3 + 1):
                slot(v, v % R3, v // R3, stages3(v))

        M_HEADS = ((0, 1), (2,), (3,), ())

        def jobs3(v, r, b):
            return 0 if isinstance(v, int) and v == -2 else 28 * b + (0, 6, 12, 22)[r] + 14

        def job3(v, r, b, name, n=0):
            first = isinstance(v, int) and v == -2
            at = dict(v=0, tc=0 if first else 2, tx=2 if first else 4, kq=(0 if first else 2) + (4 if r == 2 else 0))[name]
            return jobs3(v, r, b) + at + n

        def norm3(b, which):
            return NB * SELF3 + 2 * b + which

        block = es.enter_context(nc.Block())

        @block.sync
        def _(sp):
            def load_weights(s):
                n = WCOLS if s in MLP_NO else WCOLS // 2
                sp.dma_start(W[s % 2][:, 0:n], wts[s]).then_inc(w_in[s], 16)
                if s in ATTN_NO:
                    r = R_V + ATTN_NO[s]
                    sp.dma_start(brow[:, s % 2, 0, :], rows_in[r:r + 1, :].broadcast_to([P, E])).then_inc(brow_in[s % 2], 16)
                load_output_bias(s)

            def load_output_bias(s):
                r = R_O + s
                sp.dma_start(brow[:, s % 2, 1, :], rows_in[r:r + 1, :].broadcast_to([P, E])).then_inc(brow_in[s % 2], 16)

            sp.dma_start(X[:, 0:NT, :], x_in[:, 0:NT, :]).then_inc(x_loaded, 16)
            sp.dma_start(cols[:, :], cols_in).then_inc(consts_in, 16)
            sp.dma_start(shp, shapes_in).then_inc(consts_in, 16)
            sp.dma_start(ident[:, :], shapes_in[:, C_ID:C_ID + P]).then_inc(consts_in, 16)
            load_weights(0)
            sp.dma_start(X[:, NT:NB * NT, :], x_in[:, NT:NB * NT, :]).then_inc(x_loaded, 16)

            def load_ctx(b, par):
                sp.dma_start(ctxT[:, par, :, :], ctx_in[:, bass.ds(NC * b, NC), :]).then_inc(ctx_in_sem[par], 16)

            def attention(s):
                cross, causal, addmask = ATTN[s]
                n = ATTN_NO[s]

                def slot(u, c, b, p, on):
                    half, U, GB = c % 2, UNITS * n + u, NB * n + b
                    if cross and half == 0 and on["op"] and on["a"]:
                        sp.wait_ge(la_full, JOBS * (GB - 1) + J_K[1] + 1)
                        load_ctx(b + 1, 1 - c // 2)
                    for g in range(2):
                        if g == 1 and on["a"] is not None and on["stack1"]:
                            stack(U + 1, 1 - half, 1)
                        if g == 0 and on["tail"]:
                            move(U - 1, 1 - half, 1, GB - 1 + half)
                        if g == 0 and on["b"]:
                            max_rows(U, half, 1)
                    if on["b"]:
                        move(U, half, 0, GB)
                    if on["m"]:
                        max_rows(U + 1, 1 - half, 0)
                    if on["a"]:
                        stack(U + 2, half, 0)

                def stack(U, half, g):
                    wait(sp, st_full, 32 * (U - 2) + 16 * (g + 1))
                    for kind, parts in ((0, (hi, lo, hi)), (1, (hi, hi, lo))):
                        sp.wait_ge(split_done, 2 * U + kind + 1)
                        at = (8 if kind == 0 else 0) + G * g
                        for r, part in enumerate(parts):
                            lo_p = 64 * half + HD * r
                            sp.dma_start(stk[lo_p:lo_p + HD, at:at + G, :].bitcast(F32),
                                         part[64 * g:64 * g + 64, kind, :].bitcast(F32)).then_inc(stack_in[g], 16)

                def max_rows(U, half, g):
                    sp.wait_ge(mt_evac, 2 * U + g + 1)
                    lo_p = 64 * half + 3 * HD
                    sp.dma_start(stk[lo_p:lo_p + 2, G * g:G * g + G, :].bitcast(F32),
                                 mrows[32 * g:32 * g + 2 * G, :]).then_inc(mrow_in[g], 16)

                def move(U, half, g, GBu):
                    waits(sp, (ov_evac, 2 * U + g + 1),
                          (at_ready, BASE + U - 1),
                          (op_full, BASE + 2 * GBu))
                    sp.dma_start(raw[64 * g:64 * g + 64, half, :], ovs[0:P:2, g, :]).then_inc(ov_moved[g], 16)
                    sp.dma_start(sums[64 * g:64 * g + 64, half, :], ovs[1:P:2, g, :]).then_inc(ov_moved[g], 16)

                if cross:
                    load_ctx(0, 0)
                    load_ctx(1, 1)

                def with_stack1(u, c, b, p, on):
                    slot(u, c, b, p, dict(on, stack1=(not isinstance(u, int)) or -1 <= u < UNITS - 1))

                run_slots(sp, with_stack1)

            def layer3(s):
                for part in (2, 3):
                    sp.dma_start(W[0][:, 2048 * (part - 2):2048 * (part - 1)],
                                 wts[s][:, 2048 * part:2048 * part + 2048]).then_inc(w3_late, 16)

                def load_ctx_rows(b):
                    sp.dma_start(XH[:, :, :], ctx_rows_in[:, bass.ds(NT * b, NT), :]).then_inc(ctx_rows_loaded, 16)

                def slot(v, r, b, on):
                    par = r % 2
                    if r == 1 and on["ln"]:
                        load_ctx_rows(b + 1)
                    if on["a"]:
                        for bl in range(2):
                            wait(sp, st3_full, 16 * v + 8 * (bl + 1))
                            for kind, parts in ((0, (hi, hi, lo)), (1, (hi, lo, hi))):
                                sp.wait_ge(split3_done, 2 * (2 * (v + 2) + bl) + kind + 1)
                                for n, (part, lo_p, form) in enumerate(zip(parts, (0, 64, 0), (0, 0, 1))):
                                    at = 16 * par + 8 * (1 - kind) + 4 * form + 2 * bl
                                    sp.dma_start(stk[lo_p:lo_p + HS, at:at + 2, :].bitcast(F32),
                                                 part[:, kind, :].bitcast(F32)).then_inc(stack3_in[bl], 16)
                    if on["m"]:
                        sp.wait_ge(mt3_evac, v + 2)
                        at = 16 * (1 - par) + 4
                        sp.dma_start(stk[HS:HS + 2, at:at + G, :].bitcast(F32),
                                     mrows[32 * (1 - par):32 * (1 - par) + 2 * G, :]).then_inc(mrow3_in, 16)
                    if on["op"] and r == 0:
                        store(b - 1)

                def store(b):
                    sp.wait_ge(x_done, NB * s + b + 1)
                    sp.dma_start(out[:, bass.ds(NT * b, NT), :], xt(b, 0, NT)).then_inc(stored, 16)

                load_ctx_rows(0)
                sp.wait_ge(stack3_ones, 3)
                run_slots3(sp, slot)
                sp.wait_ge(stored, 16 * NB)

            sp.wait_ge(pool_ready, 1)
            for s in range(8):
                wait(sp, x_done, NB * s)
                if s + 1 < SELF3:
                    load_weights(s + 1)
                elif s + 1 == SELF3:
                    sp.dma_start(W[1][:, :], wts[SELF3][:, 0:WCOLS]).then_inc(w_in[SELF3], 16)
                    load_output_bias(SELF3)
                if s == CROSS1:
                    sp.dma_start(mask_q, masks_in[:, 0:NT, :]).then_inc(masks_loaded, 16)
                    sp.dma_start(mask_k, masks_in[:, NT:2 * NT, :]).then_inc(masks_loaded, 16)
                if s in ATTN:
                    attention(s)
                elif s == SELF3:
                    layer3(s)

        @block.tensor
        def _(pe):
            def mm(o, l, r, start=True, stop=True):
                return nc.tensor.matmul(o, l, r, start=start, stop=stop)

            def transpose_x(s, b, c, bank):
                if c == 0:
                    pe.wait_ge(xh_ready, NB * s + b + 1)
                return turn_tiles(c, bank)

            def turn_tiles(c, bank):
                for t in range(NT):
                    last = nc.tensor.transpose(bank[:, P * t:P * t + P], XH[:, t, P * c:P * c + P], ident[:, :])
                return last

            def attention(s):
                cross, causal, addmask = ATTN[s]
                n = ATTN_NO[s]
                wk_, wv_, wq_, wo_ = wq(s, 1), wq(s, 2), wq(s, 0), wq(s, 3)

                def slot(u, c, b, p, on):
                    half, par = c % 2, c // 2
                    U, GB = UNITS * n + u, NB * n + b
                    b1, GB1 = b + 1, NB * n + b + 1
                    for i in range(8):
                        g = i // 4
                        if on["m"] and i % 4 == 0:
                            pe.wait_ge(stack_in[g], 96 * (U + 2))
                        if on["b"] and i % 4 == 0:
                            pe.wait_ge(mrow_in[g], 16 * (U + 1))
                        for j in range(4):
                            if on["m"]:
                                max_tile(U + 1, 1 - half, i, j)
                            if on["b"]:
                                score_tile(U, half, i, j)
                        if on["b"] and i > 0:
                            values(U, half, par, i - 1)
                        elif on["tail"] and i == 0:
                            values(U - 1, 1 - half, par if half else 1 - par, 7)
                        if i == 1 and on["b"]:
                            turn_max(U, half, 1, 2 * (GB - 1 + half))
                        if half == 0 and on["op"]:
                            if i == 3:
                                project_out(GB - 1, 0, 2 * U + (2 if on["b"] else 0))
                            if i == 4:
                                project_out(GB - 1, 1, 2 * U + (2 if on["b"] else 0))
                        if on["a"]:
                            if half == 0 and i in (2, 3):
                                job(GB1, J_T + i - 2)
                                transpose_x(s, b1, i - 2, LA).then_inc(la_full, 1)
                            if i == 4:
                                if cross:
                                    pe.wait_ge(ctx_in_sem[1 - par], 16 * (4 * CROSS_NO[s] + p + 1))
                                job(GB1, J_K[half])
                                source = ctxT[:, 1 - par] if cross else hT
                                project(wk_, half, source)
                            if i == 5:
                                job(GB1, J_Q[half])
                                project(wq_, half, hT)
                            if half == 0 and i in (6, 7):
                                job(GB1, J_V + i - 6)
                                source = ctxT[:, 1 - par] if cross else hT
                                project_values(source, i - 6)
                        if i == 5 and on["m"]:
                            turn_max(U + 1, 1 - half, 0, 2 * GB)

                def job(GBj, k):
                    wait(pe, la_free, JOBS * GBj + k)

                def project(w, half, source):
                    for c in range(NC):
                        last = mm(LA[:, :], w[:, c, P * half:P * half + P], source[:, c, :], c == 0, c == NC - 1)
                    last.then_inc(la_full, 1)

                def project_values(source, j):
                    for t in range(2):
                        tok = slice(P * (2 * j + t), P * (2 * j + t) + P)
                        for c in range(NC):
                            last = mm(LAt[:, t, :], source[:, c, tok], wv_[:, c, :], c == 0, c == NC - 1)
                    last.then_inc(la_full, 1)

                def max_tile(U, half, i, qt):
                    at = 32 * U + 4 * i + qt
                    wait(pe, mx_red, at - 1)
                    lo_p, k_n = 64 * half, P * (qt + 1) if causal else S
                    q = stk[lo_p:lo_p + 3 * HD, i, P * qt:P * qt + P]
                    last = mm(MX[qt % 2][:, 0:k_n], q, stk[lo_p:lo_p + 3 * HD, 8 + i, 0:k_n], True, not causal)
                    if causal:
                        last = mm(MX[qt % 2][:, k_n - P:k_n], identb, shpb[:, C_MQ:C_MQ + P], False, True)
                    last.then_inc(mx_full, 1)

                def score_tile(U, half, i, h):
                    at, head, kt = 32 * U + 4 * i + h, G * (i // 4) + h, i % 4
                    wait(pe, ex_done, at - 1)
                    lo_p, q0 = 64 * half, P * kt if causal else 0
                    k = stk[lo_p:lo_p + ROWS, 8 + head, P * kt:P * kt + P]
                    last = mm(ST[h % 2][:, q0:S], k, stk[lo_p:lo_p + ROWS, head, q0:S], True, not causal)
                    if causal:
                        last = mm(ST[h % 2][:, q0:q0 + P], identb, shpb[:, C_MK:C_MK + P], False, True)
                    last.then_inc(st_full, 1)

                def values(U, half, vpar, i):
                    g, kt = i // 4, i % 4
                    if kt == 0:
                        wait(pe, ov_evac, 2 * U + g - 1)
                    pe.wait_ge(ex_done, 4 * (8 * U + i + 1))
                    q0 = P * kt if causal else 0
                    for h in range(G):
                        last = mm(OV[g][32 * h:32 * h + 32, q0:S], Vh[:, vpar, kt, 8 * half + G * g + h, :], Pr[:, i % 2, h, q0:S],
                                  kt == 0, kt == NT - 1)
                    last.then_inc(pv_done, 1)

                def turn_max(U, half, g, ops):
                    pe.wait_ge(max_split, 2 * U + g + 1)
                    wait(pe, mt_evac, 2 * U + g)
                    wait(pe, op_evac, BASE + ops)
                    for t in range(NT):
                        last = nc.tensor.transpose(LB[0:2 * G, P * t:P * t + P], mhl[:, half, g, t, :].bitcast(F32), ident[:, :])
                    last.then_inc(mt_full, 1)

                def project_out(GBo, j, turned):
                    pe.wait_ge(at_ready, BASE + 2 * (GBo + 1))
                    wait(pe, mt_evac, turned)
                    wait(pe, op_evac, BASE + 2 * GBo + j)
                    for t in range(2):
                        tok = slice(P * (2 * j + t), P * (2 * j + t) + P)
                        for k in range(2):
                            last = mm(LBt[:, t, :], raw[:, k, tok], wo_[:, k, :], k == 0, k == 1)
                    last.then_inc(op_full, 1)

                run_slots(pe, slot)

            def mlp(s):
                m = MLP_NO[s]
                wf = W[s % 2][:, 0:2048].rearrange("p (c o) -> p c o", c=NC)
                wp = W[s % 2][:, 2048:4096].rearrange("p (f o) -> p f o", f=NF)

                def turn(b):
                    MB = NB * m + b
                    for c, bank in enumerate((LA, LB)):
                        wait(pe, ml_evac, 2 * (MB - 1) + c + 1)
                        transpose_x(s, b, c, bank).then_inc(ml_full, 1)

                def batch(b, more):
                    MB = NB * m + b
                    pe.wait_ge(ml_evac, 2 * (MB + 1))
                    for f in range(NF):
                        wait(pe, gelu_done, NF * MB + f - 3)
                        for c in range(NC):
                            last = mm(FR[f % 4][:, :], wf[:, c, P * f:P * f + P], hT[:, c, :], c == 0, c == NC - 1)
                        last.then_inc(fc_full, 1)
                    if more:
                        turn(b + 1)
                    pe.wait_ge(gelu_done, NF * (MB + 1))
                    for j in range(2):
                        wait(pe, pr_evac, 2 * (MB - 1) + j + 1)
                        for t in range(2):
                            tok = slice(P * (2 * j + t), P * (2 * j + t) + P)
                            for f in range(NF):
                                last = mm(OV[j][:, E * t:E * t + E], h1T[:, f, tok], wp[:, f, :], f == 0, f == NF - 1)
                        last.then_inc(pr_full, 1)

                turn(0)
                batch(0, True)
                with pe.Fori(1, NB - 1) as b:
                    batch(b, True)
                batch(NB - 1, False)

            def layer3(s):
                w_q = W[1][:, 0:2048].rearrange("p (c o) -> p c o", c=NC)
                w_k = W[1][:, 2048:4096].rearrange("p (c o) -> p c o", c=NC)
                w_v = W[0][:, 0:2048].rearrange("p (c o) -> p c o", c=NC)
                w_o = W[0][:, 2048:4096].rearrange("p (k o) -> p k o", k=8)
                pe.wait_ge(w3_late, 32)
                pe.wait_ge(stack3_ones, 3)

                def slot(v, r, b, on):
                    par = r % 2
                    for i in range(4):
                        if i == 0:
                            if on["m"]:
                                pe.wait_ge(stack3_in[0], 96 * (v + 2))
                            if on["b"]:
                                pe.wait_ge(mrow3_in, 16 * (v + 1))
                        if i == 1 and on["m"]:
                            pe.wait_ge(stack3_in[1], 96 * (v + 2))
                        tiles = [(h, qt) for h in M_HEADS[i] for qt in range(NT)] if on["m"] else []
                        for kt in range(NT):
                            for h, qt in tiles[len(tiles) * kt // 4:len(tiles) * (kt + 1) // 4]:
                                max_tile(v + 1, 1 - par, h, qt)
                            if on["b"]:
                                score_tile(v, par, i, kt)
                        if on["b"] and i > 0:
                            values(v, par, i - 1)
                        elif on["tail"] and i == 0:
                            values(v - 1, 1 - par, 3)
                        if i == 0 and on["v"]:
                            for j in range(2):
                                la(job3(v, r, b, "v", j))
                                for t in range(2):
                                    tok = slice(P * (2 * j + t), P * (2 * j + t) + P)
                                    rv = (r + 1) % R3
                                    for c in range(NC):
                                        last = mm(LAt[:, t, :], cT[:, c, tok], w_v[:, c, E * rv:E * rv + E], c == 0, c == NC - 1)
                                last.then_inc(la3_full, 1)
                        if i == 0 and r == 2 and on["a"]:
                            turn_batch(v, r, b, "tc", norm3(b + 1, 0))
                        if i == 1 and r == 0 and on["op"]:
                            for j in range(2):
                                project_out(b - 1, j, v)
                        if i == 2 and r == 2 and on["a"]:
                            turn_batch(v, r, b, "tx", norm3(b + 1, 1))
                        if i in (2, 3) and on["a"]:
                            bl = 2 * ((r + 2) % R3) + i - 2
                            for kind, w in ((0, w_k), (1, w_q)):
                                la(job3(v, r, b, "kq", 2 * (i - 2) + kind))
                                source = (cT, hT)[kind]
                                for c in range(NC):
                                    last = mm(LA[:, :], w[:, c, P * bl:P * bl + P], source[:, c, :], c == 0, c == NC - 1)
                                last.then_inc(la3_full, 1)
                    if on["m"]:
                        pe.wait_ge(max3_split, v + 2)
                        wait(pe, mt3_evac, v + 1)
                        wait(pe, op3_evac, BASE + 2 * b)
                        for t in range(NT):
                            last = nc.tensor.transpose(LB[0:2 * G, P * t:P * t + P],
                                                       mhl[:, 1 - par, 0, t, :].bitcast(F32), ident[:, :])
                        last.then_inc(mt3_full, 1)

                def turn_batch(v, r, b, name, N):
                    pe.wait_ge(xh_ready, N + 1)
                    for c in range(NC):
                        la(job3(v, r, b, name, c))
                        turn_tiles(c, LA).then_inc(la3_full, 1)

                def la(k):
                    wait(pe, la3_free, k)

                def max_tile(v, par, h, qt):
                    at, k_n = 16 * v + 4 * h + qt, P * (qt + 1)
                    wait(pe, mx3_red, at - 1)
                    bank, q = MX[qt % 2], 16 * par
                    tok = slice(P * qt, P * qt + P)
                    mm(bank[:, 0:k_n], stk[:, q + h, tok], stk[:, q + 8 + h, 0:k_n], True, False)
                    mm(bank[:, 0:k_n], stk[0:HS, q + 4 + h, tok], stk[0:HS, q + 12 + h, 0:k_n], False, False)
                    mm(bank[:, k_n - P:k_n], identb, shpb[:, C_MQ:C_MQ + P], False, True).then_inc(mx3_full, 1)

                def score_tile(v, par, h, kt):
                    at, q0 = 16 * v + 4 * h + kt, P * kt
                    wait(pe, ex3_done, at - 1)
                    bank, q = ST[kt % 2], 16 * par
                    tok = slice(P * kt, P * kt + P)
                    mm(bank[:, q0:S], stk[:, q + 8 + h, tok], stk[:, q + h, q0:S], True, False)
                    mm(bank[:, q0:S], stk[0:HS + 2, q + 12 + h, tok], stk[0:HS + 2, q + 4 + h, q0:S], False, False)
                    mm(bank[:, q0:q0 + P], identb, shpb[:, C_MK:C_MK + P], False, True).then_inc(st3_full, 1)

                def values(v, par, i):
                    at = 4 * v + i
                    wait(pe, nm3_done, at - 1)
                    for kt in range(NT):
                        pe.wait_ge(ex3_done, 4 * at + kt + 1)
                        for lo_p, w in ((0, V3[:, par, kt, i, :]), (HS, ones3)):
                            last = mm(OV[i % 2][lo_p:lo_p + HS, P * kt:S], w, Pr[:, i % 2, kt, P * kt:S], kt == 0, kt == NT - 1)
                    last.then_inc(pv3_done, 1)

                def project_out(b, j, v):
                    pe.wait_ge(at3_ready, 8 * (b + 1))
                    turned = v + 1 if not isinstance(v, int) or v < UNITS3 else UNITS3
                    pe.wait_ge(mt3_evac, turned)
                    wait(pe, op3_evac, BASE + 2 * b + j)
                    for t in range(2):
                        tok = slice(P * (2 * j + t), P * (2 * j + t) + P)
                        for k in range(8):
                            last = mm(LBt[:, t, :], AT3[:, k, tok], w_o[:, k, :], k == 0, k == 7)
                    last.then_inc(op3_full, 1)

                run_slots3(pe, slot)

            pe.wait_ge(shapes_done, 1)
            pe.wait_ge(pool_ready, 1)
            for s in range(8):
                wait(pe, x_done, NB * s)
                pe.wait_ge(w_in[s], 16)
                if s in ATTN:
                    if s == CROSS1:
                        pe.wait_ge(quant, 4)
                        pe.wait_ge(ones_set, 1)
                        mm(LA[:, 0:4], ones, qabs[:, :]).then_inc(quant_pe, 1)
                        pe.wait_ge(quant, QUANT_STEPS)
                    pe.wait_ge(v_ones, 2 if s >= CROSS1 else 1)
                    attention(s)
                elif s in MLP_NO:
                    mlp(s)
                else:
                    layer3(s)

        @block.scalar
        def _(act):
            def scale_shift(s, c):
                g, o = C_G + 2 * s + c, C_B + 2 * s + c
                return dict(scale=cols[:, g:g + 1], bias=cols[:, o:o + 1])

            def attention(s):
                cross, causal, addmask = ATTN[s]
                n = ATTN_NO[s]

                def slot(u, c, b, p, on):
                    half, U, GB1 = c % 2, UNITS * n + u, NB * n + b + 1
                    for i in range(8):
                        if on["b"]:
                            for h in range(G):
                                exp_tile(u, U, i, h)
                        if i == 1 and on["b"]:
                            rows_out(U, 1)
                        if on["a"]:
                            if half == 0 and i in (2, 3):
                                act.wait_ge(la_full, JOBS * GB1 + J_T + i - 1)
                                nc.scalar.activation(hT[:, i - 2, :], LA[:, :], ACT.Identity,
                                                     **scale_shift(s, i - 2)).then_inc(la_free, 1)
                            if i in (4, 5):
                                kind = i - 4
                                k = (J_K, J_Q)[kind][half]
                                act.wait_ge(la_full, JOBS * GB1 + k + 1)
                                wait(act, split_done, 2 * (U + 2) + kind)
                                at = (C_K, C_Q)[kind] + 2 * n + half
                                nc.scalar.activation(qk32[:, :], LA[:, :], ACT.Identity, bias=cols[:, at:at + 1],
                                                     scale=1.0 if kind == 0 else HD ** -0.5).then_inc(la_free, 1)
                        if i == 5 and on["m"]:
                            rows_out(U + 1, 0)

                def exp_tile(u, U, i, h):
                    at, q0 = 32 * U + 4 * i + h, P * (i % 4) if causal else 0
                    if h == 0:
                        wait(act, pv_done, 8 * U + i - 1)
                    if addmask:
                        act.wait_ge(st_masked, 32 * u + 4 * i + h + 1)
                    else:
                        act.wait_ge(st_full, at + 1)
                    nc.scalar.activation(Pr[:, i % 2, h, q0:S], ST[h % 2][:, q0:S], ACT.Exp).then_inc(ex_done, 1)

                def rows_out(U, g):
                    act.wait_ge(mt_full, 2 * U + g + 1)
                    wait(act, mrow_in[g], 16 * U)
                    nc.scalar.activation(mrows[32 * g:32 * g + 2 * G, :], LB[0:2 * G, :], ACT.Copy).then_inc(mt_evac, 1)

                run_slots(act, slot)

            def mlp(s):
                m = MLP_NO[s]

                def turned(b):
                    for c, bank in enumerate((LA, LB)):
                        act.wait_ge(ml_full, 2 * (NB * m + b) + c + 1)
                        nc.scalar.activation(hT[:, c, :], bank[:, :], ACT.Identity, **scale_shift(s, c)).then_inc(ml_evac, 1)

                def batch(b, more):
                    for f in range(NF):
                        at = C_F + NF * m + f
                        act.wait_ge(fc_full, NF * (NB * m + b) + f + 1)
                        nc.scalar.activation(h1T[:, f, :], FR[f % 4][:, :], ACT.Gelu,
                                             bias=cols[:, at:at + 1]).then_inc(gelu_done, 1)
                    if more:
                        turned(b + 1)

                turned(0)
                batch(0, True)
                with act.Fori(1, NB - 1) as b:
                    batch(b, True)
                batch(NB - 1, False)

            def layer3(s):
                def slot(v, r, b, on):
                    par = r % 2
                    for i in range(4):
                        if on["b"]:
                            for kt in range(NT):
                                at = 16 * v + 4 * i + kt
                                if kt == 0:
                                    wait(act, pv3_done, 4 * v + i - 1)
                                act.wait_ge(st3_full, at + 1)
                                nc.scalar.activation(Pr[:, i % 2, kt, P * kt:S], ST[kt % 2][:, P * kt:S],
                                                     ACT.Exp).then_inc(ex3_done, 1)
                        for at_i, name, to in ((0, "tc", cT), (2, "tx", hT)):
                            if i == at_i and r == 2 and on["a"]:
                                for c in range(NC):
                                    act.wait_ge(la3_full, job3(v, r, b, name, c) + 1)
                                    if name == "tc" and c == 0 and on["v"]:
                                        act.wait_ge(la3_free, job3(v, r, b, "v", 2))
                                    nc.scalar.activation(to[:, c, :], LA[:, :], ACT.Identity,
                                                         **scale_shift(s, c)).then_inc(la3_free, 1)
                        if i in (2, 3) and on["a"]:
                            bl = 2 * ((r + 2) % R3) + i - 2
                            for kind in range(2):
                                act.wait_ge(la3_full, job3(v, r, b, "kq", 2 * (i - 2) + kind) + 1)
                                wait(act, split3_done, 2 * (2 * (v + 2) + i - 2) + kind)
                                at = (C_K3, C_Q3)[kind] + bl
                                nc.scalar.activation(qk32[:, :], LA[:, :], ACT.Identity, bias=cols[:, at:at + 1],
                                                     scale=1.0 if kind == 0 else HS ** -0.5).then_inc(la3_free, 1)
                    if on["m"]:
                        act.wait_ge(mt3_full, v + 2)
                        wait(act, mrow3_in, 16 * (v + 1))
                        lo_p = 32 * (1 - par)
                        nc.scalar.activation(mrows[lo_p:lo_p + 2 * G, :], LB[0:2 * G, :], ACT.Copy).then_inc(mt3_evac, 1)

                run_slots3(act, slot)

            act.wait_ge(pool_ready, 1)
            for s in range(8):
                wait(act, x_done, NB * s)
                if s in ATTN:
                    attention(s)
                elif s in MLP_NO:
                    mlp(s)
                else:
                    layer3(s)

        @block.vector
        def _(dve):
            def layer_norm(N, tile):
                at = NT * N
                wait(dve, ln_mv, at)
                for t in range(NT):
                    nc.vector.bn_stats(st6[:, t, :], tile(t)).then_inc(ln_stats, 1)
                waits(dve, (xh_ready, N), apart=True)
                for t in range(NT):
                    waits(dve, (ln_stats, at + t + 1), apart=True)
                    nc.vector.bn_aggr(mv[:, t, :], st6[:, t, :]).then_inc(ln_mv, 1)

            def layer_norm_x(N, b):
                layer_norm(N, lambda t: xt(b, t))

            def add_to_x(b, j, bank, done):
                nc.vector.tensor_tensor(xt(b, 2 * j, 2), bank, xt(b, 2 * j, 2), ALU.add).then_inc(done, 1)

            def attention(s):
                cross, causal, addmask = ATTN[s]
                n = ATTN_NO[s]

                def slot(u, c, b, p, on):
                    half, par = c % 2, c // 2
                    U, GB = UNITS * n + u, NB * n + b
                    for i in range(8):
                        if half == 0 and i == 7 and on["a"]:
                            values_out(GB + 1, 1 - par, 0)
                        if on["m"] and i % 4 == 0:
                            wait(dve, max_split, 2 * (U + 1) - 3 + i // 4)
                        for j in range(4):
                            if on["m"]:
                                max_tile(U + 1, 1 - half, i, j)
                            if on["b"] and addmask:
                                add_mask(u, U, i, j)
                        if i == 0 and half == 0 and on["a"]:
                            layer_norm_x(NB * s + b + 1, b + 1)
                        if i == 1 and on["tail"]:
                            product_out(U - 1, 1)
                        if i == 2 and on["tail"]:
                            dve.wait_ge(ov_moved[0], 32 * U)
                            dve.wait_ge(ov_moved[1], 32 * U)
                            nc.vector.reciprocal(sums[:, 1 - half, :], sums[:, 1 - half, :]).then_inc(recip_done, 1)
                        if i == 5 and on["b"]:
                            product_out(U, 0)
                        if half == 0 and on["op"] and i in (4, 5):
                            dve.wait_ge(op_full, BASE + 2 * (GB - 1) + i - 3)
                            add_to_x(b - 1, i - 4, LBt, op_evac)
                        if half == 0 and i == 7 and on["a"]:
                            values_out(GB + 1, 1 - par, 1)

                def max_tile(U, half, i, qt):
                    at = 32 * U + 4 * i + qt
                    waits(dve, (mx_full, at + 1), apart=addmask)
                    bank, m = MX[qt % 2], mx[:, half, i // 4, qt, i % 4:i % 4 + 1]
                    if addmask:
                        nc.vector.tensor_tensor_reduce(bank[:, :], bank[:, :], mask_q[:, qt, :], 1.0, -3.0e38,
                                                       ALU.add, ALU.max, m).then_inc(mx_red, 1)
                    else:
                        k_n = P * (qt + 1) if causal else S
                        nc.vector.tensor_reduce(m, bank[:, 0:k_n], AX.X, ALU.max).then_inc(mx_red, 1)

                def add_mask(u, U, i, h):
                    at = 32 * U + 4 * i + h
                    dve.wait_ge(st_full, at + 1)
                    nc.vector.tensor_tensor(ST[h % 2][:, :], ST[h % 2][:, :], mask_k[:, i % 4, :],
                                            ALU.add).then_inc(st_masked, 1)

                def product_out(U, g):
                    dve.wait_ge(pv_done, 8 * U + 4 * (g + 1))
                    wait(dve, ov_moved[g], 32 * U)
                    nc.vector.tensor_copy(ovs[:, g, :], OV[g][:, :]).then_inc(ov_evac, 1)

                def values_out(GBj, vpar, j):
                    dve.wait_ge(la_full, JOBS * GBj + J_V + j + 1)
                    to = Vh[:, vpar, 2 * j:2 * j + 2, :, :].rearrange("p t h (d two) -> p t h d two", two=2)[:, :, :, :, 0]
                    bias = brow[:, s % 2, 0:1, :].rearrange("p t (h d) -> p t h d", h=H).broadcast_to([P, 2, H, HD])
                    nc.vector.tensor_tensor(to, LAt[:, :, :].rearrange("p t (h d) -> p t h d", h=H), bias, ALU.add).then_inc(la_free, 1)

                run_slots(dve, slot)

            def mlp(s):
                m = MLP_NO[s]

                def batch(b, more):
                    if more:
                        layer_norm_x(NB * s + b + 1, b + 1)
                    for j in range(2):
                        dve.wait_ge(pr_full, 2 * (NB * m + b) + j + 1)
                        add_to_x(b, j, OV[j][:, :].rearrange("p (t n) -> p t n", t=2), pr_evac)

                layer_norm_x(NB * s, 0)
                batch(0, True)
                with dve.Fori(1, NB - 1) as b:
                    batch(b, True)
                batch(NB - 1, False)

            def quantize():
                w = W[CROSS1 % 2]
                up, down = Pr[:, 0, :, :], Pr[:, 1, :, :]
                gam, thr, neg = qst[:, 0:4], qst[:, 4:8], qst[:, 8:12]
                wm = w[:, 0:2048].rearrange("p (m n) -> p m n", m=4)
                dve.wait_ge(w_in[CROSS1], 16)
                nc.vector.tensor_reduce(qabs[:, :], wm, AX.X, ALU.add, apply_absolute_value=True).then_inc(quant, 4)
                dve.wait_ge(quant_pe, 1)
                nc.vector.tensor_scalar(gam, LA[:, 0:4], 1.0 / (E * E), None, ALU.mult).then_inc(quant, 1)
                dve.wait_ge(quant, 5)
                nc.vector.tensor_scalar(thr, gam, 1e-5, 0.5, ALU.add, ALU.mult).then_inc(quant, 1)
                dve.wait_ge(quant, 6)
                nc.vector.tensor_scalar(neg, thr, -1.0, None, ALU.mult).then_inc(quant, 1)
                dve.wait_ge(quant, 7)
                for k in range(4):
                    nc.vector.tensor_scalar(up[:, k, :], wm[:, k, :], thr[:, k:k + 1], gam[:, k:k + 1],
                                            ALU.is_gt, ALU.mult).then_inc(quant, 1)
                    nc.vector.tensor_scalar(down[:, k, :], wm[:, k, :], neg[:, k:k + 1], gam[:, k:k + 1],
                                            ALU.is_lt, ALU.mult).then_inc(quant, 1)
                dve.wait_ge(quant, 15)
                nc.vector.tensor_tensor(up, up, down, ALU.subtract).then_inc(quant, 1)
                dve.wait_ge(quant, 16)
                nc.vector.tensor_tensor(up, up, wm, ALU.subtract).then_inc(quant, 1)
                dve.wait_ge(quant, 17)
                nc.vector.tensor_tensor(wm, wm, up, ALU.add).then_inc(quant, 1)

            def layer3(s):
                def slot(v, r, b, on):
                    par = r % 2
                    for i in range(4):
                        if on["m"]:
                            if i == 0:
                                wait(dve, max3_split, v)
                            for h in M_HEADS[i]:
                                for qt in range(NT):
                                    dve.wait_ge(mx3_full, 16 * (v + 1) + 4 * h + qt + 1)
                                    nc.vector.tensor_reduce(mx[:, 1 - par, 0, qt, h:h + 1], MX[qt % 2][:, 0:P * (qt + 1)],
                                                            AX.X, ALU.max).then_inc(mx3_red, 1)
                        if i == 0 and on["v"]:
                            if on["tail"]:
                                dve.wait_ge(pv3_done, 4 * v)
                            for j in range(2):
                                dve.wait_ge(la3_full, job3(v, r, b, "v", j) + 1)
                                nc.vector.tensor_copy(V3[:, 1 - par, 2 * j:2 * j + 2, :, :],
                                                      LAt[:, :, :].rearrange("p t (h d) -> p t h d", h=G)).then_inc(la3_free, 1)
                        if i == 1 and r == 0 and on["op"]:
                            for j in range(2):
                                dve.wait_ge(op3_full, 2 * (b - 1) + j + 1)
                                add_to_x(b - 1, j, LBt, op3_evac)
                        if on["b"] and i > 0:
                            normalize(v, r, b, i - 1)
                        elif on["tail"] and i == 0:
                            normalize(v - 1, (r - 1) % R3, None, 3)
                        if i == 2 and r == 1 and on["ln"]:
                            norm_ctx(b + 1)
                        if i == 0 and r == 2 and on["a"] and on["b"]:
                            norm_x(b + 1)

                def normalize(v, r, b, i):
                    at = 4 * v + i
                    dve.wait_ge(pv3_done, at + 1)
                    nc.vector.reciprocal(sums[0:HS, i % 2, :], OV[i % 2][HS:P, :]).then_inc(rc3_done, 1)
                    if r == 0 and i == 0:
                        wait(dve, op3_full, 2 * b)
                    dve.wait_ge(rc3_done, at + 1)
                    lo_p = HS * (i % 2)
                    nc.vector.tensor_tensor(AT3[lo_p:lo_p + HS, 2 * r + i // 2, :], OV[i % 2][0:HS, :],
                                            sums[0:HS, i % 2, :], ALU.mult).then_inc(nm3_done, 1)

                def norm_ctx(b):
                    dve.wait_ge(ctx_rows_loaded, 16 * (b + 1))
                    layer_norm(norm3(b, 0), lambda t: XH[:, t, :])

                def norm_x(b):
                    layer_norm_x(norm3(b, 1), b)

                norm_ctx(0)
                norm_x(0)
                run_slots3(dve, slot)

            dve.wait_ge(consts_in, 48)
            for n, done in enumerate((op_full, op_evac, op3_evac, at_ready)):
                nc.vector.memset(qst[:, n:n + 1], 0.0).then_inc(done, BASE)
            nc.vector.tensor_copy(shpb[:, :], shp).then_inc(shapes_done, 1)
            dve.wait_ge(x_loaded, 32)
            dve.wait_ge(shapes_done, 1)
            for s in range(8):
                wait(dve, x_done, NB * s)
                dve.wait_ge(brow_in[s % 2], brow_count(s))
                if s in ATTN:
                    if s == CROSS1:
                        quantize()
                    if addmask_of(s):
                        dve.wait_ge(masks_loaded, 32)
                    attention(s)
                elif s in MLP_NO:
                    mlp(s)
                else:
                    layer3(s)

        @block.gpsimd
        def _(pool):
            def layer_norm(N, rows, turned=None, turned_at=0):
                waits(pool, (ln_mv, NT * (N + 1)),
                      (xh_ready, N), apart=True)
                nc.gpsimd.tensor_scalar(rstd[:, 0, :], mv[:, :, 1], EPS, None, ALU.add).then_inc(ln_pool, 1)
                pool.wait_ge(ln_pool, 3 * N + 1)
                nc.gpsimd.tensor_tensor(rstd[:, 1, :], rstd[:, 0, :], mhalf[:, :], ALU.pow).then_inc(ln_pool, 1)
                pool.wait_ge(ln_pool, 3 * N + 2)
                if turned is not None:
                    wait(pool, turned, turned_at)
                nc.gpsimd.tensor_tensor(XH[:, :, :], rows, mv[:, :, 0:1].broadcast_to([P, NT, E]),
                                        ALU.subtract).then_inc(ln_pool, 1)
                pool.wait_ge(ln_pool, 3 * N + 3)
                nc.gpsimd.tensor_tensor(XH[:, :, :], XH[:, :, :], rstd[:, 1, :].rearrange("p (t a) -> p t a", a=1).broadcast_to([P, NT, E]),
                                        ALU.mult).then_inc(xh_ready, 1)

            def add_bias(s, b):
                bias = brow[:, s % 2, 1:2, :].broadcast_to([P, NT, E])
                nc.gpsimd.tensor_tensor(xt(b, 0, NT), xt(b, 0, NT), bias, ALU.add).then_inc(x_done, 1)

            def split(kind, hi_sem, lo_sem, at):
                nc.gpsimd.tensor_copy(hi[:, kind, :], qk32[:, :]).then_inc(hi_sem, 1)
                pool.wait_ge(hi_sem, at + 1)
                nc.gpsimd.tensor_tensor(lo[:, kind, :], qk32[:, :], hi[:, kind, :].bitcast(F32),
                                        ALU.subtract).then_inc(lo_sem, 1)

            def split_max(half, g, hi_sem, lo_sem, at):
                nc.gpsimd.tensor_copy(mhl[:, half, g, :, 0:G], mx[:, half, g, :, :]).then_inc(hi_sem, 1)
                pool.wait_ge(hi_sem, at + 1)
                nc.gpsimd.tensor_tensor(mhl[:, half, g, :, G:2 * G], mx[:, half, g, :, :],
                                        mhl[:, half, g, :, 0:G].bitcast(F32), ALU.subtract).then_inc(lo_sem, 1)

            def attention(s):
                n = ATTN_NO[s]

                def slot(u, c, b, p, on):
                    half = c % 2
                    U, GB = UNITS * n + u, NB * n + b
                    if on["b"]:
                        maxima(U, half, 1)
                    if half == 0 and on["a"]:
                        layer_norm(NB * s + b + 1, xt(b + 1, 0, NT), la_full, JOBS * GB + 2)
                    if on["tail"]:
                        pool.wait_ge(recip_done, U)
                        nc.gpsimd.tensor_tensor(raw[:, 1 - half, :], raw[:, 1 - half, :], sums[:, 1 - half, :],
                                                ALU.mult).then_inc(at_ready, 1)
                    if on["a"]:
                        key_query(U, half, b, 0)
                    if on["m"]:
                        maxima(U + 1, 1 - half, 0)
                    if on["a"]:
                        key_query(U, half, b, 1)
                    if half == 0 and on["op"]:
                        pool.wait_ge(op_evac, BASE + 2 * GB)
                        add_bias(s, b - 1)

                def key_query(U, half, b, kind):
                    done = (la_free, JOBS * (NB * n + b + 1) + (J_K, J_Q)[kind][half] + 1)
                    if kind == 0:
                        waits(pool, done, (stack_in[0], 96 * (U + 2)), (stack_in[1], 96 * (U + 2)), apart=True)
                    else:
                        waits(pool, done, apart=True)
                    split(kind, split_hi, split_done, 2 * (U + 2) + kind)

                def maxima(U, half, g):
                    waits(pool, (mx_red, 32 * U + 16 * (g + 1)),
                          (mt_full, 2 * (U - 2) + g + 1), apart=True)
                    split_max(half, g, max_hi, max_split, 2 * U + g)

                run_slots(pool, slot)

            def mlp(s):
                m = MLP_NO[s]

                def batch(b, more):
                    if more:
                        layer_norm(NB * s + b + 1, xt(b + 1, 0, NT), ml_full, 2 * (NB * m + b + 1))
                    pool.wait_ge(pr_evac, 2 * (NB * m + b + 1))
                    add_bias(s, b)

                layer_norm(NB * s, xt(0, 0, NT))
                batch(0, True)
                with pool.Fori(1, NB - 1) as b:
                    batch(b, True)
                batch(NB - 1, False)

            def layer3(s):
                def slot(v, r, b, on):
                    par = r % 2
                    if r == 2 and on["a"]:
                        layer_norm(norm3(b + 1, 1), xt(b + 1, 0, NT), la3_full, job3(v, r, b, "tc", 1) + 1)
                    if on["tail"]:
                        value_bias(v - 1, (r - 1) % R3, 1)
                    if r == 0 and on["op"]:
                        pool.wait_ge(op3_evac, BASE + 2 * b)
                        add_bias(s, b - 1)
                    if on["b"]:
                        value_bias(v, r, 0)
                    if r == 1 and on["ln"]:
                        layer_norm(norm3(b + 1, 0), XH[:, :, :])
                    for bl in range(2):
                        if on["a"]:
                            for kind in range(2):
                                done = (la3_free, job3(v, r, b, "kq", 2 * bl + kind) + 1)
                                if kind == 0:
                                    waits(pool, done, (stack3_in[1 - bl], 96 * (v + 2 + bl)), apart=True)
                                else:
                                    waits(pool, done, apart=True)
                                split(kind, split3_hi, split3_done, 2 * (2 * (v + 2) + bl) + kind)
                        if bl == 0 and on["m"]:
                            waits(pool, (mx3_red, 16 * (v + 2)),
                                  (mt3_full, v), apart=True)
                            split_max(1 - par, 0, max3_hi, max3_split, v + 1)

                def value_bias(v, r, j):
                    waits(pool, (nm3_done, 4 * v + 2 * (j + 1)), apart=True)
                    blk = 2 * r + j
                    nc.gpsimd.tensor_scalar(AT3[:, blk, :], AT3[:, blk, :], cols[:, C_V + blk:C_V + blk + 1], None,
                                            ALU.add).then_inc(at3_ready, 1)

                nc.gpsimd.memset(ones3, 1.0).then_inc(stack3_ones, 1)
                for par in range(2):
                    pool.wait_ge(stack3_ones, par + 1)
                    nc.gpsimd.memset(stk[HS:P, 16 * par + 12:16 * par + 16, :].bitcast(F32), -1.0).then_inc(stack3_ones, 1)
                pool.wait_ge(stack3_ones, 3)
                layer_norm(norm3(0, 0), XH[:, :, :])
                run_slots3(pool, slot)

            def columns_of_one():
                ones_at = Vh[:, :, :, :, :].rearrange("p a t h (d two) -> p (a t h) d two", two=2)[:, :, :, 1]
                nc.gpsimd.memset(ones_at, 1.0).then_inc(v_ones, 1)

            nc.gpsimd.memset(mhalf[:, :], -0.5).then_inc(pool_init, 1)
            for half in range(2):
                lo_p = 64 * half + 32
                pool.wait_ge(pool_init, half + 1)
                nc.gpsimd.memset(stk[lo_p:lo_p + 32, 8:16, :].bitcast(F32), -1.0).then_inc(pool_init, 1)
            pool.wait_ge(pool_init, 3)
            columns_of_one()
            pool.wait_ge(v_ones, 1)
            pool.wait_ge(consts_in, 48)
            nc.gpsimd.tensor_scalar(cols[:, C_Q:C_Q + 10], cols[:, C_Q:C_Q + 10], HD ** -0.5, None, ALU.mult).then_inc(pool_init, 1)
            pool.wait_ge(pool_init, 4)
            nc.gpsimd.tensor_scalar(cols[:, C_Q3:C_Q3 + 8], cols[:, C_Q3:C_Q3 + 8], HS ** -0.5, None, ALU.mult).then_inc(pool_init, 1)
            pool.wait_ge(pool_init, 5)
            pool.wait_ge(x_loaded, 32)
            nc.gpsimd.memset(qst[:, 12:16], 0.0).then_inc(pool_ready, 1)
            for s in range(8):
                wait(pool, x_done, NB * s)
                if s in ATTN:
                    if s == CROSS1:
                        nc.gpsimd.memset(ones, 1.0).then_inc(ones_set, 1)
                        pool.wait_ge(ones_set, 1)
                        columns_of_one()
                        pool.wait_ge(v_ones, 2)
                    attention(s)
                elif s in MLP_NO:
                    mlp(s)
                else:
                    layer3(s)


ATTN_NAMES = {SELF0: ("L0_xattn_ln1_g", "L0_xattn_ln1_b", None, "L0_xattn_attn_proj_w", None, "L0_xattn_attn_proj_b"),
              CROSS0: ("L0_xattn_ln2_g", "L0_xattn_ln2_b", ("L0_xattn_q_w", "L0_xattn_k_w", "L0_xattn_v_w"),
                       "L0_xattn_ca_proj_w", ("L0_xattn_q_b", "L0_xattn_k_b", "L0_xattn_v_b"), "L0_xattn_ca_proj_b"),
              CROSS1: ("L1_xattn_ln_gamma", "L1_xattn_ln_beta", ("L1_xattn_Wq", "L1_xattn_Wk", "L1_xattn_Wv"),
                       "L1_xattn_Wo", ("L1_xattn_bq", "L1_xattn_bk", "L1_xattn_bv"), "L1_xattn_bo"),
              SELF2: ("L2_xattn_attn_ln_w", "L2_xattn_attn_ln_b", ("L2_xattn_q_w", "L2_xattn_k_w", "L2_xattn_v_w"),
                      "L2_xattn_o_w", ("L2_xattn_q_b", None, "L2_xattn_v_b"), "L2_xattn_o_b"),
              CROSS2: ("L2_xattn_cross_ln_w", "L2_xattn_cross_ln_b", ("L2_xattn_cq_w", "L2_xattn_ck_w", "L2_xattn_cv_w"),
                       "L2_xattn_co_w", ("L2_xattn_cq_b", None, "L2_xattn_cv_b"), "L2_xattn_co_b")}
MLP_NAMES = {MLP0: ("L0_xattn_ln3_g", "L0_xattn_ln3_b", "L0_xattn_fc_w", "L0_xattn_fc_b", "L0_xattn_proj_w", "L0_xattn_proj_b"),
             MLP2: ("L2_xattn_mlp_ln_w", "L2_xattn_mlp_ln_b", "L2_xattn_fc1_w", "L2_xattn_fc1_b", "L2_xattn_fc2_w",
                    "L2_xattn_fc2_b")}


def by_partition(w):
    return w.reshape(-1, P, w.shape[1]).transpose(1, 0, 2).reshape(P, -1)


def head_order():
    return np.arange(E).reshape(2, 2, G, HD).transpose(0, 1, 3, 2).reshape(-1)


def head_order3():
    return np.arange(H * HS).reshape(H // 2, 2, HS).transpose(0, 2, 1).reshape(-1)


def kernel(**inputs):
    import concourse.bacc as bacc
    from concourse.bass_utils import run_bass_kernel_spmd

    a = {k: np.asarray(v) for k, v in inputs.items()}
    zero = np.zeros(E, np.float32)
    order, order3 = head_order(), head_order3()
    weights, cols, rows = [None] * 8, np.zeros((P, N_COLS), np.float32), np.zeros((N_ROWS, E), np.float32)

    def put(at, vector):
        cols[:, at:at + vector.size // P] = vector.reshape(-1, P).T

    for s, (g, o, qkv, wo, qkv_b, bo) in ATTN_NAMES.items():
        if qkv is None:
            q_w, k_w, v_w = np.split(a["L0_xattn_attn_qkv_w"], 3)
            q_b, k_b, v_b = np.split(a["L0_xattn_attn_qkv_b"], 3)
        else:
            q_w, k_w, v_w = (a[x] for x in qkv)
            q_b, k_b, v_b = (zero if x is None else a[x] for x in qkv_b)
        weights[s] = np.concatenate([by_partition(q_w[order].T), by_partition(k_w[order].T), by_partition(v_w.T),
                                     by_partition(a[wo].T)], axis=1)
        put(C_Q + 2 * ATTN_NO[s], q_b[order])
        put(C_K + 2 * ATTN_NO[s], k_b[order])
        rows[R_V + ATTN_NO[s]], rows[R_O + s] = v_b, a[bo]
        put(C_G + 2 * s, a[g])
        put(C_B + 2 * s, a[o])
    for s, (g, o, fw, fb, pw, pb_) in MLP_NAMES.items():
        weights[s] = np.concatenate([by_partition(a[fw].T), by_partition(a[pw].T)], axis=1)
        put(C_F + NF * MLP_NO[s], a[fb])
        rows[R_O + s] = a[pb_]
        put(C_G + 2 * s, a[g])
        put(C_B + 2 * s, a[o])
    k3, v3 = np.split(a["L3_xattn_wkv"], 2, axis=1)
    kb3, vb3 = np.split(a["L3_xattn_bkv"], 2)
    weights[SELF3] = np.concatenate([by_partition(a["L3_xattn_wq"][:, order3]), by_partition(k3[:, order3]),
                                     by_partition(v3), by_partition(a["L3_xattn_wo"])], axis=1)
    put(C_Q3, a["L3_xattn_bq"][order3])
    put(C_K3, kb3[order3])
    put(C_V, vb3)
    rows[R_O + SELF3] = a["L3_xattn_bo"]
    put(C_G + 2 * SELF3, a["L3_xattn_ln_g"])
    put(C_B + 2 * SELF3, a["L3_xattn_ln_b"])

    later = np.triu(np.full((P, P), NEG, np.float32), 1)
    arrays = {
        "x_t": a["x"].reshape(NB * NT, P, E).transpose(1, 0, 2),
        "ctx_t": a["ctx_1024"].transpose(2, 0, 1).reshape(NC, P, NB, S).transpose(1, 2, 0, 3).reshape(P, NB * NC, S),
        "ctx_rows": a["ctx_1024"].reshape(NB * NT, P, E).transpose(1, 0, 2),
        "masks": np.concatenate([m.reshape(NT, P, S).transpose(1, 0, 2) for m in (a["mask_SxS_fc0"], a["mask_SxS_fc0"].T)], axis=1),
        "shapes": np.concatenate([np.eye(P, dtype=np.float32), later, later.T], axis=1),
        "cols": cols,
        "rows": rows,
        **{f"w{s}": w for s, w in enumerate(weights)},
    }
    arrays = {k: np.ascontiguousarray(v) for k, v in arrays.items()}
    nc = bacc.Bacc("TRN2", target_bir_lowering=False, num_devices=1)
    aps = {k: nc.dram_tensor("in_" + k, v.shape, F32, kind="ExternalInput").ap() for k, v in arrays.items()}
    out = nc.dram_tensor("out_x", (P, NB * NT, E), F32, kind="ExternalOutput").ap()
    program(nc, aps["x_t"], aps["ctx_t"], aps["ctx_rows"], aps["masks"], aps["shapes"], aps["cols"], aps["rows"],
            [aps[f"w{s}"] for s in range(8)], out)
    r = run_bass_kernel_spmd(nc, [{"in_" + k: v for k, v in arrays.items()}], core_ids=[0])
    return r.results[0]["out_x"].transpose(1, 0, 2).reshape(NB, S, E)
```

```python
from contextlib import ExitStack

import numpy as np

import concourse.bass as bass
from concourse import mybir

F32 = mybir.dt.float32
F32R = mybir.dt.float32r
BF16 = mybir.dt.bfloat16
ALU = mybir.AluOpType
ACT = mybir.ActivationFunctionType
AX = mybir.AxisListType

P = 128
NB = 8
S = 512
E = 256
NT = S // P
NC = E // P
H = 16
HD = E // H
HS = 64
F = 4 * E
NF = F // P
EPS = 1e-5
NEG = -1e30

SELF0, CROSS0, MLP0, CROSS1, SELF2, CROSS2, MLP2, SELF3 = range(8)
ATTN = {SELF0: (False, True, False), CROSS0: (True, False, False), CROSS1: (True, False, False),
        SELF2: (False, False, True), CROSS2: (True, False, False)}
ATTN_NO = {s: n for n, s in enumerate(ATTN)}
CROSS_NO = {CROSS0: 0, CROSS1: 1, CROSS2: 2}
MLP_NO = {MLP0: 0, MLP2: 1}

UNITS = 2 * NB
G = 4
ROWS = 3 * HD + 2
R3 = H // 4
UNITS3 = R3 * NB

C_G, C_B = 0, 16
C_Q, C_K = 32, 42
C_Q3, C_K3 = 52, 60
C_V, C_F = 68, 76
N_COLS = 92
R_V, R_O = 0, 5
N_ROWS = 13
C_ID, C_MQ, C_MK = 0, P, 2 * P

BASE = 1
WCOLS = 4096


def program(nc, x_in, ctx_in, ctx_rows_in, masks_in, shapes_in, cols_in, rows_in, wts, out):
    es = ExitStack()
    with es:
        def sb(name, shape, dt=F32):
            return es.enter_context(nc.sbuf_tensor(name, shape, dt))

        def pb(name):
            return es.enter_context(nc.psum_tensor(name, [P, 512], F32))

        def sem(name):
            return es.enter_context(nc.semaphore(name))

        X = sb("X", [P, NB * NT, E])
        W = [sb("W_even", [P, WCOLS]), sb("W_odd", [P, WCOLS])]
        stk = sb("stk", [P, 32, S], F32R)
        misc = sb("misc", [P, 8, 512])
        V = sb("V", [P, 2, NT * H * 32])
        Pr = sb("Pr", [P, 2, G, S])
        sums = sb("sums", [P, 2, S])
        XH = sb("XH", [P, NT, E])
        hT = sb("hT", [P, NC, S])
        hi = sb("hi", [P, 2, S], F32R)
        lo = sb("lo", [P, 2, S], F32R)
        mrows = sb("mrows", [P, S])
        cols = sb("cols", [P, N_COLS])
        brow = sb("brow", [P, 2, 2, E])
        ident = sb("ident", [P, P])
        shpb = sb("shpb", [P, 3 * P], BF16)
        st6 = sb("st6", [P, NT, 6])
        mv = sb("mv", [P, NT, 2])
        rstd = sb("rstd", [P, 2, NT])
        mhalf = sb("mhalf", [P, NT])
        mx = sb("mx", [P, 2, 2, NT, G])
        mhl = sb("mhl", [P, 2, 2, NT, 2 * G], F32R)
        qabs = sb("qabs", [P, 4])
        qst = sb("qst", [P, 16])
        ctxT = misc[:, 0:4, :].rearrange("p (a c) n -> p a c n", a=2)
        ovs = misc[:, 4:6, :]
        raw = misc[:, 6:8, :]
        AT3 = misc
        Vh = V[:, :, :].rearrange("p a (t h c) -> p a t h c", t=NT, h=H)
        Vf = V[:, :, :].rearrange("p a n -> p (a n)")
        v3_n = 2 * NT * G * HS
        V3 = Vf[:, 0:v3_n].rearrange("p (a t h c) -> p a t h c", a=2, t=NT, h=G)
        cT = Vf[:, v3_n:v3_n + NC * S].rearrange("p (c n) -> p c n", c=NC)
        ones3 = Vf[:, v3_n + NC * S:v3_n + NC * S + HS]
        h1T = V[:, :, :].rearrange("p a (b n) -> p (a b) n", n=S)
        ones = XH[:, 0, 0:P]
        shp = XH[:, 0:2, :].rearrange("p a n -> p (a n)")[:, 0:3 * P]
        identb = shpb[:, C_ID:C_ID + P]
        mask_q = W[0][:, 2048:4096].rearrange("p (t n) -> p t n", t=NT)
        mask_k = W[1][:, 2048:4096].rearrange("p (t n) -> p t n", t=NT)
        columns3 = Pr[:, 0, 0:2, :].rearrange("p a (k m) -> p (a k) m", m=P)

        MX = [pb("MX0"), pb("MX1")]
        ST = [pb("ST0"), pb("ST1")]
        OV = [pb("OV0"), pb("OV1")]
        LA = pb("LA")
        LB = pb("LB")
        LBt = LB[:, :].rearrange("p (t n) -> p t n", t=2)
        LAt = LA[:, :].rearrange("p (t n) -> p t n", t=2)
        FR = [MX[0], MX[1], ST[0], ST[1]]

        x_loaded, consts_in = sem("x_loaded"), sem("consts_in")
        w_in = [sem(f"w_in{s}") for s in range(8)]
        w3_late = sem("w3_late")
        masks_loaded = sem("masks_loaded")
        ctx_rows_loaded = sem("ctx_rows_loaded")
        ctx_in_sem = [sem("ctx_even"), sem("ctx_odd")]
        brow_in = [sem("brow_even"), sem("brow_odd")]
        shapes_done, pool_ready = sem("shapes_done"), sem("pool_ready")
        quant = sem("quant")
        quant_pe = sem("quant_pe")
        ln_stats, ln_mv, ln_pool, xh_ready = sem("ln_stats"), sem("ln_mv"), sem("ln_pool"), sem("xh_ready")
        la_full, la_free = sem("la_full"), sem("la_free")
        hi_done, wq_scaled = sem("hi_done"), sem("wq_scaled")
        stack_in = [[sem(f"stack_in{g}_{kind}") for kind in "kq"] for g in range(2)]
        mx_full, mx_red = sem("mx_full"), sem("mx_red")
        max_hi, max_split = sem("max_hi"), sem("max_split")
        mt_full, mt_evac = sem("mt_full"), sem("mt_evac")
        mrow_in = [sem("mrow_in0"), sem("mrow_in1")]
        st_full, st_masked, ex_done = sem("st_full"), sem("st_masked"), sem("ex_done")
        pv_done, ov_evac = sem("pv_done"), sem("ov_evac")
        ov_moved = [sem("ov_moved0"), sem("ov_moved1")]
        recip_done, at_ready = sem("recip_done"), sem("at_ready")
        op_full, op_evac, x_done = sem("op_full"), sem("op_evac"), sem("x_done")
        v_ones = sem("v_ones")
        fc_full, gelu_done, pr_full, pr_evac, ml_full, ml_evac = (
            sem("fc_full"), sem("gelu_done"), sem("pr_full"), sem("pr_evac"), sem("ml_full"), sem("ml_evac"))
        la3_full, la3_free = sem("la3_full"), sem("la3_free")
        hi3_done = sem("hi3_done")
        stack3_in = [[sem(f"stack3_in{bl}_{kind}") for kind in "kq"] for bl in range(2)]
        mx3_full, mx3_red = sem("mx3_full"), sem("mx3_red")
        max3_hi, max3_split = sem("max3_hi"), sem("max3_split")
        mt3_full, mt3_evac, mrow3_in = sem("mt3_full"), sem("mt3_evac"), sem("mrow3_in")
        st3_full, ex3_done, pv3_done = sem("st3_full"), sem("ex3_done"), sem("pv3_done")
        ov3_evac, rc3_done, at3_ready = sem("ov3_evac"), sem("rc3_done"), sem("at3_ready")
        bias3 = sem("bias3")
        op3_full, op3_evac = sem("op3_full"), sem("op3_evac")
        stack3_ones = sem("stack3_ones")
        stored = sem("stored")
        pool_init, ones_set = sem("pool_init"), sem("ones_set")

        def wait(eng, s, v):
            if not isinstance(v, int) or v > 0:
                eng.wait_ge(s, v)

        QUANT_STEPS = 18
        SCALED = {s: n + 1 for n, s in enumerate([*ATTN, SELF3])}

        def waits(eng, *pairs, apart=False):
            pairs = [(s, v if isinstance(v, int) else eng.to_reg(v)) for s, v in pairs]
            if apart and any(not isinstance(v, int) for _, v in pairs):
                eng.wait_ge(pool_ready, 1)
            for s, v in pairs:
                wait(eng, s, v)

        def brow_count(s):
            return 16 * sum(2 if x in ATTN_NO else 1 for x in range(s % 2, s + 1, 2))

        def addmask_of(s):
            return ATTN[s][2]

        def xt(b, t, n=1):
            return X[:, bass.ds(NT * b + t, n), :]

        def wq(s, m):
            return W[s % 2][:, 512 * m:512 * m + 512].rearrange("p (c o) -> p c o", c=NC)

        def stages(u):
            return dict(a=u < UNITS - 2, m=-1 <= u < UNITS - 1, b=0 <= u < UNITS, tail=u >= 1, op=u >= 2)

        def run_slots(eng, slot):
            for u in range(-2, 2):
                slot(u, u % 4, u // 2, (u // 2 + 1) // 2, stages(u))
            with eng.Fori(0, 3) as k:
                for n in range(4):
                    slot(4 * k + (2 + n), (2 + n) % 4, 2 * k + (1 + n // 2), k + 1, stages(2 + n))
            for u in range(UNITS - 2, UNITS + 1):
                slot(u, u % 4, u // 2, (u // 2 + 1) // 2, stages(u))

        J_T, J_K, J_Q, J_V, JOBS = 0, (2, 6), (3, 7), 4, 8

        def stages3(v):
            return dict(a=v < UNITS3 - 2, v=-1 <= v < UNITS3 - 1, m=-1 <= v < UNITS3 - 1, b=0 <= v < UNITS3,
                        tail=v >= 1, op=v >= 1, ln=v < UNITS3 - R3)

        def run_slots3(eng, slot):
            for v in range(-2, 1):
                slot(v, v % R3, v // R3, stages3(v))
            with eng.Fori(0, NB - 1) as k:
                for n in range(R3):
                    slot(R3 * k + (1 + n), (1 + n) % R3, k + (1 + n) // R3, stages3(1 + n))
            for v in range(UNITS3 - R3 + 1, UNITS3 + 1):
                slot(v, v % R3, v // R3, stages3(v))

        M_HEADS = ((0, 1), (2,), (3,), ())

        def jobs3(v, r, b):
            return 0 if isinstance(v, int) and v == -2 else 28 * b + (0, 6, 12, 22)[r] + 14

        def job3(v, r, b, name, n=0):
            first = 0 if isinstance(v, int) and v == -2 else 2
            tc, tx = (2, 2) if r == 2 else (0, 0)
            at = {("v", 0): 0, ("v", 1): 1, ("v", 2): 2, ("tc", 0): first, ("tc", 1): first + 1, ("kq", 0): first + tc,
                  ("tx", 0): first + tc + 1, ("tx", 1): first + tc + 2}
            at.update({("kq", k): first + tc + tx + k for k in (1, 2, 3)})
            return jobs3(v, r, b) + at[name, n]

        def norm3(b, which):
            return NB * SELF3 + 2 * b + which

        block = es.enter_context(nc.Block())

        @block.sync
        def _(sp):
            def load_weights(s):
                n = WCOLS if s in MLP_NO else WCOLS // 2
                sp.dma_start(W[s % 2][:, 0:n], wts[s]).then_inc(w_in[s], 16)
                if s in ATTN_NO:
                    r = R_V + ATTN_NO[s]
                    sp.dma_start(brow[:, s % 2, 0, :], rows_in[r:r + 1, :].broadcast_to([P, E])).then_inc(brow_in[s % 2], 16)
                load_output_bias(s)

            def load_output_bias(s):
                r = R_O + s
                sp.dma_start(brow[:, s % 2, 1, :], rows_in[r:r + 1, :].broadcast_to([P, E])).then_inc(brow_in[s % 2], 16)

            sp.dma_start(X[:, 0:NT, :], x_in[:, 0:NT, :]).then_inc(x_loaded, 16)
            sp.dma_start(cols[:, :], cols_in).then_inc(consts_in, 16)
            sp.dma_start(shp, shapes_in).then_inc(consts_in, 16)
            sp.dma_start(ident[:, :], shapes_in[:, C_ID:C_ID + P]).then_inc(consts_in, 16)
            load_weights(0)
            sp.dma_start(X[:, NT:NB * NT, :], x_in[:, NT:NB * NT, :]).then_inc(x_loaded, 16)

            def load_ctx(b, par):
                sp.dma_start(ctxT[:, par, :, :], ctx_in[:, bass.ds(NC * b, NC), :]).then_inc(ctx_in_sem[par], 16)

            def attention(s):
                cross, causal, addmask = ATTN[s]
                n = ATTN_NO[s]

                def slot(u, c, b, p, on):
                    half, U, GB = c % 2, UNITS * n + u, NB * n + b
                    if cross and half == 0 and on["op"] and on["a"]:
                        sp.wait_ge(la_full, JOBS * (GB - 1) + J_K[1] + 1)
                        load_ctx(b + 1, 1 - c // 2)
                    if on["stack1"]:
                        stack(U + 1, 1 - half, 1, GB + half)
                    if on["tail"]:
                        move(U - 1, 1 - half, 1, GB - 1 + half)
                    if on["b"]:
                        max_rows(U, half, 1)
                    if on["m"]:
                        max_rows(U + 1, 1 - half, 0)
                    if on["a"]:
                        stack(U + 2, half, 0, GB + 1)
                    if on["b"]:
                        move(U, half, 0, GB)

                def stack(U, half, g, GBj):
                    free = (st_full, 32 * (U - 2) + 16 * (g + 1))
                    for kind, parts in ((0, (hi, lo, hi)), (1, (hi, hi, lo))):
                        parts_in = (la_free, JOBS * GBj + (J_K, J_Q)[kind][half] + 1)
                        waits(sp, *([free, parts_in] if kind == 0 else [parts_in]))
                        at = (8 if kind == 0 else 0) + G * g
                        for r, part in enumerate(parts):
                            lo_p = 64 * half + HD * r
                            sp.dma_start(stk[lo_p:lo_p + HD, at:at + G, :].bitcast(F32),
                                         part[64 * g:64 * g + 64, kind, :].bitcast(F32)).then_inc(stack_in[g][kind], 16)

                def max_rows(U, half, g):
                    sp.wait_ge(mt_evac, 2 * U + g + 1)
                    lo_p = 64 * half + 3 * HD
                    sp.dma_start(stk[lo_p:lo_p + 2, G * g:G * g + G, :].bitcast(F32),
                                 mrows[32 * g:32 * g + 2 * G, :]).then_inc(mrow_in[g], 16)

                def move(U, half, g, GBu):
                    waits(sp, (ov_evac, 2 * U + g + 1),
                          (at_ready, BASE + U - 1),
                          (op_full, BASE + 2 * GBu))
                    sp.dma_start(raw[64 * g:64 * g + 64, half, :], ovs[0:P:2, g, :]).then_inc(ov_moved[g], 16)
                    sp.dma_start(sums[64 * g:64 * g + 64, half, :], ovs[1:P:2, g, :]).then_inc(ov_moved[g], 16)

                if cross:
                    load_ctx(0, 0)
                    load_ctx(1, 1)

                def with_stack1(u, c, b, p, on):
                    slot(u, c, b, p, dict(on, stack1=(not isinstance(u, int)) or -1 <= u < UNITS - 1))

                run_slots(sp, with_stack1)

            def layer3(s):
                for part in (2, 3):
                    sp.dma_start(W[0][:, 2048 * (part - 2):2048 * (part - 1)],
                                 wts[s][:, 2048 * part:2048 * part + 2048]).then_inc(w3_late, 16)

                def load_ctx_rows(b):
                    sp.dma_start(XH[:, :, :], ctx_rows_in[:, bass.ds(NT * b, NT), :]).then_inc(ctx_rows_loaded, 16)

                def slot(v, r, b, on):
                    par = r % 2
                    if r == 1 and on["ln"]:
                        load_ctx_rows(b + 1)
                    if on["a"]:
                        stack(v, r, b, 0)
                    if on["m"]:
                        sp.wait_ge(mt3_evac, v + 2)
                        at = 16 * (1 - par) + 4
                        sp.dma_start(stk[HS:HS + 2, at:at + G, :].bitcast(F32),
                                     mrows[32 * (1 - par):32 * (1 - par) + 2 * G, :]).then_inc(mrow3_in, 16)
                    if on["a"]:
                        stack(v, r, b, 1)
                    if on["op"] and r == 0:
                        store(b - 1)

                def stack(v, r, b, bl):
                    free = (st3_full, 16 * v + 8 * (bl + 1))
                    for kind, parts in ((0, (hi, hi, lo)), (1, (hi, lo, hi))):
                        parts_in = (la3_free, job3(v, r, b, "kq", 2 * bl + kind) + 1)
                        waits(sp, *([free, parts_in] if kind == 0 else [parts_in]))
                        for part, lo_p, form in zip(parts, (0, 64, 0), (0, 0, 1)):
                            at = 16 * (r % 2) + 8 * (1 - kind) + 4 * form + 2 * bl
                            sp.dma_start(stk[lo_p:lo_p + HS, at:at + 2, :].bitcast(F32),
                                         part[:, kind, :].bitcast(F32)).then_inc(stack3_in[bl][kind], 16)

                def store(b):
                    sp.wait_ge(x_done, NB * s + b + 1)
                    sp.dma_start(out[:, bass.ds(NT * b, NT), :], xt(b, 0, NT)).then_inc(stored, 16)

                load_ctx_rows(0)
                sp.wait_ge(stack3_ones, 3)
                run_slots3(sp, slot)
                sp.wait_ge(stored, 16 * NB)

            sp.wait_ge(pool_ready, 1)
            for s in range(8):
                wait(sp, x_done, NB * s)
                if s + 1 < SELF3:
                    load_weights(s + 1)
                elif s + 1 == SELF3:
                    sp.dma_start(W[1][:, :], wts[SELF3][:, 0:WCOLS]).then_inc(w_in[SELF3], 16)
                    load_output_bias(SELF3)
                if s == CROSS1:
                    sp.dma_start(mask_q, masks_in[:, 0:NT, :]).then_inc(masks_loaded, 16)
                    sp.dma_start(mask_k, masks_in[:, NT:2 * NT, :]).then_inc(masks_loaded, 16)
                if s in ATTN:
                    attention(s)
                elif s == SELF3:
                    layer3(s)

        @block.tensor
        def _(pe):
            def mm(o, l, r, start=True, stop=True):
                return nc.tensor.matmul(o, l, r, start=start, stop=stop)

            def transpose_x(s, b, c, bank):
                if c == 0:
                    pe.wait_ge(xh_ready, NB * s + b + 1)
                return turn_tiles(c, bank)

            def turn_tiles(c, bank):
                for t in range(NT):
                    last = nc.tensor.transpose(bank[:, P * t:P * t + P], XH[:, t, P * c:P * c + P], ident[:, :])
                return last

            def attention(s):
                cross, causal, addmask = ATTN[s]
                n = ATTN_NO[s]
                wk_, wv_, wq_, wo_ = wq(s, 1), wq(s, 2), wq(s, 0), wq(s, 3)

                def slot(u, c, b, p, on):
                    half, par = c % 2, c // 2
                    U, GB = UNITS * n + u, NB * n + b
                    b1, GB1 = b + 1, NB * n + b + 1
                    source = ctxT[:, 1 - par] if cross else hT
                    turned = 2 * U + (2 if on["b"] else 0) + (1 if on["m"] else 0)
                    for i in range(8):
                        g = i // 4
                        if on["m"] and i % 4 == 0:
                            for kind in range(2):
                                pe.wait_ge(stack_in[g][kind], 48 * (U + 2))
                        if on["b"] and i % 4 == 0:
                            pe.wait_ge(mrow_in[g], 16 * (U + 1))
                        for j in range(4):
                            if on["m"]:
                                max_tile(U + 1, 1 - half, i, j)
                            if on["b"]:
                                score_tile(U, half, i, j)
                            at = (i, j)
                            if j == 1 and on["b"] and i > 0:
                                values(U, half, par, i - 1)
                            if at == (0, 1) and on["tail"]:
                                values(U - 1, 1 - half, par if half else 1 - par, 7)
                            if at == (1, 0) and on["b"]:
                                turn_max(U, half, 1, 2 * (GB - 1 + half))
                            if at == (4, 0) and on["m"]:
                                turn_max(U + 1, 1 - half, 0, 2 * (GB - 1 + half))
                            if half == 0 and on["op"] and at in ((5, 0), (5, 2)):
                                project_out(GB - 1, 0, j // 2, turned)
                            if half == 0 and on["op"] and at in ((6, 2), (6, 3)):
                                project_out(GB - 1, 1, j - 2, turned)
                            if on["a"]:
                                if half == 0 and at in ((3, 0), (3, 2)):
                                    job(GB1, J_T + j // 2)
                                    transpose_x(s, b1, j // 2, LA).then_inc(la_full, 1)
                                if at in ((4, 2), (4, 3)):
                                    if cross and j == 2:
                                        pe.wait_ge(ctx_in_sem[1 - par], 16 * (4 * CROSS_NO[s] + p + 1))
                                    project(GB1, J_K[half], wk_, half, source, j - 2)
                                if at in ((5, 3), (6, 0)):
                                    project(GB1, J_Q[half], wq_, half, hT, i - 5)
                                if half == 0 and at in ((7, 0), (7, 2)):
                                    project_values(GB1, source, 0, j // 2)
                                if half == 1 and at in ((0, 2), (0, 3)):
                                    project_values(GB1, source, 1, j - 2)

                def job(GBj, k):
                    wait(pe, la_free, JOBS * GBj + k)

                def project(GBj, k, w, half, source, c):
                    if c == 0:
                        job(GBj, k)
                    last = mm(LA[:, :], w[:, c, P * half:P * half + P], source[:, c, :], c == 0, c == NC - 1)
                    if c == NC - 1:
                        last.then_inc(la_full, 1)

                def project_values(GBj, source, j, t):
                    if t == 0:
                        job(GBj, J_V + j)
                    tok = slice(P * (2 * j + t), P * (2 * j + t) + P)
                    for c in range(NC):
                        last = mm(LAt[:, t, :], source[:, c, tok], wv_[:, c, :], c == 0, c == NC - 1)
                    if t == 1:
                        last.then_inc(la_full, 1)

                def max_tile(U, half, i, qt):
                    at = 32 * U + 4 * i + qt
                    wait(pe, mx_red, at - 1)
                    lo_p, k_n = 64 * half, P * (qt + 1) if causal else S
                    q = stk[lo_p:lo_p + 3 * HD, i, P * qt:P * qt + P]
                    last = mm(MX[qt % 2][:, 0:k_n], q, stk[lo_p:lo_p + 3 * HD, 8 + i, 0:k_n], True, not causal)
                    if causal:
                        last = mm(MX[qt % 2][:, k_n - P:k_n], identb, shpb[:, C_MQ:C_MQ + P], False, True)
                    last.then_inc(mx_full, 1)

                def score_tile(U, half, i, h):
                    at, head, kt = 32 * U + 4 * i + h, G * (i // 4) + h, i % 4
                    wait(pe, ex_done, at - 1)
                    lo_p, q0 = 64 * half, P * kt if causal else 0
                    k = stk[lo_p:lo_p + ROWS, 8 + head, P * kt:P * kt + P]
                    last = mm(ST[h % 2][:, q0:S], k, stk[lo_p:lo_p + ROWS, head, q0:S], True, not causal)
                    if causal:
                        last = mm(ST[h % 2][:, q0:q0 + P], identb, shpb[:, C_MK:C_MK + P], False, True)
                    last.then_inc(st_full, 1)

                def values(U, half, vpar, i):
                    g, kt = i // 4, i % 4
                    if kt == 0:
                        wait(pe, ov_evac, 2 * U + g - 1)
                    pe.wait_ge(ex_done, 4 * (8 * U + i + 1))
                    q0 = P * kt if causal else 0
                    for h in range(G):
                        last = mm(OV[g][32 * h:32 * h + 32, q0:S], Vh[:, vpar, kt, 8 * half + G * g + h, :], Pr[:, i % 2, h, q0:S],
                                  kt == 0, kt == NT - 1)
                    last.then_inc(pv_done, 1)

                def turn_max(U, half, g, ops):
                    pe.wait_ge(max_split, 2 * U + g + 1)
                    wait(pe, mt_evac, 2 * U + g)
                    wait(pe, op_evac, BASE + ops)
                    for t in range(NT):
                        last = nc.tensor.transpose(LB[0:2 * G, P * t:P * t + P], mhl[:, half, g, t, :].bitcast(F32), ident[:, :])
                    last.then_inc(mt_full, 1)

                def project_out(GBo, j, t, turned):
                    if t == 0:
                        pe.wait_ge(at_ready, BASE + 2 * (GBo + 1))
                        wait(pe, mt_evac, turned)
                        wait(pe, op_evac, BASE + 2 * GBo + j)
                    tok = slice(P * (2 * j + t), P * (2 * j + t) + P)
                    for k in range(2):
                        last = mm(LBt[:, t, :], raw[:, k, tok], wo_[:, k, :], k == 0, k == 1)
                    if t == 1:
                        last.then_inc(op_full, 1)

                run_slots(pe, slot)

            def mlp(s):
                m = MLP_NO[s]
                wf = W[s % 2][:, 0:2048].rearrange("p (c o) -> p c o", c=NC)
                wp = W[s % 2][:, 2048:4096].rearrange("p (f o) -> p f o", f=NF)

                def turn(b):
                    MB = NB * m + b
                    for c, bank in enumerate((LA, LB)):
                        wait(pe, ml_evac, 2 * (MB - 1) + c + 1)
                        transpose_x(s, b, c, bank).then_inc(ml_full, 1)

                def batch(b, more):
                    MB = NB * m + b
                    pe.wait_ge(ml_evac, 2 * (MB + 1))
                    for f in range(NF):
                        wait(pe, gelu_done, NF * MB + f - 3)
                        for c in range(NC):
                            last = mm(FR[f % 4][:, :], wf[:, c, P * f:P * f + P], hT[:, c, :], c == 0, c == NC - 1)
                        last.then_inc(fc_full, 1)
                    if more:
                        turn(b + 1)
                    pe.wait_ge(gelu_done, NF * (MB + 1))
                    for j in range(2):
                        wait(pe, pr_evac, 2 * (MB - 1) + j + 1)
                        for t in range(2):
                            tok = slice(P * (2 * j + t), P * (2 * j + t) + P)
                            for f in range(NF):
                                last = mm(OV[j][:, E * t:E * t + E], h1T[:, f, tok], wp[:, f, :], f == 0, f == NF - 1)
                        last.then_inc(pr_full, 1)

                turn(0)
                batch(0, True)
                with pe.Fori(1, NB - 1) as b:
                    batch(b, True)
                batch(NB - 1, False)

            def layer3(s):
                w_q = W[1][:, 0:2048].rearrange("p (c o) -> p c o", c=NC)
                w_k = W[1][:, 2048:4096].rearrange("p (c o) -> p c o", c=NC)
                w_v = W[0][:, 0:2048].rearrange("p (c o) -> p c o", c=NC)
                w_o = W[0][:, 2048:4096].rearrange("p (k o) -> p k o", k=8)
                pe.wait_ge(wq_scaled, SCALED[s])
                pe.wait_ge(w3_late, 32)
                pe.wait_ge(stack3_ones, 3)
                pe.wait_ge(bias3, 1)
                for k in range(8):
                    last = mm(LB[:, 0:E], columns3[:, k, :], w_o[:, k, :], k == 0, k == 7)
                last.then_inc(bias3, 1)
                pe.wait_ge(bias3, 3)

                def slot(v, r, b, on):
                    par = r % 2
                    for i in range(4):
                        if i == 0:
                            if on["m"]:
                                for kind in range(2):
                                    pe.wait_ge(stack3_in[0][kind], 48 * (v + 2))
                            if on["b"]:
                                pe.wait_ge(mrow3_in, 16 * (v + 1))
                        if i == 1 and on["m"]:
                            for kind in range(2):
                                pe.wait_ge(stack3_in[1][kind], 48 * (v + 2))
                        tiles = [(h, qt) for h in M_HEADS[i] for qt in range(NT)] if on["m"] else []
                        for kt in range(NT):
                            for h, qt in tiles[len(tiles) * kt // 4:len(tiles) * (kt + 1) // 4]:
                                max_tile(v + 1, 1 - par, h, qt)
                            if on["b"]:
                                score_tile(v, par, i, kt)
                            at = (i, kt)
                            for key_tile in ((), (0,), (1,), (2, 3))[kt]:
                                if on["b"] and i > 0:
                                    values(v, par, i - 1, key_tile)
                            for key_tile in ((0, 1), (2, 3), (), ())[kt]:
                                if on["tail"] and i == 0:
                                    values(v - 1, 1 - par, 3, key_tile)
                            if on["v"] and at in ((0, 2), (1, 0)):
                                project_values(v, r, b, i)
                            if on["a"]:
                                if r == 2 and at in ((1, 1), (1, 2)):
                                    turn_batch(v, r, b, "tc", kt - 1)
                                if r == 2 and at in ((2, 1), (2, 2)):
                                    turn_batch(v, r, b, "tx", kt - 1)
                                if at in ((1, 3), (2, 3)):
                                    project(v, r, b, 0, i - 1)
                                if at in ((3, 1), (3, 3)):
                                    project(v, r, b, 1, kt // 2)
                            if r == 0 and on["op"]:
                                if at in ((2, 0), (2, 1)):
                                    project_out(b - 1, 0, kt, v)
                                if at in ((2, 3), (3, 0)):
                                    project_out(b - 1, 1, i - 2, v)
                            if on["m"] and at == (3, 2 if r == 0 else 0):
                                turn_max(v, r, b)

                def turn_max(v, r, b):
                    pe.wait_ge(max3_split, v + 2)
                    wait(pe, mt3_evac, v + 1)
                    wait(pe, op3_evac, BASE + 2 * b)
                    for t in range(NT):
                        last = nc.tensor.transpose(LB[0:2 * G, P * t:P * t + P],
                                                   mhl[:, (r + 1) % 2, 0, t, :].bitcast(F32), ident[:, :])
                    last.then_inc(mt3_full, 1)

                def project_values(v, r, b, j):
                    la(job3(v, r, b, "v", j))
                    rv = (r + 1) % R3
                    for t in range(2):
                        tok = slice(P * (2 * j + t), P * (2 * j + t) + P)
                        for c in range(NC):
                            last = mm(LAt[:, t, :], cT[:, c, tok], w_v[:, c, E * rv:E * rv + E], c == 0, c == NC - 1)
                    last.then_inc(la3_full, 1)

                def project(v, r, b, block, kind):
                    la(job3(v, r, b, "kq", 2 * block + kind))
                    bl = 2 * ((r + 2) % R3) + block
                    w, source = ((w_k, cT), (w_q, hT))[kind]
                    for c in range(NC):
                        last = mm(LA[:, :], w[:, c, P * bl:P * bl + P], source[:, c, :], c == 0, c == NC - 1)
                    last.then_inc(la3_full, 1)

                def turn_batch(v, r, b, name, c):
                    if c == 0:
                        pe.wait_ge(xh_ready, norm3(b + 1, 0 if name == "tc" else 1) + 1)
                    la(job3(v, r, b, name, c))
                    turn_tiles(c, LA).then_inc(la3_full, 1)

                def la(k):
                    wait(pe, la3_free, k)

                def max_tile(v, par, h, qt):
                    at, k_n = 16 * v + 4 * h + qt, P * (qt + 1)
                    wait(pe, mx3_red, at - 1)
                    bank, q = MX[qt % 2], 16 * par
                    tok = slice(P * qt, P * qt + P)
                    mm(bank[:, 0:k_n], stk[:, q + h, tok], stk[:, q + 8 + h, 0:k_n], True, False)
                    mm(bank[:, 0:k_n], stk[0:HS, q + 4 + h, tok], stk[0:HS, q + 12 + h, 0:k_n], False, False)
                    mm(bank[:, k_n - P:k_n], identb, shpb[:, C_MQ:C_MQ + P], False, True).then_inc(mx3_full, 1)

                def score_tile(v, par, h, kt):
                    at, q0 = 16 * v + 4 * h + kt, P * kt
                    wait(pe, ex3_done, at - 1)
                    bank, q = ST[kt % 2], 16 * par
                    tok = slice(P * kt, P * kt + P)
                    mm(bank[:, q0:S], stk[:, q + 8 + h, tok], stk[:, q + h, q0:S], True, False)
                    mm(bank[:, q0:S], stk[0:HS + 2, q + 12 + h, tok], stk[0:HS + 2, q + 4 + h, q0:S], False, False)
                    mm(bank[:, q0:q0 + P], identb, shpb[:, C_MK:C_MK + P], False, True).then_inc(st3_full, 1)

                def values(v, par, i, kt):
                    if i % 2 == 0 and kt == 0:
                        wait(pe, ov3_evac, 4 * v + i)
                    lo_p = HS * (i % 2)
                    pe.wait_ge(ex3_done, 16 * v + 4 * i + kt + 1)
                    for bank, w in ((OV[0], V3[:, par, kt, i, :]), (OV[1], ones3)):
                        last = mm(bank[lo_p:lo_p + HS, P * kt:S], w, Pr[:, i % 2, kt, P * kt:S], kt == 0, kt == NT - 1)
                    if kt == NT - 1:
                        last.then_inc(pv3_done, 1)

                def project_out(b, j, t, v):
                    if t == 0:
                        pe.wait_ge(at3_ready, 8 * (b + 1))
                        turned = v + 1 if not isinstance(v, int) or v < UNITS3 else UNITS3
                        pe.wait_ge(mt3_evac, turned)
                        wait(pe, op3_evac, BASE + 2 * b + j)
                    tok = slice(P * (2 * j + t), P * (2 * j + t) + P)
                    for k in range(8):
                        last = mm(LBt[:, t, :], AT3[:, k, tok], w_o[:, k, :], k == 0, k == 7)
                    if t == 1:
                        last.then_inc(op3_full, 1)

                run_slots3(pe, slot)

            pe.wait_ge(shapes_done, 1)
            pe.wait_ge(pool_ready, 1)
            for s in range(8):
                wait(pe, x_done, NB * s)
                pe.wait_ge(w_in[s], 16)
                if s in ATTN:
                    if s == CROSS1:
                        pe.wait_ge(quant, 4)
                        pe.wait_ge(ones_set, 1)
                        mm(LA[:, 0:4], ones, qabs[:, :]).then_inc(quant_pe, 1)
                        pe.wait_ge(quant, QUANT_STEPS)
                    pe.wait_ge(wq_scaled, SCALED[s])
                    pe.wait_ge(v_ones, 2 if s >= CROSS1 else 1)
                    attention(s)
                elif s in MLP_NO:
                    mlp(s)
                else:
                    layer3(s)

        @block.scalar
        def _(act):
            def scale_shift(s, c):
                g, o = C_G + 2 * s + c, C_B + 2 * s + c
                return dict(scale=cols[:, g:g + 1], bias=cols[:, o:o + 1])

            def attention(s):
                cross, causal, addmask = ATTN[s]
                n = ATTN_NO[s]

                def slot(u, c, b, p, on):
                    half, U, GB1 = c % 2, UNITS * n + u, NB * n + b + 1
                    for i in range(8):
                        for h in range(G):
                            if on["b"]:
                                exp_tile(u, U, i, h)
                            at = (i, h)
                            if at == (1, 0) and on["tail"]:
                                product_out(U - 1, 1)
                            if at == (1, 1) and on["b"]:
                                rows_out(U, 1)
                            if at == (4, 1) and on["m"]:
                                rows_out(U + 1, 0)
                            if at == (5, 0) and on["b"]:
                                product_out(U, 0)
                            if half == 0 and at in ((3, 1), (3, 3)) and on["a"]:
                                c = h // 2
                                act.wait_ge(la_full, JOBS * GB1 + J_T + c + 1)
                                nc.scalar.activation(hT[:, c, :], LA[:, :], ACT.Identity, **scale_shift(s, c)).then_inc(la_free, 1)
                            if at in ((5, 0), (6, 1)) and on["a"]:
                                high_part(U, GB1, half, i - 5)

                def high_part(U, GBj, half, kind):
                    act.wait_ge(la_full, JOBS * GBj + (J_K, J_Q)[kind][half] + 1)
                    for g in range(2):
                        wait(act, stack_in[g][kind], 48 * (U + 2))
                    at = (C_K, C_Q)[kind] + 2 * n + half
                    nc.scalar.activation(hi[:, kind, :], LA[:, :], ACT.Identity, bias=cols[:, at:at + 1]).then_inc(hi_done, 1)

                def product_out(U, g):
                    act.wait_ge(pv_done, 8 * U + 4 * (g + 1))
                    wait(act, ov_moved[g], 32 * U)
                    nc.scalar.activation(ovs[:, g, :], OV[g][:, :], ACT.Copy).then_inc(ov_evac, 1)

                def exp_tile(u, U, i, h):
                    at, q0 = 32 * U + 4 * i + h, P * (i % 4) if causal else 0
                    if h == 0:
                        wait(act, pv_done, 8 * U + i - 1)
                    if addmask:
                        act.wait_ge(st_masked, 32 * u + 4 * i + h + 1)
                    else:
                        act.wait_ge(st_full, at + 1)
                    nc.scalar.activation(Pr[:, i % 2, h, q0:S], ST[h % 2][:, q0:S], ACT.Exp).then_inc(ex_done, 1)

                def rows_out(U, g):
                    act.wait_ge(mt_full, 2 * U + g + 1)
                    wait(act, mrow_in[g], 16 * U)
                    nc.scalar.activation(mrows[32 * g:32 * g + 2 * G, :], LB[0:2 * G, :], ACT.Copy).then_inc(mt_evac, 1)

                run_slots(act, slot)

            def mlp(s):
                m = MLP_NO[s]

                def turned(b):
                    for c, bank in enumerate((LA, LB)):
                        act.wait_ge(ml_full, 2 * (NB * m + b) + c + 1)
                        nc.scalar.activation(hT[:, c, :], bank[:, :], ACT.Identity, **scale_shift(s, c)).then_inc(ml_evac, 1)

                def batch(b, more):
                    for f in range(NF):
                        at = C_F + NF * m + f
                        act.wait_ge(fc_full, NF * (NB * m + b) + f + 1)
                        nc.scalar.activation(h1T[:, f, :], FR[f % 4][:, :], ACT.Gelu,
                                             bias=cols[:, at:at + 1]).then_inc(gelu_done, 1)
                    if more:
                        turned(b + 1)

                turned(0)
                batch(0, True)
                with act.Fori(1, NB - 1) as b:
                    batch(b, True)
                batch(NB - 1, False)

            def layer3(s):
                def slot(v, r, b, on):
                    par = r % 2
                    for i in range(4):
                        for kt in range(NT):
                            if on["b"]:
                                exp_tile(v, i, kt)
                            at = (i, kt)
                            if at == (1, 0) and on["tail"]:
                                pair_out(v - 1, (r - 1) % R3, b, 1)
                            if at == (3, 0) and on["b"]:
                                pair_out(v, r, b, 0)
                            if on["a"]:
                                if r == 2 and at in ((1, 1), (1, 2)):
                                    turned(v, r, b, "tc", kt - 1, cT)
                                if r == 2 and at in ((2, 1), (2, 2)):
                                    turned(v, r, b, "tx", kt - 1, hT)
                                if at in ((2, 0), (3, 0)):
                                    high_part(v, r, b, 0, i - 2)
                                if at in ((3, 2), (3, 3)):
                                    high_part(v, r, b, 1, kt - 2)
                            if at == (3, 2 if r == 0 else 0) and on["m"]:
                                rows_out(v, par)

                def exp_tile(v, i, kt):
                    if kt == 0:
                        wait(act, pv3_done, 4 * v + i - 1)
                    act.wait_ge(st3_full, 16 * v + 4 * i + kt + 1)
                    nc.scalar.activation(Pr[:, i % 2, kt, P * kt:S], ST[kt % 2][:, P * kt:S], ACT.Exp).then_inc(ex3_done, 1)

                def turned(v, r, b, name, c, to):
                    act.wait_ge(la3_full, job3(v, r, b, name, c) + 1)
                    nc.scalar.activation(to[:, c, :], LA[:, :], ACT.Identity, **scale_shift(s, c)).then_inc(la3_free, 1)

                def high_part(v, r, b, block, kind):
                    act.wait_ge(la3_full, job3(v, r, b, "kq", 2 * block + kind) + 1)
                    wait(act, stack3_in[1 - block][kind], 48 * (v + 2 + block))
                    at = (C_K3, C_Q3)[kind] + 2 * ((r + 2) % R3) + block
                    nc.scalar.activation(hi[:, kind, :], LA[:, :], ACT.Identity, bias=cols[:, at:at + 1]).then_inc(hi3_done, 1)

                def rows_out(v, par):
                    act.wait_ge(mt3_full, v + 2)
                    wait(act, mrow3_in, 16 * (v + 1))
                    lo_p = 32 * (1 - par)
                    nc.scalar.activation(mrows[lo_p:lo_p + 2 * G, :], LB[0:2 * G, :], ACT.Copy).then_inc(mt3_evac, 1)

                def pair_out(v, r, b, j):
                    act.wait_ge(pv3_done, 4 * v + 2 * j + 2)
                    if r == 0 and j == 0:
                        wait(act, op3_full, 2 * b)
                    nc.scalar.activation(AT3[:, 2 * r + j, :], OV[0][:, :], ACT.Copy).then_inc(ov3_evac, 1)
                    wait(act, at3_ready, 2 * v + j - 1)
                    nc.scalar.activation(sums[:, j, :], OV[1][:, :], ACT.Copy).then_inc(ov3_evac, 1)

                run_slots3(act, slot)

            act.wait_ge(pool_ready, 1)
            for s in range(8):
                wait(act, x_done, NB * s)
                if s in ATTN:
                    attention(s)
                elif s in MLP_NO:
                    mlp(s)
                else:
                    layer3(s)

        @block.vector
        def _(dve):
            def statistics(N, rows, t):
                if t == 0:
                    wait(dve, ln_mv, NT * N)
                nc.vector.bn_stats(st6[:, t, :], rows).then_inc(ln_stats, 1)

            def combine(N):
                waits(dve, (xh_ready, N), apart=True)
                for t in range(NT):
                    waits(dve, (ln_stats, NT * N + t + 1), apart=True)
                    nc.vector.bn_aggr(mv[:, t, :], st6[:, t, :]).then_inc(ln_mv, 1)

            def layer_norm(N, tile):
                for t in range(NT):
                    statistics(N, tile(t), t)
                combine(N)

            def layer_norm_x(N, b):
                layer_norm(N, lambda t: xt(b, t))

            def add_to_x(b, j, bank, done):
                nc.vector.tensor_tensor(xt(b, 2 * j, 2), bank, xt(b, 2 * j, 2), ALU.add).then_inc(done, 1)

            def attention(s):
                cross, causal, addmask = ATTN[s]
                n = ATTN_NO[s]

                def slot(u, c, b, p, on):
                    half, par = c % 2, c // 2
                    U, GB = UNITS * n + u, NB * n + b
                    for i in range(8):
                        if on["m"] and i % 4 == 0:
                            wait(dve, max_split, 2 * (U + 1) - 3 + i // 4)
                        for j in range(4):
                            if on["m"]:
                                max_tile(U + 1, 1 - half, i, j)
                            if on["b"] and addmask:
                                add_mask(u, U, i, j)
                            at = (i, j)
                            if i == 0 and half == 0 and on["a"]:
                                statistics(NB * s + b + 1, xt(b + 1, j), j)
                            if at == (1, 3) and half == 0 and on["a"]:
                                combine(NB * s + b + 1)
                            if i == 2 and on["tail"]:
                                invert(U, 1 - half, j)
                            if at in ((5, 1), (6, 2)) and on["a"]:
                                low_part(U, half, i - 5)
                            if at in ((6, 0), (7, 1)) and half == 0 and on["op"]:
                                dve.wait_ge(op_full, BASE + 2 * (GB - 1) + i - 5)
                                add_to_x(b - 1, i - 6, LBt, op_evac)
                            if at == (7, 3) and half == 0 and on["a"]:
                                values_out(GB + 1, 1 - par, 0)
                            if at == (1, 1) and half == 1 and on["a"]:
                                values_out(GB + 1, 1 - par, 1)

                def max_tile(U, half, i, qt):
                    at = 32 * U + 4 * i + qt
                    waits(dve, (mx_full, at + 1), apart=addmask)
                    bank, m = MX[qt % 2], mx[:, half, i // 4, qt, i % 4:i % 4 + 1]
                    if addmask:
                        nc.vector.tensor_tensor_reduce(bank[:, :], bank[:, :], mask_q[:, qt, :], 1.0, -3.0e38,
                                                       ALU.add, ALU.max, m).then_inc(mx_red, 1)
                    else:
                        k_n = P * (qt + 1) if causal else S
                        nc.vector.tensor_reduce(m, bank[:, 0:k_n], AX.X, ALU.max).then_inc(mx_red, 1)

                def add_mask(u, U, i, h):
                    at = 32 * U + 4 * i + h
                    dve.wait_ge(st_full, at + 1)
                    nc.vector.tensor_tensor(ST[h % 2][:, :], ST[h % 2][:, :], mask_k[:, i % 4, :],
                                            ALU.add).then_inc(st_masked, 1)

                def invert(U, half, j):
                    if j == 0:
                        dve.wait_ge(ov_moved[0], 32 * U)
                        dve.wait_ge(ov_moved[1], 32 * U)
                    part = sums[:, half, P * j:P * j + P]
                    nc.vector.reciprocal(part, part).then_inc(recip_done, 1)

                def low_part(U, half, kind):
                    dve.wait_ge(hi_done, 2 * (U + 2) + kind + 1)
                    at = (C_K, C_Q)[kind] + 2 * n + half
                    nc.vector.scalar_tensor_tensor(lo[:, kind, :], LA[:, :], cols[:, at:at + 1], hi[:, kind, :].bitcast(F32),
                                                   ALU.add, ALU.subtract).then_inc(la_free, 1)

                def values_out(GBj, vpar, j):
                    dve.wait_ge(la_full, JOBS * GBj + J_V + j + 1)
                    to = Vh[:, vpar, 2 * j:2 * j + 2, :, :].rearrange("p t h (d two) -> p t h d two", two=2)[:, :, :, :, 0]
                    bias = brow[:, s % 2, 0:1, :].rearrange("p t (h d) -> p t h d", h=H).broadcast_to([P, 2, H, HD])
                    nc.vector.tensor_tensor(to, LAt[:, :, :].rearrange("p t (h d) -> p t h d", h=H), bias, ALU.add).then_inc(la_free, 1)

                run_slots(dve, slot)

            def mlp(s):
                m = MLP_NO[s]

                def batch(b, more):
                    if more:
                        layer_norm_x(NB * s + b + 1, b + 1)
                    for j in range(2):
                        dve.wait_ge(pr_full, 2 * (NB * m + b) + j + 1)
                        add_to_x(b, j, OV[j][:, :].rearrange("p (t n) -> p t n", t=2), pr_evac)

                layer_norm_x(NB * s, 0)
                batch(0, True)
                with dve.Fori(1, NB - 1) as b:
                    batch(b, True)
                batch(NB - 1, False)

            def scale_queries(s, w, width):
                dve.wait_ge(w_in[s], 16)
                nc.vector.tensor_scalar(w, w, width ** -0.5, None, ALU.mult).then_inc(wq_scaled, 1)

            def quantize():
                w = W[CROSS1 % 2]
                up, down = Pr[:, 0, :, :], Pr[:, 1, :, :]
                gam, thr, neg = qst[:, 0:4], qst[:, 4:8], qst[:, 8:12]
                wm = w[:, 0:2048].rearrange("p (m n) -> p m n", m=4)
                dve.wait_ge(w_in[CROSS1], 16)
                nc.vector.tensor_reduce(qabs[:, :], wm, AX.X, ALU.add, apply_absolute_value=True).then_inc(quant, 4)
                dve.wait_ge(quant_pe, 1)
                nc.vector.tensor_scalar(gam, LA[:, 0:4], 1.0 / (E * E), None, ALU.mult).then_inc(quant, 1)
                dve.wait_ge(quant, 5)
                nc.vector.tensor_scalar(thr, gam, 1e-5, 0.5, ALU.add, ALU.mult).then_inc(quant, 1)
                dve.wait_ge(quant, 6)
                nc.vector.tensor_scalar(neg, thr, -1.0, None, ALU.mult).then_inc(quant, 1)
                dve.wait_ge(quant, 7)
                for k in range(4):
                    nc.vector.tensor_scalar(up[:, k, :], wm[:, k, :], thr[:, k:k + 1], gam[:, k:k + 1],
                                            ALU.is_gt, ALU.mult).then_inc(quant, 1)
                    nc.vector.tensor_scalar(down[:, k, :], wm[:, k, :], neg[:, k:k + 1], gam[:, k:k + 1],
                                            ALU.is_lt, ALU.mult).then_inc(quant, 1)
                dve.wait_ge(quant, 15)
                nc.vector.tensor_tensor(up, up, down, ALU.subtract).then_inc(quant, 1)
                dve.wait_ge(quant, 16)
                nc.vector.tensor_tensor(up, up, wm, ALU.subtract).then_inc(quant, 1)
                dve.wait_ge(quant, 17)
                nc.vector.tensor_tensor(wm, wm, up, ALU.add).then_inc(quant, 1)

            def layer3(s):
                def slot(v, r, b, on):
                    par = r % 2
                    for i in range(4):
                        tiles = [(h, qt) for h in M_HEADS[i] for qt in range(NT)] if on["m"] else []
                        if i == 0 and on["m"]:
                            wait(dve, max3_split, v)
                        for kt in range(NT):
                            for h, qt in tiles[len(tiles) * kt // 4:len(tiles) * (kt + 1) // 4]:
                                dve.wait_ge(mx3_full, 16 * (v + 1) + 4 * h + qt + 1)
                                nc.vector.tensor_reduce(mx[:, 1 - par, 0, qt, h:h + 1], MX[qt % 2][:, 0:P * (qt + 1)],
                                                        AX.X, ALU.max).then_inc(mx3_red, 1)
                            at = (i, kt)
                            if on["v"] and at in ((0, 3), (1, 1)):
                                values_out(v, r, b, par, i, on)
                            if i == 1 and on["tail"]:
                                invert(v - 1, 1, kt)
                            if i == 3 and on["b"]:
                                invert(v, 0, kt)
                            if on["a"]:
                                if at in ((2, 0), (3, 0)):
                                    low_part(v, r, 0, i - 2)
                                if at in ((3, 2), (3, 3)):
                                    low_part(v, r, 1, kt - 2)
                            if r == 0 and on["op"] and at in ((2, 2), (3, 1)):
                                add_out(b - 1, i - 2)
                        if i == 2 and r == 1 and on["ln"]:
                            norm_ctx(b + 1)
                        if i == 0 and r == 2 and on["a"] and on["b"]:
                            norm_x(b + 1)

                def values_out(v, r, b, par, j, on):
                    if on["tail"] and j == 0:
                        dve.wait_ge(pv3_done, 4 * v)
                    dve.wait_ge(la3_full, job3(v, r, b, "v", j) + 1)
                    nc.vector.tensor_copy(V3[:, 1 - par, 2 * j:2 * j + 2, :, :],
                                          LAt[:, :, :].rearrange("p t (h d) -> p t h d", h=G)).then_inc(la3_free, 1)

                def invert(v, j, quarter):
                    if quarter == 0:
                        dve.wait_ge(ov3_evac, 4 * v + 2 * j + 2)
                    part = sums[:, j, P * quarter:P * quarter + P]
                    nc.vector.reciprocal(part, part).then_inc(rc3_done, 1)

                def add_out(b, j):
                    dve.wait_ge(op3_full, 2 * b + j + 1)
                    add_to_x(b, j, LBt, op3_evac)

                def low_part(v, r, bl, kind):
                    dve.wait_ge(hi3_done, 2 * (2 * (v + 2) + bl) + kind + 1)
                    at = (C_K3, C_Q3)[kind] + 2 * ((r + 2) % R3) + bl
                    nc.vector.scalar_tensor_tensor(lo[:, kind, :], LA[:, :], cols[:, at:at + 1], hi[:, kind, :].bitcast(F32),
                                                   ALU.add, ALU.subtract).then_inc(la3_free, 1)

                def norm_ctx(b):
                    dve.wait_ge(ctx_rows_loaded, 16 * (b + 1))
                    layer_norm(norm3(b, 0), lambda t: XH[:, t, :])

                def norm_x(b):
                    layer_norm_x(norm3(b, 1), b)

                nc.vector.tensor_copy(columns3, cols[:, C_V:C_V + 8].rearrange("p (k a) -> p k a", a=1).broadcast_to([P, 8, P])
                                      ).then_inc(bias3, 1)
                dve.wait_ge(bias3, 2)
                row = brow[:, SELF3 % 2, 1, :]
                nc.vector.tensor_tensor(row, LB[:, 0:E], row, ALU.add).then_inc(bias3, 1)
                norm_ctx(0)
                norm_x(0)
                run_slots3(dve, slot)

            dve.wait_ge(consts_in, 48)
            for n, done in enumerate((op_full, op_evac, op3_evac, at_ready)):
                nc.vector.memset(qst[:, n:n + 1], 0.0).then_inc(done, BASE)
            nc.vector.tensor_copy(shpb[:, :], shp).then_inc(shapes_done, 1)
            dve.wait_ge(x_loaded, 32)
            dve.wait_ge(shapes_done, 1)
            for s in range(8):
                wait(dve, x_done, NB * s)
                dve.wait_ge(brow_in[s % 2], brow_count(s))
                if s in ATTN:
                    if s == CROSS1:
                        quantize()
                        dve.wait_ge(quant, QUANT_STEPS)
                    scale_queries(s, W[s % 2][:, 0:512], HD)
                    if addmask_of(s):
                        dve.wait_ge(masks_loaded, 32)
                    attention(s)
                elif s in MLP_NO:
                    mlp(s)
                else:
                    scale_queries(s, W[s % 2][:, 0:2048], HS)
                    layer3(s)

        @block.gpsimd
        def _(pool):
            def layer_norm(N, rows, turned=None, turned_at=0):
                waits(pool, (ln_mv, NT * (N + 1)),
                      (xh_ready, N), apart=True)
                nc.gpsimd.tensor_scalar(rstd[:, 0, :], mv[:, :, 1], EPS, None, ALU.add).then_inc(ln_pool, 1)
                pool.wait_ge(ln_pool, 3 * N + 1)
                nc.gpsimd.tensor_tensor(rstd[:, 1, :], rstd[:, 0, :], mhalf[:, :], ALU.pow).then_inc(ln_pool, 1)
                pool.wait_ge(ln_pool, 3 * N + 2)
                if turned is not None:
                    wait(pool, turned, turned_at)
                nc.gpsimd.tensor_tensor(XH[:, :, :], rows, mv[:, :, 0:1].broadcast_to([P, NT, E]),
                                        ALU.subtract).then_inc(ln_pool, 1)
                pool.wait_ge(ln_pool, 3 * N + 3)
                nc.gpsimd.tensor_tensor(XH[:, :, :], XH[:, :, :], rstd[:, 1, :].rearrange("p (t a) -> p t a", a=1).broadcast_to([P, NT, E]),
                                        ALU.mult).then_inc(xh_ready, 1)

            def add_bias(s, b):
                bias = brow[:, s % 2, 1:2, :].broadcast_to([P, NT, E])
                nc.gpsimd.tensor_tensor(xt(b, 0, NT), xt(b, 0, NT), bias, ALU.add).then_inc(x_done, 1)

            def split_max(half, g, hi_sem, lo_sem, at):
                nc.gpsimd.tensor_copy(mhl[:, half, g, :, 0:G], mx[:, half, g, :, :]).then_inc(hi_sem, 1)
                pool.wait_ge(hi_sem, at + 1)
                nc.gpsimd.tensor_tensor(mhl[:, half, g, :, G:2 * G], mx[:, half, g, :, :],
                                        mhl[:, half, g, :, 0:G].bitcast(F32), ALU.subtract).then_inc(lo_sem, 1)

            def attention(s):
                n = ATTN_NO[s]

                def slot(u, c, b, p, on):
                    half = c % 2
                    U, GB = UNITS * n + u, NB * n + b
                    if on["b"]:
                        maxima(U, half, 1)
                    if half == 0 and on["a"]:
                        layer_norm(NB * s + b + 1, xt(b + 1, 0, NT), la_full, JOBS * GB + 2)
                    if on["tail"]:
                        pool.wait_ge(recip_done, 4 * U)
                        nc.gpsimd.tensor_tensor(raw[:, 1 - half, :], raw[:, 1 - half, :], sums[:, 1 - half, :],
                                                ALU.mult).then_inc(at_ready, 1)
                    if on["m"]:
                        maxima(U + 1, 1 - half, 0)
                    if half == 0 and on["op"]:
                        pool.wait_ge(op_evac, BASE + 2 * GB)
                        add_bias(s, b - 1)

                def maxima(U, half, g):
                    waits(pool, (mx_red, 32 * U + 16 * (g + 1)),
                          (mt_full, 2 * (U - 2) + g + 1), apart=True)
                    split_max(half, g, max_hi, max_split, 2 * U + g)

                run_slots(pool, slot)

            def mlp(s):
                m = MLP_NO[s]

                def batch(b, more):
                    if more:
                        layer_norm(NB * s + b + 1, xt(b + 1, 0, NT), ml_full, 2 * (NB * m + b + 1))
                    pool.wait_ge(pr_evac, 2 * (NB * m + b + 1))
                    add_bias(s, b)

                layer_norm(NB * s, xt(0, 0, NT))
                batch(0, True)
                with pool.Fori(1, NB - 1) as b:
                    batch(b, True)
                batch(NB - 1, False)

            def layer3(s):
                def slot(v, r, b, on):
                    par = r % 2
                    if r == 2 and on["a"]:
                        layer_norm(norm3(b + 1, 1), xt(b + 1, 0, NT), la3_full, job3(v, r, b, "tc", 1) + 1)
                    if on["tail"]:
                        normalize(v - 1, (r - 1) % R3, 1)
                    if r == 1 and on["ln"]:
                        layer_norm(norm3(b + 1, 0), XH[:, :, :])
                    if on["m"]:
                        waits(pool, (mx3_red, 16 * (v + 2)),
                              (mt3_full, v), apart=True)
                        split_max(1 - par, 0, max3_hi, max3_split, v + 1)
                    if r == 0 and on["op"]:
                        pool.wait_ge(op3_evac, BASE + 2 * b)
                        add_bias(s, b - 1)
                    if on["b"]:
                        normalize(v, r, 0)

                def normalize(v, r, j):
                    pool.wait_ge(rc3_done, 8 * v + 4 * (j + 1))
                    pair = AT3[:, 2 * r + j, :]
                    nc.gpsimd.tensor_tensor(pair, pair, sums[:, j, :], ALU.mult).then_inc(at3_ready, 1)

                nc.gpsimd.memset(ones3, 1.0).then_inc(stack3_ones, 1)
                for par in range(2):
                    pool.wait_ge(stack3_ones, par + 1)
                    nc.gpsimd.memset(stk[HS:P, 16 * par + 12:16 * par + 16, :].bitcast(F32), -1.0).then_inc(stack3_ones, 1)
                pool.wait_ge(stack3_ones, 3)
                layer_norm(norm3(0, 0), XH[:, :, :])
                pool.wait_ge(bias3, 3)
                run_slots3(pool, slot)

            def columns_of_one():
                ones_at = Vh[:, :, :, :, :].rearrange("p a t h (d two) -> p (a t h) d two", two=2)[:, :, :, 1]
                nc.gpsimd.memset(ones_at, 1.0).then_inc(v_ones, 1)

            nc.gpsimd.memset(mhalf[:, :], -0.5).then_inc(pool_init, 1)
            for half in range(2):
                lo_p = 64 * half + 32
                pool.wait_ge(pool_init, half + 1)
                nc.gpsimd.memset(stk[lo_p:lo_p + 32, 8:16, :].bitcast(F32), -1.0).then_inc(pool_init, 1)
            pool.wait_ge(pool_init, 3)
            columns_of_one()
            pool.wait_ge(v_ones, 1)
            pool.wait_ge(consts_in, 48)
            nc.gpsimd.tensor_scalar(cols[:, C_Q:C_Q + 10], cols[:, C_Q:C_Q + 10], HD ** -0.5, None, ALU.mult).then_inc(pool_init, 1)
            pool.wait_ge(pool_init, 4)
            nc.gpsimd.tensor_scalar(cols[:, C_Q3:C_Q3 + 8], cols[:, C_Q3:C_Q3 + 8], HS ** -0.5, None, ALU.mult).then_inc(pool_init, 1)
            pool.wait_ge(pool_init, 5)
            pool.wait_ge(x_loaded, 32)
            nc.gpsimd.memset(qst[:, 12:16], 0.0).then_inc(pool_ready, 1)
            for s in range(8):
                wait(pool, x_done, NB * s)
                if s in ATTN:
                    if s == CROSS1:
                        nc.gpsimd.memset(ones, 1.0).then_inc(ones_set, 1)
                        pool.wait_ge(ones_set, 1)
                        columns_of_one()
                        pool.wait_ge(v_ones, 2)
                    attention(s)
                elif s in MLP_NO:
                    mlp(s)
                else:
                    layer3(s)


ATTN_NAMES = {SELF0: ("L0_xattn_ln1_g", "L0_xattn_ln1_b", None, "L0_xattn_attn_proj_w", None, "L0_xattn_attn_proj_b"),
              CROSS0: ("L0_xattn_ln2_g", "L0_xattn_ln2_b", ("L0_xattn_q_w", "L0_xattn_k_w", "L0_xattn_v_w"),
                       "L0_xattn_ca_proj_w", ("L0_xattn_q_b", "L0_xattn_k_b", "L0_xattn_v_b"), "L0_xattn_ca_proj_b"),
              CROSS1: ("L1_xattn_ln_gamma", "L1_xattn_ln_beta", ("L1_xattn_Wq", "L1_xattn_Wk", "L1_xattn_Wv"),
                       "L1_xattn_Wo", ("L1_xattn_bq", "L1_xattn_bk", "L1_xattn_bv"), "L1_xattn_bo"),
              SELF2: ("L2_xattn_attn_ln_w", "L2_xattn_attn_ln_b", ("L2_xattn_q_w", "L2_xattn_k_w", "L2_xattn_v_w"),
                      "L2_xattn_o_w", ("L2_xattn_q_b", None, "L2_xattn_v_b"), "L2_xattn_o_b"),
              CROSS2: ("L2_xattn_cross_ln_w", "L2_xattn_cross_ln_b", ("L2_xattn_cq_w", "L2_xattn_ck_w", "L2_xattn_cv_w"),
                       "L2_xattn_co_w", ("L2_xattn_cq_b", None, "L2_xattn_cv_b"), "L2_xattn_co_b")}
MLP_NAMES = {MLP0: ("L0_xattn_ln3_g", "L0_xattn_ln3_b", "L0_xattn_fc_w", "L0_xattn_fc_b", "L0_xattn_proj_w", "L0_xattn_proj_b"),
             MLP2: ("L2_xattn_mlp_ln_w", "L2_xattn_mlp_ln_b", "L2_xattn_fc1_w", "L2_xattn_fc1_b", "L2_xattn_fc2_w",
                    "L2_xattn_fc2_b")}


def by_partition(w):
    return w.reshape(-1, P, w.shape[1]).transpose(1, 0, 2).reshape(P, -1)


def head_order():
    return np.arange(E).reshape(2, 2, G, HD).transpose(0, 1, 3, 2).reshape(-1)


def head_order3():
    return np.arange(H * HS).reshape(H // 2, 2, HS).transpose(0, 2, 1).reshape(-1)


def kernel(**inputs):
    import concourse.bacc as bacc
    from concourse.bass_utils import run_bass_kernel_spmd

    a = {k: np.asarray(v) for k, v in inputs.items()}
    zero = np.zeros(E, np.float32)
    order, order3 = head_order(), head_order3()
    weights, cols, rows = [None] * 8, np.zeros((P, N_COLS), np.float32), np.zeros((N_ROWS, E), np.float32)

    def put(at, vector):
        cols[:, at:at + vector.size // P] = vector.reshape(-1, P).T

    for s, (g, o, qkv, wo, qkv_b, bo) in ATTN_NAMES.items():
        if qkv is None:
            q_w, k_w, v_w = np.split(a["L0_xattn_attn_qkv_w"], 3)
            q_b, k_b, v_b = np.split(a["L0_xattn_attn_qkv_b"], 3)
        else:
            q_w, k_w, v_w = (a[x] for x in qkv)
            q_b, k_b, v_b = (zero if x is None else a[x] for x in qkv_b)
        weights[s] = np.concatenate([by_partition(q_w[order].T), by_partition(k_w[order].T), by_partition(v_w.T),
                                     by_partition(a[wo].T)], axis=1)
        put(C_Q + 2 * ATTN_NO[s], q_b[order])
        put(C_K + 2 * ATTN_NO[s], k_b[order])
        rows[R_V + ATTN_NO[s]], rows[R_O + s] = v_b, a[bo]
        put(C_G + 2 * s, a[g])
        put(C_B + 2 * s, a[o])
    for s, (g, o, fw, fb, pw, pb_) in MLP_NAMES.items():
        weights[s] = np.concatenate([by_partition(a[fw].T), by_partition(a[pw].T)], axis=1)
        put(C_F + NF * MLP_NO[s], a[fb])
        rows[R_O + s] = a[pb_]
        put(C_G + 2 * s, a[g])
        put(C_B + 2 * s, a[o])
    k3, v3 = np.split(a["L3_xattn_wkv"], 2, axis=1)
    kb3, vb3 = np.split(a["L3_xattn_bkv"], 2)
    weights[SELF3] = np.concatenate([by_partition(a["L3_xattn_wq"][:, order3]), by_partition(k3[:, order3]),
                                     by_partition(v3), by_partition(a["L3_xattn_wo"])], axis=1)
    put(C_Q3, a["L3_xattn_bq"][order3])
    put(C_K3, kb3[order3])
    put(C_V, vb3)
    rows[R_O + SELF3] = a["L3_xattn_bo"]
    put(C_G + 2 * SELF3, a["L3_xattn_ln_g"])
    put(C_B + 2 * SELF3, a["L3_xattn_ln_b"])

    later = np.triu(np.full((P, P), NEG, np.float32), 1)
    arrays = {
        "x_t": a["x"].reshape(NB * NT, P, E).transpose(1, 0, 2),
        "ctx_t": a["ctx_1024"].transpose(2, 0, 1).reshape(NC, P, NB, S).transpose(1, 2, 0, 3).reshape(P, NB * NC, S),
        "ctx_rows": a["ctx_1024"].reshape(NB * NT, P, E).transpose(1, 0, 2),
        "masks": np.concatenate([m.reshape(NT, P, S).transpose(1, 0, 2) for m in (a["mask_SxS_fc0"], a["mask_SxS_fc0"].T)], axis=1),
        "shapes": np.concatenate([np.eye(P, dtype=np.float32), later, later.T], axis=1),
        "cols": cols,
        "rows": rows,
        **{f"w{s}": w for s, w in enumerate(weights)},
    }
    arrays = {k: np.ascontiguousarray(v) for k, v in arrays.items()}
    nc = bacc.Bacc("TRN2", target_bir_lowering=False, num_devices=1)
    aps = {k: nc.dram_tensor("in_" + k, v.shape, F32, kind="ExternalInput").ap() for k, v in arrays.items()}
    out = nc.dram_tensor("out_x", (P, NB * NT, E), F32, kind="ExternalOutput").ap()
    program(nc, aps["x_t"], aps["ctx_t"], aps["ctx_rows"], aps["masks"], aps["shapes"], aps["cols"], aps["rows"],
            [aps[f"w{s}"] for s in range(8)], out)
    r = run_bass_kernel_spmd(nc, [{"in_" + k: v for k, v in arrays.items()}], core_ids=[0])
    return r.results[0]["out_x"].transpose(1, 0, 2).reshape(NB, S, E)
```

```python
from contextlib import ExitStack

import numpy as np

import concourse.bass as bass
from concourse import mybir

F32 = mybir.dt.float32
F32R = mybir.dt.float32r
BF16 = mybir.dt.bfloat16
ALU = mybir.AluOpType
ACT = mybir.ActivationFunctionType
AX = mybir.AxisListType

P = 128
NB = 8
S = 512
E = 256
NT = S // P
NC = E // P
H = 16
HD = E // H
HS = 64
F = 4 * E
NF = F // P
EPS = 1e-5
NEG = -1e30

SELF0, CROSS0, MLP0, CROSS1, SELF2, CROSS2, MLP2, SELF3 = range(8)
ATTN = {SELF0: (False, True, False), CROSS0: (True, False, False), CROSS1: (True, False, False),
        SELF2: (False, False, True), CROSS2: (True, False, False)}
ATTN_NO = {s: n for n, s in enumerate(ATTN)}
CROSS_NO = {CROSS0: 0, CROSS1: 1, CROSS2: 2}
MLP_NO = {MLP0: 0, MLP2: 1}

UNITS = 2 * NB
G = 4
ROWS = 3 * HD + 2
R3 = H // 4
UNITS3 = R3 * NB

C_G, C_B = 0, 16
C_Q, C_K = 32, 42
C_Q3, C_K3 = 52, 60
C_V, C_F = 68, 76
N_COLS = 92
R_V, R_O = 0, 5
N_ROWS = 13
C_ID, C_MQ, C_MK = 0, P, 2 * P

BASE = 1
WCOLS = 4096


def program(nc, x_in, ctx_in, ctx_rows_in, masks_in, shapes_in, cols_in, rows_in, wts, out):
    es = ExitStack()
    with es:
        def sb(name, shape, dt=F32):
            return es.enter_context(nc.sbuf_tensor(name, shape, dt))

        def pb(name):
            return es.enter_context(nc.psum_tensor(name, [P, 512], F32))

        def sem(name):
            return es.enter_context(nc.semaphore(name))

        X = sb("X", [P, NB * NT, E])
        W = [sb("W_even", [P, WCOLS]), sb("W_odd", [P, WCOLS])]
        stk = sb("stk", [P, 32, S], F32R)
        misc = sb("misc", [P, 8, 512])
        V = sb("V", [P, 2, NT * H * 32])
        Pr = sb("Pr", [P, 2, G, S])
        sums = sb("sums", [P, 2, S])
        XH = sb("XH", [P, NT, E])
        hT = sb("hT", [P, NC, S])
        hi = sb("hi", [P, 2, S], F32R)
        lo = sb("lo", [P, 2, S], F32R)
        mrows = sb("mrows", [P, S])
        cols = sb("cols", [P, N_COLS])
        brow = sb("brow", [P, 2, 2, E])
        ident = sb("ident", [P, P])
        identr = sb("identr", [P, P], F32R)
        shpb = sb("shpb", [P, 3 * P], BF16)
        st6 = sb("st6", [P, NT, 6])
        mv = sb("mv", [P, NT, 2])
        rstd = sb("rstd", [P, 2, NT])
        mhalf = sb("mhalf", [P, NT])
        mx = sb("mx", [P, 2, 2, NT, G])
        mhl = sb("mhl", [P, 2, 2, NT, 2 * G], F32R)
        qabs = sb("qabs", [P, 4])
        qst = sb("qst", [P, 16])
        ctxT = misc[:, 0:4, :].rearrange("p (a c) n -> p a c n", a=2)
        ovs = misc[:, 4:6, :]
        raw = misc[:, 6:8, :]
        AT3 = misc
        Vh = V[:, :, :].rearrange("p a (t h c) -> p a t h c", t=NT, h=H)
        Vf = V[:, :, :].rearrange("p a n -> p (a n)")
        v3_n = 2 * NT * G * HS
        V3 = Vf[:, 0:v3_n].rearrange("p (a t h c) -> p a t h c", a=2, t=NT, h=G)
        cT = Vf[:, v3_n:v3_n + NC * S].rearrange("p (c n) -> p c n", c=NC)
        ones3 = Vf[:, v3_n + NC * S:v3_n + NC * S + HS]
        h1T = V[:, :, :].rearrange("p a (b n) -> p (a b) n", n=S)
        ones = XH[:, 0, 0:P]
        shp = XH[:, 0:2, :].rearrange("p a n -> p (a n)")[:, 0:3 * P]
        identb = shpb[:, C_ID:C_ID + P]
        mask_q = W[0][:, 2048:4096].rearrange("p (t n) -> p t n", t=NT)
        mask_k = W[1][:, 2048:4096].rearrange("p (t n) -> p t n", t=NT)
        mask_hi, mask_lo = stk[:, 16:20, :], stk[:, 20:24, :]
        columns3 = Pr[:, 0, 0:2, :].rearrange("p a (k m) -> p (a k) m", m=P)

        MX = [pb("MX0"), pb("MX1")]
        ST = [pb("ST0"), pb("ST1")]
        OV = [pb("OV0"), pb("OV1")]
        LA = pb("LA")
        LB = pb("LB")
        LBt = LB[:, :].rearrange("p (t n) -> p t n", t=2)
        LAt = LA[:, :].rearrange("p (t n) -> p t n", t=2)
        FR = [MX[0], MX[1], ST[0], ST[1]]

        x_loaded, consts_in = sem("x_loaded"), sem("consts_in")
        w_in = [sem(f"w_in{s}") for s in range(8)]
        w3_late = sem("w3_late")
        masks_loaded = sem("masks_loaded")
        ctx_rows_loaded = sem("ctx_rows_loaded")
        ctx_in_sem = [sem("ctx_even"), sem("ctx_odd")]
        brow_in = [sem("brow_even"), sem("brow_odd")]
        shapes_done, pool_ready = sem("shapes_done"), sem("pool_ready")
        quant = sem("quant")
        quant_pe = sem("quant_pe")
        ln_stats, ln_mv, ln_pool, xh_ready = sem("ln_stats"), sem("ln_mv"), sem("ln_pool"), sem("xh_ready")
        la_full, la_free = sem("la_full"), sem("la_free")
        hi_done, wq_scaled = sem("hi_done"), sem("wq_scaled")
        stack_in = [[sem(f"stack_in{g}_{kind}") for kind in "kq"] for g in range(2)]
        mx_full, mx_red = sem("mx_full"), sem("mx_red")
        max_hi, max_split = sem("max_hi"), sem("max_split")
        mt_full, mt_evac = sem("mt_full"), sem("mt_evac")
        mrow_in = [sem("mrow_in0"), sem("mrow_in1")]
        st_full, st_masked, ex_done = sem("st_full"), sem("st_masked"), sem("ex_done")
        mask_split = sem("mask_split")
        pv_done, ov_evac = sem("pv_done"), sem("ov_evac")
        ov_moved = [sem("ov_moved0"), sem("ov_moved1")]
        recip_done, at_ready = sem("recip_done"), sem("at_ready")
        op_full, op_evac, x_done = sem("op_full"), sem("op_evac"), sem("x_done")
        v_ones = sem("v_ones")
        fc_full, gelu_done, pr_full, pr_evac, ml_full, ml_evac = (
            sem("fc_full"), sem("gelu_done"), sem("pr_full"), sem("pr_evac"), sem("ml_full"), sem("ml_evac"))
        la3_full, la3_free = sem("la3_full"), sem("la3_free")
        hi3_done = sem("hi3_done")
        stack3_in = [[sem(f"stack3_in{bl}_{kind}") for kind in "kq"] for bl in range(2)]
        mx3_full, mx3_red = sem("mx3_full"), sem("mx3_red")
        max3_hi, max3_split = sem("max3_hi"), sem("max3_split")
        mt3_full, mt3_evac, mrow3_in = sem("mt3_full"), sem("mt3_evac"), sem("mrow3_in")
        st3_full, ex3_done, pv3_done = sem("st3_full"), sem("ex3_done"), sem("pv3_done")
        ov3_evac, rc3_done, at3_ready = sem("ov3_evac"), sem("rc3_done"), sem("at3_ready")
        bias3 = sem("bias3")
        op3_full, op3_evac = sem("op3_full"), sem("op3_evac")
        stack3_ones = sem("stack3_ones")
        stored = sem("stored")
        pool_init, ones_set = sem("pool_init"), sem("ones_set")

        def wait(eng, s, v):
            if not isinstance(v, int) or v > 0:
                eng.wait_ge(s, v)

        QUANT_STEPS = 18
        JOINED = (CROSS0, SELF2, CROSS2)
        SCALED = {s: n + 1 for n, s in enumerate([*ATTN, SELF3])}

        def waits(eng, *pairs, apart=False):
            pairs = [(s, v if isinstance(v, int) else eng.to_reg(v)) for s, v in pairs]
            if apart and any(not isinstance(v, int) for _, v in pairs):
                eng.wait_ge(pool_ready, 1)
            for s, v in pairs:
                wait(eng, s, v)

        MASKED_BY_PE = (1, 2, 3)

        def brow_count(s):
            return 16 * sum(2 if x in ATTN_NO else 1 for x in range(s % 2, s + 1, 2))

        def addmask_of(s):
            return ATTN[s][2]

        def xt(b, t, n=1):
            return X[:, bass.ds(NT * b + t, n), :]

        def wq(s, m):
            return W[s % 2][:, 512 * m:512 * m + 512].rearrange("p (c o) -> p c o", c=NC)

        def stages(u):
            return dict(a=u < UNITS - 2, m=-1 <= u < UNITS - 1, b=0 <= u < UNITS, tail=u >= 1, op=u >= 2)

        def run_slots(eng, s, slot):
            for u in range(0 if s in JOINED else -2, 2):
                on = stages(u)
                if s in JOINED and u == 0:
                    on.update(tail=True, op=True)
                slot(u, u % 4, u // 2, (u // 2 + 1) // 2, on)
            with eng.Fori(0, 3) as k:
                for n in range(4):
                    slot(4 * k + (2 + n), (2 + n) % 4, 2 * k + (1 + n // 2), k + 1, stages(2 + n))
            for u in range(UNITS - 2, UNITS if s + 1 in JOINED else UNITS + 1):
                on = stages(u)
                if s + 1 in JOINED:
                    on.update(a=True, m=True)
                slot(u, u % 4, u // 2, (u // 2 + 1) // 2, on)

        def a_of(s, u, b):
            return (s + 1, b + 1 - NB) if isinstance(u, int) and u >= UNITS - 2 else (s, b + 1)

        def m_of(s, u):
            return s + 1 if isinstance(u, int) and u == UNITS - 1 else s

        def end_of(s, u, b):
            return (s - 1, NB - 1) if isinstance(u, int) and u == 0 else (s, b - 1)

        J_T, J_K, J_Q, J_V, JOBS = 0, (2, 6), (3, 7), 4, 8

        def stages3(v):
            return dict(a=v < UNITS3 - 2, v=-1 <= v < UNITS3 - 1, m=-1 <= v < UNITS3 - 1, b=0 <= v < UNITS3,
                        tail=v >= 1, op=v >= 1, ln=v < UNITS3 - R3)

        def run_slots3(eng, slot):
            for v in range(-2, 1):
                slot(v, v % R3, v // R3, stages3(v))
            with eng.Fori(0, NB - 1) as k:
                for n in range(R3):
                    slot(R3 * k + (1 + n), (1 + n) % R3, k + (1 + n) // R3, stages3(1 + n))
            for v in range(UNITS3 - R3 + 1, UNITS3 + 1):
                slot(v, v % R3, v // R3, stages3(v))

        EVACS = 3
        M_HEADS = ((0, 1), (2,), (3,), ())

        def jobs3(v, r, b):
            return 0 if isinstance(v, int) and v == -2 else 28 * b + (0, 6, 12, 22)[r] + 14

        def job3(v, r, b, name, n=0):
            first = 0 if isinstance(v, int) and v == -2 else 2
            tc, tx = (2, 2) if r == 2 else (0, 0)
            at = {("v", 0): 0, ("v", 1): 1, ("v", 2): 2, ("tc", 0): first, ("tc", 1): first + 1, ("kq", 0): first + tc,
                  ("tx", 0): first + tc + 1, ("tx", 1): first + tc + 2}
            at.update({("kq", k): first + tc + tx + k for k in (1, 2, 3)})
            return jobs3(v, r, b) + at[name, n]

        def norm3(b, which):
            return NB * SELF3 + 2 * b + which

        block = es.enter_context(nc.Block())

        @block.sync
        def _(sp):
            def load_weights(s):
                n = WCOLS if s in MLP_NO else WCOLS // 2
                sp.dma_start(W[s % 2][:, 0:n], wts[s]).then_inc(w_in[s], 16)
                if s in ATTN_NO:
                    r = R_V + ATTN_NO[s]
                    sp.dma_start(brow[:, s % 2, 0, :], rows_in[r:r + 1, :].broadcast_to([P, E])).then_inc(brow_in[s % 2], 16)
                load_output_bias(s)

            def load_output_bias(s):
                r = R_O + s
                sp.dma_start(brow[:, s % 2, 1, :], rows_in[r:r + 1, :].broadcast_to([P, E])).then_inc(brow_in[s % 2], 16)

            sp.dma_start(X[:, 0:NT, :], x_in[:, 0:NT, :]).then_inc(x_loaded, 16)
            sp.dma_start(cols[:, :], cols_in).then_inc(consts_in, 16)
            sp.dma_start(shp, shapes_in).then_inc(consts_in, 16)
            sp.dma_start(ident[:, :], shapes_in[:, C_ID:C_ID + P]).then_inc(consts_in, 16)
            load_weights(0)
            sp.dma_start(X[:, NT:NB * NT, :], x_in[:, NT:NB * NT, :]).then_inc(x_loaded, 16)

            def load_ctx(b, par):
                sp.dma_start(ctxT[:, par, :, :], ctx_in[:, bass.ds(NC * b, NC), :]).then_inc(ctx_in_sem[par], 16)

            def attention(s):
                cross, causal, addmask = ATTN[s]
                n = ATTN_NO[s]

                def slot(u, c, b, p, on):
                    half, U, GB = c % 2, UNITS * n + u, NB * n + b
                    if isinstance(u, int) and u == 1:
                        load_next(s)
                    loads_ctx = not isinstance(u, int) or 2 <= u < UNITS - 2
                    if cross and half == 0 and loads_ctx:
                        sp.wait_ge(la_full, JOBS * (GB - 1) + J_K[1] + 1)
                        load_ctx(b + 1, 1 - c // 2)
                    if on["stack1"]:
                        stack(U + 1, 1 - half, 1, GB + half)
                    if on["tail"]:
                        move(U - 1, 1 - half, 1, GB - 1 + half)
                    if on["b"]:
                        max_rows(U, half, 1)
                    if on["m"]:
                        max_rows(U + 1, 1 - half, 0)
                    if on["a"]:
                        stack(U + 2, half, 0, GB + 1)
                    if on["b"]:
                        move(U, half, 0, GB)

                def stack(U, half, g, GBj):
                    free = (st_full, 32 * (U - 2) + 16 * (g + 1))
                    for kind, parts in ((0, (hi, lo, hi)), (1, (hi, hi, lo))):
                        parts_in = (la_free, JOBS * GBj + (J_K, J_Q)[kind][half] + 1)
                        waits(sp, *([free, parts_in] if kind == 0 else [parts_in]))
                        at = (8 if kind == 0 else 0) + G * g
                        for r, part in enumerate(parts):
                            lo_p = 64 * half + HD * r
                            sp.dma_start(stk[lo_p:lo_p + HD, at:at + G, :].bitcast(F32),
                                         part[64 * g:64 * g + 64, kind, :].bitcast(F32)).then_inc(stack_in[g][kind], 16)

                def max_rows(U, half, g):
                    sp.wait_ge(mt_evac, 2 * U + g + 1)
                    lo_p = 64 * half + 3 * HD
                    sp.dma_start(stk[lo_p:lo_p + 2, G * g:G * g + G, :].bitcast(F32),
                                 mrows[32 * g:32 * g + 2 * G, :]).then_inc(mrow_in[g], 16)

                def move(U, half, g, GBu):
                    waits(sp, (ov_evac, 2 * U + g + 1),
                          (at_ready, BASE + U - 1),
                          (op_full, BASE + 2 * GBu))
                    sp.dma_start(raw[64 * g:64 * g + 64, half, :], ovs[0:P:2, g, :]).then_inc(ov_moved[g], 16)
                    sp.dma_start(sums[64 * g:64 * g + 64, half, :], ovs[1:P:2, g, :]).then_inc(ov_moved[g], 16)

                if cross and s not in JOINED:
                    load_ctx(0, 0)
                    load_ctx(1, 1)

                def with_stack1(u, c, b, p, on):
                    slot(u, c, b, p, dict(on, stack1=on["m"]))

                run_slots(sp, s, with_stack1)

            def layer3(s):
                for part in (2, 3):
                    sp.dma_start(W[0][:, 2048 * (part - 2):2048 * (part - 1)],
                                 wts[s][:, 2048 * part:2048 * part + 2048]).then_inc(w3_late, 16)

                def load_ctx_rows(b):
                    sp.dma_start(XH[:, :, :], ctx_rows_in[:, bass.ds(NT * b, NT), :]).then_inc(ctx_rows_loaded, 16)

                def slot(v, r, b, on):
                    par = r % 2
                    if r == 1 and on["ln"]:
                        load_ctx_rows(b + 1)
                    if on["a"]:
                        stack(v, r, b, 0)
                    if on["m"]:
                        sp.wait_ge(mt3_evac, v + 2)
                        at = 16 * (1 - par) + 4
                        sp.dma_start(stk[HS:HS + 2, at:at + G, :].bitcast(F32),
                                     mrows[32 * (1 - par):32 * (1 - par) + 2 * G, :]).then_inc(mrow3_in, 16)
                    if on["a"]:
                        stack(v, r, b, 1)
                    if on["op"] and r == 0:
                        store(b - 1)

                def stack(v, r, b, bl):
                    free = (st3_full, 16 * v + 8 * (bl + 1))
                    for kind, parts in ((0, (hi, hi, lo)), (1, (hi, lo, hi))):
                        parts_in = (la3_free, job3(v, r, b, "kq", 2 * bl + kind) + 1)
                        waits(sp, *([free, parts_in] if kind == 0 else [parts_in]))
                        for part, lo_p, form in zip(parts, (0, 64, 0), (0, 0, 1)):
                            at = 16 * (r % 2) + 8 * (1 - kind) + 4 * form + 2 * bl
                            sp.dma_start(stk[lo_p:lo_p + HS, at:at + 2, :].bitcast(F32),
                                         part[:, kind, :].bitcast(F32)).then_inc(stack3_in[bl][kind], 16)

                def store(b):
                    sp.wait_ge(x_done, NB * s + b + 1)
                    sp.dma_start(out[:, bass.ds(NT * b, NT), :], xt(b, 0, NT)).then_inc(stored, 16)

                load_ctx_rows(0)
                sp.wait_ge(stack3_ones, 3)
                run_slots3(sp, slot)
                sp.wait_ge(stored, 16 * NB)

            def load_next(s):
                wait(sp, x_done, NB * s)
                if s + 1 < SELF3:
                    load_weights(s + 1)
                elif s + 1 == SELF3:
                    sp.dma_start(W[1][:, :], wts[SELF3][:, 0:WCOLS]).then_inc(w_in[SELF3], 16)
                    load_output_bias(SELF3)
                if s == CROSS1:
                    sp.dma_start(mask_q, masks_in[:, 0:NT, :]).then_inc(masks_loaded, 16)
                    sp.dma_start(mask_k, masks_in[:, NT:2 * NT, :]).then_inc(masks_loaded, 16)
                if s + 1 in JOINED and s + 1 in CROSS_NO:
                    load_ctx(0, 0)
                    load_ctx(1, 1)

            sp.wait_ge(pool_ready, 1)
            for s in range(8):
                if s not in JOINED:
                    wait(sp, x_done, NB * s)
                if s not in ATTN:
                    load_next(s)
                if s in ATTN:
                    attention(s)
                elif s == SELF3:
                    layer3(s)

        @block.tensor
        def _(pe):
            def mm(o, l, r, start=True, stop=True):
                return nc.tensor.matmul(o, l, r, start=start, stop=stop)

            def transpose_x(s, b, c, bank):
                if c == 0:
                    pe.wait_ge(xh_ready, NB * s + b + 1)
                return turn_tiles(c, bank)

            def turn_tiles(c, bank):
                for t in range(NT):
                    last = nc.tensor.transpose(bank[:, P * t:P * t + P], XH[:, t, P * c:P * c + P], ident[:, :])
                return last

            def attention(s):
                n = ATTN_NO[s]

                def slot(u, c, b, p, on):
                    half, par = c % 2, c // 2
                    U, GB = UNITS * n + u, NB * n + b
                    GB1 = NB * n + b + 1
                    sa, ba = a_of(s, u, b)
                    if on["a"]:
                        cross_a = ATTN[sa][0]
                        source = ctxT[:, 1 - par] if cross_a else hT
                    se, _ = end_of(s, u, b)
                    if isinstance(u, int) and u == UNITS - 2 and on["a"]:
                        weights_ready(s + 1)
                    turned = 2 * U + (2 if on["b"] else 0) + (1 if on["m"] else 0)
                    for i in range(8):
                        g = i // 4
                        if on["m"] and i % 4 == 0:
                            for kind in range(2):
                                pe.wait_ge(stack_in[g][kind], 48 * (U + 2))
                        if on["b"] and i % 4 == 0:
                            pe.wait_ge(mrow_in[g], 16 * (U + 1))
                        for j in range(4):
                            if on["m"]:
                                max_tile(ATTN[m_of(s, u)][1], U + 1, 1 - half, i, j)
                            if on["b"]:
                                score_tile(U, half, i, j)
                            at = (i, j)
                            if j == 1 and on["b"] and i > 0:
                                values(ATTN[s][1], U, half, par, i - 1)
                            if at == (0, 1) and on["tail"]:
                                causal_e = ATTN[s - 1 if isinstance(u, int) and u == 0 else s][1]
                                values(causal_e, U - 1, 1 - half, par if half else 1 - par, 7)
                            if at == (2, 0) and on["b"]:
                                turn_max(U, half, 1, 2 * (GB - 1 + half))
                            if at == (4, 2) and on["m"]:
                                turn_max(U + 1, 1 - half, 0, 2 * (GB - 1 + half))
                            if half == 0 and on["op"] and at in ((5, 2), (6, 0)):
                                project_out(se, GB - 1, 0, i - 5, turned)
                            if half == 0 and on["op"] and at in ((6, 2), (7, 0)):
                                project_out(se, GB - 1, 1, i - 6, turned)
                            if on["a"]:
                                if half == 0 and at in ((2, 3), (3, 1)):
                                    job(GB1, J_T + i - 2)
                                    transpose_x(sa, ba, i - 2, LA).then_inc(la_full, 1)
                                if at in ((4, 0), (4, 1)):
                                    if cross_a and j == 0:
                                        pa = p if sa == s else 0
                                        pe.wait_ge(ctx_in_sem[1 - par], 16 * (4 * CROSS_NO[sa] + pa + 1))
                                    project(GB1, J_K[half], wq(sa, 1), half, source, j)
                                if at in ((5, 0), (5, 1)):
                                    project(GB1, J_Q[half], wq(sa, 0), half, hT, j)
                                if half == 0 and at in ((6, 3), (7, 2)):
                                    project_values(GB1, wq(sa, 2), source, 0, i - 6)
                                if half == 1 and at in ((0, 2), (0, 3)):
                                    project_values(GB1, wq(sa, 2), source, 1, j - 2)

                def job(GBj, k):
                    wait(pe, la_free, JOBS * GBj + k)

                def project(GBj, k, w, half, source, c):
                    if c == 0:
                        job(GBj, k)
                    last = mm(LA[:, :], w[:, c, P * half:P * half + P], source[:, c, :], c == 0, c == NC - 1)
                    if c == NC - 1:
                        last.then_inc(la_full, 1)

                def project_values(GBj, w, source, j, t):
                    if t == 0:
                        job(GBj, J_V + j)
                    tok = slice(P * (2 * j + t), P * (2 * j + t) + P)
                    for c in range(NC):
                        last = mm(LAt[:, t, :], source[:, c, tok], w[:, c, :], c == 0, c == NC - 1)
                    if t == 1:
                        last.then_inc(la_full, 1)

                def max_tile(causal, U, half, i, qt):
                    at = 32 * U + 4 * i + qt
                    wait(pe, mx_red, at - 1)
                    lo_p, k_n = 64 * half, P * (qt + 1) if causal else S
                    q = stk[lo_p:lo_p + 3 * HD, i, P * qt:P * qt + P]
                    last = mm(MX[qt % 2][:, 0:k_n], q, stk[lo_p:lo_p + 3 * HD, 8 + i, 0:k_n], True, not causal)
                    if causal:
                        last = mm(MX[qt % 2][:, k_n - P:k_n], identb, shpb[:, C_MQ:C_MQ + P], False, True)
                    last.then_inc(mx_full, 1)

                def score_tile(U, half, i, h):
                    _, causal, addmask = ATTN[s]
                    at, head, kt = 32 * U + 4 * i + h, G * (i // 4) + h, i % 4
                    wait(pe, ex_done, at - 1)
                    lo_p, q0 = 64 * half, P * kt if causal else 0
                    k = stk[lo_p:lo_p + ROWS, 8 + head, P * kt:P * kt + P]
                    last = mm(ST[h % 2][:, q0:S], k, stk[lo_p:lo_p + ROWS, head, q0:S], True,
                              not (causal or (addmask and h in MASKED_BY_PE)))
                    if addmask and h in MASKED_BY_PE:
                        mm(ST[h % 2][:, :], identr[:, :], mask_hi[:, kt, :], False, False)
                        last = mm(ST[h % 2][:, :], identr[:, :], mask_lo[:, kt, :], False, True)
                    if causal:
                        last = mm(ST[h % 2][:, q0:q0 + P], identb, shpb[:, C_MK:C_MK + P], False, True)
                    last.then_inc(st_full, 1)

                def values(causal, U, half, vpar, i):
                    g, kt = i // 4, i % 4
                    if kt == 0:
                        wait(pe, ov_evac, 2 * U + g - 1)
                    pe.wait_ge(ex_done, 4 * (8 * U + i + 1))
                    q0 = P * kt if causal else 0
                    for h in range(G):
                        last = mm(OV[g][32 * h:32 * h + 32, q0:S], Vh[:, vpar, kt, 8 * half + G * g + h, :], Pr[:, i % 2, h, q0:S],
                                  kt == 0, kt == NT - 1)
                    last.then_inc(pv_done, 1)

                def turn_max(U, half, g, ops):
                    pe.wait_ge(max_split, 2 * U + g + 1)
                    wait(pe, mt_evac, 2 * U + g)
                    wait(pe, op_evac, BASE + ops)
                    for t in range(NT):
                        last = nc.tensor.transpose(LB[0:2 * G, P * t:P * t + P], mhl[:, half, g, t, :].bitcast(F32), ident[:, :])
                    last.then_inc(mt_full, 1)

                def project_out(so, GBo, j, t, turned):
                    if t == 0:
                        pe.wait_ge(at_ready, BASE + 2 * (GBo + 1))
                        wait(pe, mt_evac, turned)
                        wait(pe, op_evac, BASE + 2 * GBo + j)
                    tok = slice(P * (2 * j + t), P * (2 * j + t) + P)
                    for k in range(2):
                        last = mm(LBt[:, t, :], raw[:, k, tok], wq(so, 3)[:, k, :], k == 0, k == 1)
                    if t == 1:
                        last.then_inc(op_full, 1)

                run_slots(pe, s, slot)

            def mlp(s):
                m = MLP_NO[s]
                wf = W[s % 2][:, 0:2048].rearrange("p (c o) -> p c o", c=NC)
                wp = W[s % 2][:, 2048:4096].rearrange("p (f o) -> p f o", f=NF)

                def turn(b):
                    MB = NB * m + b
                    for c, bank in enumerate((LA, LB)):
                        wait(pe, ml_evac, 2 * (MB - 1) + c + 1)
                        transpose_x(s, b, c, bank).then_inc(ml_full, 1)

                def batch(b, more):
                    MB = NB * m + b
                    pe.wait_ge(ml_evac, 2 * (MB + 1))
                    for f in range(NF):
                        wait(pe, gelu_done, NF * MB + f - 3)
                        for c in range(NC):
                            last = mm(FR[f % 4][:, :], wf[:, c, P * f:P * f + P], hT[:, c, :], c == 0, c == NC - 1)
                        last.then_inc(fc_full, 1)
                    if more:
                        turn(b + 1)
                    pe.wait_ge(gelu_done, NF * (MB + 1))
                    for j in range(2):
                        wait(pe, pr_evac, 2 * (MB - 1) + j + 1)
                        for t in range(2):
                            tok = slice(P * (2 * j + t), P * (2 * j + t) + P)
                            for f in range(NF):
                                last = mm(OV[j][:, E * t:E * t + E], h1T[:, f, tok], wp[:, f, :], f == 0, f == NF - 1)
                        last.then_inc(pr_full, 1)

                turn(0)
                batch(0, True)
                with pe.Fori(1, NB - 1) as b:
                    batch(b, True)
                batch(NB - 1, False)

            def layer3(s):
                w_q = W[1][:, 0:2048].rearrange("p (c o) -> p c o", c=NC)
                w_k = W[1][:, 2048:4096].rearrange("p (c o) -> p c o", c=NC)
                w_v = W[0][:, 0:2048].rearrange("p (c o) -> p c o", c=NC)
                w_o = W[0][:, 2048:4096].rearrange("p (k o) -> p k o", k=8)
                pe.wait_ge(wq_scaled, SCALED[s])
                pe.wait_ge(w3_late, 32)
                pe.wait_ge(stack3_ones, 3)
                pe.wait_ge(bias3, 1)
                for k in range(8):
                    last = mm(LB[:, 0:E], columns3[:, k, :], w_o[:, k, :], k == 0, k == 7)
                last.then_inc(bias3, 1)
                pe.wait_ge(bias3, 3)

                def slot(v, r, b, on):
                    par = r % 2
                    for i in range(4):
                        if i == 0:
                            if on["m"]:
                                for kind in range(2):
                                    pe.wait_ge(stack3_in[0][kind], 48 * (v + 2))
                            if on["b"]:
                                pe.wait_ge(mrow3_in, 16 * (v + 1))
                        if i == 1 and on["m"]:
                            for kind in range(2):
                                pe.wait_ge(stack3_in[1][kind], 48 * (v + 2))
                        tiles = [(h, qt) for h in M_HEADS[i] for qt in range(NT)] if on["m"] else []
                        for kt in range(NT):
                            for h, qt in tiles[len(tiles) * kt // 4:len(tiles) * (kt + 1) // 4]:
                                max_tile(v + 1, 1 - par, h, qt)
                            if on["b"]:
                                score_tile(v, par, i, kt)
                            at = (i, kt)
                            for key_tile in ((), (0,), (1,), (2, 3))[kt]:
                                if on["b"] and i > 0:
                                    values(v, par, i - 1, key_tile)
                            for key_tile in ((0, 1), (2, 3), (), ())[kt]:
                                if on["tail"] and i == 0:
                                    values(v - 1, 1 - par, 3, key_tile)
                            if on["v"] and at in ((0, 2), (1, 0)):
                                project_values(v, r, b, i)
                            if on["a"]:
                                if r == 2 and at in ((1, 1), (1, 2)):
                                    turn_batch(v, r, b, "tc", kt - 1)
                                if r == 2 and at in ((2, 1), (2, 2)):
                                    turn_batch(v, r, b, "tx", kt - 1)
                                if at in ((1, 3), (2, 3)):
                                    project(v, r, b, 0, i - 1)
                                if at in ((3, 1), (3, 3)):
                                    project(v, r, b, 1, kt // 2)
                            if r == 0 and on["op"]:
                                if at in ((2, 0), (2, 1)):
                                    project_out(b - 1, 0, kt, v)
                                if at in ((2, 3), (3, 0)):
                                    project_out(b - 1, 1, i - 2, v)
                            if on["m"] and at == (3, 2 if r == 0 else 0):
                                turn_max(v, r, b)

                def turn_max(v, r, b):
                    pe.wait_ge(max3_split, v + 2)
                    wait(pe, mt3_evac, v + 1)
                    wait(pe, op3_evac, BASE + 2 * b)
                    for t in range(NT):
                        last = nc.tensor.transpose(LB[0:2 * G, P * t:P * t + P],
                                                   mhl[:, (r + 1) % 2, 0, t, :].bitcast(F32), ident[:, :])
                    last.then_inc(mt3_full, 1)

                def project_values(v, r, b, j):
                    la(job3(v, r, b, "v", j))
                    rv = (r + 1) % R3
                    for t in range(2):
                        tok = slice(P * (2 * j + t), P * (2 * j + t) + P)
                        for c in range(NC):
                            last = mm(LAt[:, t, :], cT[:, c, tok], w_v[:, c, E * rv:E * rv + E], c == 0, c == NC - 1)
                    last.then_inc(la3_full, 1)

                def project(v, r, b, block, kind):
                    la(job3(v, r, b, "kq", 2 * block + kind))
                    bl = 2 * ((r + 2) % R3) + block
                    w, source = ((w_k, cT), (w_q, hT))[kind]
                    for c in range(NC):
                        last = mm(LA[:, :], w[:, c, P * bl:P * bl + P], source[:, c, :], c == 0, c == NC - 1)
                    last.then_inc(la3_full, 1)

                def turn_batch(v, r, b, name, c):
                    if c == 0:
                        pe.wait_ge(xh_ready, norm3(b + 1, 0 if name == "tc" else 1) + 1)
                    la(job3(v, r, b, name, c))
                    turn_tiles(c, LA).then_inc(la3_full, 1)

                def la(k):
                    wait(pe, la3_free, k)

                def max_tile(v, par, h, qt):
                    at, k_n = 16 * v + 4 * h + qt, P * (qt + 1)
                    wait(pe, mx3_red, at - 1)
                    bank, q = MX[qt % 2], 16 * par
                    tok = slice(P * qt, P * qt + P)
                    mm(bank[:, 0:k_n], stk[:, q + h, tok], stk[:, q + 8 + h, 0:k_n], True, False)
                    mm(bank[:, 0:k_n], stk[0:HS, q + 4 + h, tok], stk[0:HS, q + 12 + h, 0:k_n], False, False)
                    mm(bank[:, k_n - P:k_n], identb, shpb[:, C_MQ:C_MQ + P], False, True).then_inc(mx3_full, 1)

                def score_tile(v, par, h, kt):
                    at, q0 = 16 * v + 4 * h + kt, P * kt
                    wait(pe, ex3_done, at - 1)
                    bank, q = ST[kt % 2], 16 * par
                    tok = slice(P * kt, P * kt + P)
                    mm(bank[:, q0:S], stk[:, q + 8 + h, tok], stk[:, q + h, q0:S], True, False)
                    mm(bank[:, q0:S], stk[0:HS + 2, q + 12 + h, tok], stk[0:HS + 2, q + 4 + h, q0:S], False, False)
                    mm(bank[:, q0:q0 + P], identb, shpb[:, C_MK:C_MK + P], False, True).then_inc(st3_full, 1)

                def values(v, par, i, kt):
                    if i % 2 == 0 and kt == 0:
                        wait(pe, ov3_evac, EVACS * (2 * v + i // 2))
                    pe.wait_ge(ex3_done, 16 * v + 4 * i + kt + 1)
                    for bank, w, lo_p in ((OV[0], V3[:, par, kt, i, :], HS * (i % 2)), (OV[1], ones3, HS * (1 - i % 2))):
                        last = mm(bank[lo_p:lo_p + HS, P * kt:S], w, Pr[:, i % 2, kt, P * kt:S], kt == 0, kt == NT - 1)
                    if kt == NT - 1:
                        last.then_inc(pv3_done, 1)

                def project_out(b, j, t, v):
                    if t == 0:
                        pe.wait_ge(at3_ready, 8 * (b + 1))
                        turned = v + 1 if not isinstance(v, int) or v < UNITS3 else UNITS3
                        pe.wait_ge(mt3_evac, turned)
                        wait(pe, op3_evac, BASE + 2 * b + j)
                    tok = slice(P * (2 * j + t), P * (2 * j + t) + P)
                    for k in range(8):
                        last = mm(LBt[:, t, :], AT3[:, k, tok], w_o[:, k, :], k == 0, k == 7)
                    if t == 1:
                        last.then_inc(op3_full, 1)

                run_slots3(pe, slot)

            pe.wait_ge(shapes_done, 2)
            pe.wait_ge(pool_ready, 1)
            def weights_ready(s):
                pe.wait_ge(w_in[s], 16)
                pe.wait_ge(wq_scaled, SCALED[s])
                pe.wait_ge(v_ones, 2 if s >= CROSS1 else 1)

            for s in range(8):
                if s not in JOINED:
                    wait(pe, x_done, NB * s)
                    pe.wait_ge(w_in[s], 16)
                if s in ATTN:
                    if s == CROSS1:
                        pe.wait_ge(quant, 4)
                        pe.wait_ge(ones_set, 1)
                        mm(LA[:, 0:4], ones, qabs[:, :]).then_inc(quant_pe, 1)
                        pe.wait_ge(quant, QUANT_STEPS)
                    if s not in JOINED:
                        weights_ready(s)
                    if addmask_of(s):
                        pe.wait_ge(mask_split, 2)
                    attention(s)
                elif s in MLP_NO:
                    mlp(s)
                else:
                    layer3(s)

        @block.scalar
        def _(act):
            def scale_shift(s, c):
                g, o = C_G + 2 * s + c, C_B + 2 * s + c
                return dict(scale=cols[:, g:g + 1], bias=cols[:, o:o + 1])

            def attention(s):
                cross, causal, addmask = ATTN[s]
                n = ATTN_NO[s]

                def slot(u, c, b, p, on):
                    half, U, GB1 = c % 2, UNITS * n + u, NB * n + b + 1
                    sa, _ = a_of(s, u, b)
                    for i in range(8):
                        for h in range(G):
                            if on["b"]:
                                exp_tile(u, U, i, h)
                            at = (i, h)
                            if at == (1, 0) and on["tail"]:
                                product_out(U - 1, 1)
                            if at == (2, 1) and on["b"]:
                                rows_out(U, 1)
                            if at == (4, 3) and on["m"]:
                                rows_out(U + 1, 0)
                            if at == (5, 0) and on["b"]:
                                product_out(U, 0)
                            if half == 0 and at in ((3, 0), (3, 2)) and on["a"]:
                                c = h // 2
                                act.wait_ge(la_full, JOBS * GB1 + J_T + c + 1)
                                nc.scalar.activation(hT[:, c, :], LA[:, :], ACT.Identity, **scale_shift(sa, c)).then_inc(la_free, 1)
                            if at in ((4, 1), (5, 1)) and on["a"]:
                                high_part(sa, U, GB1, half, i - 4)

                def high_part(sa, U, GBj, half, kind):
                    act.wait_ge(la_full, JOBS * GBj + (J_K, J_Q)[kind][half] + 1)
                    for g in range(2):
                        wait(act, stack_in[g][kind], 48 * (U + 2))
                    at = (C_K, C_Q)[kind] + 2 * ATTN_NO[sa] + half
                    nc.scalar.activation(hi[:, kind, :], LA[:, :], ACT.Identity, bias=cols[:, at:at + 1]).then_inc(hi_done, 1)

                def product_out(U, g):
                    act.wait_ge(pv_done, 8 * U + 4 * (g + 1))
                    wait(act, ov_moved[g], 32 * U)
                    nc.scalar.activation(ovs[:, g, :], OV[g][:, :], ACT.Copy).then_inc(ov_evac, 1)

                def exp_tile(u, U, i, h):
                    at, q0 = 32 * U + 4 * i + h, P * (i % 4) if causal else 0
                    if h == 0:
                        wait(act, pv_done, 8 * U + i - 1)
                    if addmask and h not in MASKED_BY_PE:
                        act.wait_ge(st_masked, 8 * u + i + 1)
                    else:
                        act.wait_ge(st_full, at + 1)
                    nc.scalar.activation(Pr[:, i % 2, h, q0:S], ST[h % 2][:, q0:S], ACT.Exp).then_inc(ex_done, 1)

                def rows_out(U, g):
                    act.wait_ge(mt_full, 2 * U + g + 1)
                    wait(act, mrow_in[g], 16 * U)
                    nc.scalar.activation(mrows[32 * g:32 * g + 2 * G, :], LB[0:2 * G, :], ACT.Copy).then_inc(mt_evac, 1)

                run_slots(act, s, slot)

            def mlp(s):
                m = MLP_NO[s]

                def turned(b):
                    for c, bank in enumerate((LA, LB)):
                        act.wait_ge(ml_full, 2 * (NB * m + b) + c + 1)
                        nc.scalar.activation(hT[:, c, :], bank[:, :], ACT.Identity, **scale_shift(s, c)).then_inc(ml_evac, 1)

                def batch(b, more):
                    for f in range(NF):
                        at = C_F + NF * m + f
                        act.wait_ge(fc_full, NF * (NB * m + b) + f + 1)
                        nc.scalar.activation(h1T[:, f, :], FR[f % 4][:, :], ACT.Gelu,
                                             bias=cols[:, at:at + 1]).then_inc(gelu_done, 1)
                    if more:
                        turned(b + 1)

                turned(0)
                batch(0, True)
                with act.Fori(1, NB - 1) as b:
                    batch(b, True)
                batch(NB - 1, False)

            def layer3(s):
                def slot(v, r, b, on):
                    par = r % 2
                    for i in range(4):
                        for kt in range(NT):
                            if on["b"]:
                                exp_tile(v, i, kt)
                            at = (i, kt)
                            if at == (0, 2) and on["tail"]:
                                pair_out(v - 1, (r - 1) % R3, b, 1)
                            if at == (2, 3) and on["b"]:
                                pair_out(v, r, b, 0)
                            if on["a"]:
                                if r == 2 and at in ((1, 1), (1, 2)):
                                    turned(v, r, b, "tc", kt - 1, cT)
                                if r == 2 and at in ((2, 1), (2, 2)):
                                    turned(v, r, b, "tx", kt - 1, hT)
                                if at in ((2, 0), (3, 0)):
                                    high_part(v, r, b, 0, i - 2)
                                if at in ((3, 2), (3, 3)):
                                    high_part(v, r, b, 1, kt - 2)
                            if at == (3, 2 if r == 0 else 0) and on["m"]:
                                rows_out(v, par)

                def exp_tile(v, i, kt):
                    if kt == 0:
                        wait(act, pv3_done, 4 * v + i - 1)
                    act.wait_ge(st3_full, 16 * v + 4 * i + kt + 1)
                    nc.scalar.activation(Pr[:, i % 2, kt, P * kt:S], ST[kt % 2][:, P * kt:S], ACT.Exp).then_inc(ex3_done, 1)

                def turned(v, r, b, name, c, to):
                    act.wait_ge(la3_full, job3(v, r, b, name, c) + 1)
                    nc.scalar.activation(to[:, c, :], LA[:, :], ACT.Identity, **scale_shift(s, c)).then_inc(la3_free, 1)

                def high_part(v, r, b, block, kind):
                    act.wait_ge(la3_full, job3(v, r, b, "kq", 2 * block + kind) + 1)
                    wait(act, stack3_in[1 - block][kind], 48 * (v + 2 + block))
                    at = (C_K3, C_Q3)[kind] + 2 * ((r + 2) % R3) + block
                    nc.scalar.activation(hi[:, kind, :], LA[:, :], ACT.Identity, bias=cols[:, at:at + 1]).then_inc(hi3_done, 1)

                def rows_out(v, par):
                    act.wait_ge(mt3_full, v + 2)
                    wait(act, mrow3_in, 16 * (v + 1))
                    lo_p = 32 * (1 - par)
                    nc.scalar.activation(mrows[lo_p:lo_p + 2 * G, :], LB[0:2 * G, :], ACT.Copy).then_inc(mt3_evac, 1)

                def pair_out(v, r, b, j):
                    act.wait_ge(pv3_done, 4 * v + 2 * j + 2)
                    if r == 0 and j == 0:
                        wait(act, op3_full, 2 * b)
                    nc.scalar.activation(AT3[:, 2 * r + j, :], OV[0][:, :], ACT.Copy).then_inc(ov3_evac, 1)
                    wait(act, at3_ready, 2 * v + j - 1)
                    for lo_p in (0, HS):
                        nc.scalar.activation(sums[lo_p:lo_p + HS, j, :], OV[1][HS - lo_p:P - lo_p, :], ACT.Copy).then_inc(ov3_evac, 1)

                run_slots3(act, slot)

            act.wait_ge(pool_ready, 1)
            for s in range(8):
                if s not in JOINED:
                    wait(act, x_done, NB * s)
                if s in ATTN:
                    attention(s)
                elif s in MLP_NO:
                    mlp(s)
                else:
                    layer3(s)

        @block.vector
        def _(dve):
            def statistics(N, rows, t):
                if t == 0:
                    wait(dve, ln_mv, NT * N)
                nc.vector.bn_stats(st6[:, t, :], rows).then_inc(ln_stats, 1)

            def combine(N):
                waits(dve, (xh_ready, N), apart=True)
                for t in range(NT):
                    waits(dve, (ln_stats, NT * N + t + 1), apart=True)
                    nc.vector.bn_aggr(mv[:, t, :], st6[:, t, :]).then_inc(ln_mv, 1)

            def layer_norm(N, tile):
                for t in range(NT):
                    statistics(N, tile(t), t)
                combine(N)

            def layer_norm_x(N, b):
                layer_norm(N, lambda t: xt(b, t))

            def add_to_x(b, j, bank, done):
                nc.vector.tensor_tensor(xt(b, 2 * j, 2), bank, xt(b, 2 * j, 2), ALU.add).then_inc(done, 1)

            def attention(s):
                cross, causal, addmask = ATTN[s]
                n = ATTN_NO[s]

                def slot(u, c, b, p, on):
                    half, par = c % 2, c // 2
                    U, GB = UNITS * n + u, NB * n + b
                    sa, ba = a_of(s, u, b)
                    se, be = end_of(s, u, b)
                    if isinstance(u, int) and u == UNITS - 2 and on["a"]:
                        prepare(s + 1)
                    for i in range(8):
                        if on["m"] and i % 4 == 0:
                            wait(dve, max_split, 2 * (U + 1) - 3 + i // 4)
                        for j in range(4):
                            if on["m"]:
                                max_tile(m_of(s, u), U + 1, 1 - half, i, j)
                            if on["b"] and addmask and j not in MASKED_BY_PE:
                                add_mask(u, U, i, j)
                            at = (i, j)
                            if i == 0 and half == 0 and on["a"]:
                                if j == 0 and sa > 0:
                                    wait(dve, x_done, NB * (sa - 1) + ba + 1)
                                statistics(NB * sa + ba, xt(ba, j), j)
                            if at == (1, 0) and half == 0 and on["a"]:
                                combine(NB * sa + ba)
                            if at in ((3, 1), (3, 2), (4, 0), (4, 1)) and on["tail"]:
                                invert(U, 1 - half, j - 1 if i == 3 else j + 2)
                            if at in ((4, 2), (5, 2)) and on["a"]:
                                low_part(sa, U, half, i - 4)
                            if at in ((6, 1), (7, 1)) and half == 0 and on["op"]:
                                dve.wait_ge(op_full, BASE + 2 * (GB - 1) + i - 5)
                                add_to_x(be, i - 6, LBt, op_evac)
                            if at == (7, 3) and half == 0 and on["a"]:
                                values_out(sa, GB + 1, 1 - par, 0)
                            if at == (1, 1) and half == 1 and on["a"]:
                                values_out(sa, GB + 1, 1 - par, 1)

                def max_tile(sm, U, half, i, qt):
                    _, causal, addmask = ATTN[sm]
                    at = 32 * U + 4 * i + qt
                    waits(dve, (mx_full, at + 1), apart=addmask)
                    bank, m = MX[qt % 2], mx[:, half, i // 4, qt, i % 4:i % 4 + 1]
                    if addmask:
                        nc.vector.tensor_tensor_reduce(bank[:, :], bank[:, :], mask_q[:, qt, :], 1.0, -3.0e38,
                                                       ALU.add, ALU.max, m).then_inc(mx_red, 1)
                    else:
                        k_n = P * (qt + 1) if causal else S
                        nc.vector.tensor_reduce(m, bank[:, 0:k_n], AX.X, ALU.max).then_inc(mx_red, 1)

                def add_mask(u, U, i, h):
                    at = 32 * U + 4 * i + h
                    dve.wait_ge(st_full, at + 1)
                    nc.vector.tensor_tensor(ST[h % 2][:, :], ST[h % 2][:, :], mask_k[:, i % 4, :],
                                            ALU.add).then_inc(st_masked, 1)

                def invert(U, half, j):
                    if j == 0:
                        dve.wait_ge(ov_moved[0], 32 * U)
                        dve.wait_ge(ov_moved[1], 32 * U)
                    part = sums[:, half, P * j:P * j + P]
                    nc.vector.reciprocal(part, part).then_inc(recip_done, 1)

                def low_part(sa, U, half, kind):
                    dve.wait_ge(hi_done, 2 * (U + 2) + kind + 1)
                    at = (C_K, C_Q)[kind] + 2 * ATTN_NO[sa] + half
                    nc.vector.scalar_tensor_tensor(lo[:, kind, :], LA[:, :], cols[:, at:at + 1], hi[:, kind, :].bitcast(F32),
                                                   ALU.add, ALU.subtract).then_inc(la_free, 1)

                def values_out(sa, GBj, vpar, j):
                    dve.wait_ge(la_full, JOBS * GBj + J_V + j + 1)
                    to = Vh[:, vpar, 2 * j:2 * j + 2, :, :].rearrange("p t h (d two) -> p t h d two", two=2)[:, :, :, :, 0]
                    bias = brow[:, sa % 2, 0:1, :].rearrange("p t (h d) -> p t h d", h=H).broadcast_to([P, 2, H, HD])
                    nc.vector.tensor_tensor(to, LAt[:, :, :].rearrange("p t (h d) -> p t h d", h=H), bias, ALU.add).then_inc(la_free, 1)

                run_slots(dve, s, slot)

            def mlp(s):
                m = MLP_NO[s]

                def batch(b, more):
                    if more:
                        layer_norm_x(NB * s + b + 1, b + 1)
                    for j in range(2):
                        dve.wait_ge(pr_full, 2 * (NB * m + b) + j + 1)
                        add_to_x(b, j, OV[j][:, :].rearrange("p (t n) -> p t n", t=2), pr_evac)

                layer_norm_x(NB * s, 0)
                batch(0, True)
                with dve.Fori(1, NB - 1) as b:
                    batch(b, True)
                batch(NB - 1, False)

            def scale_queries(s, w, width):
                dve.wait_ge(w_in[s], 16)
                nc.vector.tensor_scalar(w, w, width ** -0.5, None, ALU.mult).then_inc(wq_scaled, 1)

            def quantize():
                w = W[CROSS1 % 2]
                up, down = Pr[:, 0, :, :], Pr[:, 1, :, :]
                gam, thr, neg = qst[:, 0:4], qst[:, 4:8], qst[:, 8:12]
                wm = w[:, 0:2048].rearrange("p (m n) -> p m n", m=4)
                dve.wait_ge(w_in[CROSS1], 16)
                nc.vector.tensor_reduce(qabs[:, :], wm, AX.X, ALU.add, apply_absolute_value=True).then_inc(quant, 4)
                dve.wait_ge(quant_pe, 1)
                nc.vector.tensor_scalar(gam, LA[:, 0:4], 1.0 / (E * E), None, ALU.mult).then_inc(quant, 1)
                dve.wait_ge(quant, 5)
                nc.vector.tensor_scalar(thr, gam, 1e-5, 0.5, ALU.add, ALU.mult).then_inc(quant, 1)
                dve.wait_ge(quant, 6)
                nc.vector.tensor_scalar(neg, thr, -1.0, None, ALU.mult).then_inc(quant, 1)
                dve.wait_ge(quant, 7)
                for k in range(4):
                    nc.vector.tensor_scalar(up[:, k, :], wm[:, k, :], thr[:, k:k + 1], gam[:, k:k + 1],
                                            ALU.is_gt, ALU.mult).then_inc(quant, 1)
                    nc.vector.tensor_scalar(down[:, k, :], wm[:, k, :], neg[:, k:k + 1], gam[:, k:k + 1],
                                            ALU.is_lt, ALU.mult).then_inc(quant, 1)
                dve.wait_ge(quant, 15)
                nc.vector.tensor_tensor(up, up, down, ALU.subtract).then_inc(quant, 1)
                dve.wait_ge(quant, 16)
                nc.vector.tensor_tensor(up, up, wm, ALU.subtract).then_inc(quant, 1)
                dve.wait_ge(quant, 17)
                nc.vector.tensor_tensor(wm, wm, up, ALU.add).then_inc(quant, 1)

            def layer3(s):
                def slot(v, r, b, on):
                    par = r % 2
                    for i in range(4):
                        tiles = [(h, qt) for h in M_HEADS[i] for qt in range(NT)] if on["m"] else []
                        if i == 0 and on["m"]:
                            wait(dve, max3_split, v)
                        for kt in range(NT):
                            for h, qt in tiles[len(tiles) * kt // 4:len(tiles) * (kt + 1) // 4]:
                                dve.wait_ge(mx3_full, 16 * (v + 1) + 4 * h + qt + 1)
                                nc.vector.tensor_reduce(mx[:, 1 - par, 0, qt, h:h + 1], MX[qt % 2][:, 0:P * (qt + 1)],
                                                        AX.X, ALU.max).then_inc(mx3_red, 1)
                            at = (i, kt)
                            if on["v"] and at in ((0, 3), (1, 1)):
                                values_out(v, r, b, par, i, on)
                            if i == 1 and on["tail"]:
                                invert(v - 1, 1, kt)
                            if i == 3 and on["b"]:
                                invert(v, 0, kt)
                            if on["a"]:
                                if at in ((2, 0), (3, 0)):
                                    low_part(v, r, 0, i - 2)
                                if at in ((3, 2), (3, 3)):
                                    low_part(v, r, 1, kt - 2)
                            if r == 0 and on["op"] and at in ((2, 2), (3, 1)):
                                add_out(b - 1, i - 2)
                        if i == 2 and r == 1 and on["ln"]:
                            norm_ctx(b + 1)
                        if i == 0 and r == 2 and on["a"] and on["b"]:
                            norm_x(b + 1)

                def values_out(v, r, b, par, j, on):
                    if on["tail"] and j == 0:
                        dve.wait_ge(pv3_done, 4 * v)
                    dve.wait_ge(la3_full, job3(v, r, b, "v", j) + 1)
                    nc.vector.tensor_copy(V3[:, 1 - par, 2 * j:2 * j + 2, :, :],
                                          LAt[:, :, :].rearrange("p t (h d) -> p t h d", h=G)).then_inc(la3_free, 1)

                def invert(v, j, quarter):
                    if quarter == 0:
                        dve.wait_ge(ov3_evac, EVACS * (2 * v + j + 1))
                    part = sums[:, j, P * quarter:P * quarter + P]
                    nc.vector.reciprocal(part, part).then_inc(rc3_done, 1)

                def add_out(b, j):
                    dve.wait_ge(op3_full, 2 * b + j + 1)
                    add_to_x(b, j, LBt, op3_evac)

                def low_part(v, r, bl, kind):
                    dve.wait_ge(hi3_done, 2 * (2 * (v + 2) + bl) + kind + 1)
                    at = (C_K3, C_Q3)[kind] + 2 * ((r + 2) % R3) + bl
                    nc.vector.scalar_tensor_tensor(lo[:, kind, :], LA[:, :], cols[:, at:at + 1], hi[:, kind, :].bitcast(F32),
                                                   ALU.add, ALU.subtract).then_inc(la3_free, 1)

                def norm_ctx(b):
                    dve.wait_ge(ctx_rows_loaded, 16 * (b + 1))
                    layer_norm(norm3(b, 0), lambda t: XH[:, t, :])

                def norm_x(b):
                    layer_norm_x(norm3(b, 1), b)

                nc.vector.tensor_copy(columns3, cols[:, C_V:C_V + 8].rearrange("p (k a) -> p k a", a=1).broadcast_to([P, 8, P])
                                      ).then_inc(bias3, 1)
                dve.wait_ge(bias3, 2)
                row = brow[:, SELF3 % 2, 1, :]
                nc.vector.tensor_tensor(row, LB[:, 0:E], row, ALU.add).then_inc(bias3, 1)
                norm_ctx(0)
                norm_x(0)
                run_slots3(dve, slot)

            dve.wait_ge(consts_in, 48)
            for n, done in enumerate((op_full, op_evac, op3_evac, at_ready)):
                nc.vector.memset(qst[:, n:n + 1], 0.0).then_inc(done, BASE)
            nc.vector.tensor_copy(identr[:, :], ident[:, :]).then_inc(shapes_done, 1)
            nc.vector.tensor_copy(shpb[:, :], shp).then_inc(shapes_done, 1)
            dve.wait_ge(x_loaded, 32)
            dve.wait_ge(shapes_done, 2)
            def prepare(s):
                dve.wait_ge(brow_in[s % 2], brow_count(s))
                if s == CROSS1:
                    quantize()
                    dve.wait_ge(quant, QUANT_STEPS)
                scale_queries(s, W[s % 2][:, 0:512], HD)
                if addmask_of(s):
                    dve.wait_ge(masks_loaded, 32)
                    nc.vector.tensor_copy(mask_hi, mask_k).then_inc(mask_split, 1)
                    dve.wait_ge(mask_split, 1)
                    nc.vector.tensor_tensor(mask_lo, mask_k, mask_hi.bitcast(F32), ALU.subtract).then_inc(mask_split, 1)

            for s in range(8):
                if s not in JOINED:
                    wait(dve, x_done, NB * s)
                if s in ATTN:
                    if s not in JOINED:
                        prepare(s)
                    attention(s)
                elif s in MLP_NO:
                    dve.wait_ge(brow_in[s % 2], brow_count(s))
                    mlp(s)
                else:
                    dve.wait_ge(brow_in[s % 2], brow_count(s))
                    scale_queries(s, W[s % 2][:, 0:2048], HS)
                    layer3(s)

        @block.gpsimd
        def _(pool):
            def layer_norm(N, rows, turned=None, turned_at=0):
                waits(pool, (ln_mv, NT * (N + 1)),
                      (xh_ready, N), apart=True)
                nc.gpsimd.tensor_scalar(rstd[:, 0, :], mv[:, :, 1], EPS, None, ALU.add).then_inc(ln_pool, 1)
                pool.wait_ge(ln_pool, 3 * N + 1)
                nc.gpsimd.tensor_tensor(rstd[:, 1, :], rstd[:, 0, :], mhalf[:, :], ALU.pow).then_inc(ln_pool, 1)
                pool.wait_ge(ln_pool, 3 * N + 2)
                if turned is not None:
                    wait(pool, turned, turned_at)
                nc.gpsimd.tensor_tensor(XH[:, :, :], rows, mv[:, :, 0:1].broadcast_to([P, NT, E]),
                                        ALU.subtract).then_inc(ln_pool, 1)
                pool.wait_ge(ln_pool, 3 * N + 3)
                nc.gpsimd.tensor_tensor(XH[:, :, :], XH[:, :, :], rstd[:, 1, :].rearrange("p (t a) -> p t a", a=1).broadcast_to([P, NT, E]),
                                        ALU.mult).then_inc(xh_ready, 1)

            def add_bias(s, b):
                bias = brow[:, s % 2, 1:2, :].broadcast_to([P, NT, E])
                nc.gpsimd.tensor_tensor(xt(b, 0, NT), xt(b, 0, NT), bias, ALU.add).then_inc(x_done, 1)

            def split_max(half, g, hi_sem, lo_sem, at):
                nc.gpsimd.tensor_copy(mhl[:, half, g, :, 0:G], mx[:, half, g, :, :]).then_inc(hi_sem, 1)
                pool.wait_ge(hi_sem, at + 1)
                nc.gpsimd.tensor_tensor(mhl[:, half, g, :, G:2 * G], mx[:, half, g, :, :],
                                        mhl[:, half, g, :, 0:G].bitcast(F32), ALU.subtract).then_inc(lo_sem, 1)

            def attention(s):
                n = ATTN_NO[s]

                def slot(u, c, b, p, on):
                    half = c % 2
                    U, GB = UNITS * n + u, NB * n + b
                    if on["b"]:
                        maxima(U, half, 1)
                    if half == 0 and on["a"]:
                        sa, ba = a_of(s, u, b)
                        layer_norm(NB * sa + ba, xt(ba, 0, NT), la_full, JOBS * GB + 2)
                    if on["m"]:
                        maxima(U + 1, 1 - half, 0)
                    if on["tail"]:
                        pool.wait_ge(recip_done, 4 * U)
                        nc.gpsimd.tensor_tensor(raw[:, 1 - half, :], raw[:, 1 - half, :], sums[:, 1 - half, :],
                                                ALU.mult).then_inc(at_ready, 1)
                    if half == 0 and on["op"]:
                        pool.wait_ge(op_evac, BASE + 2 * GB)
                        add_bias(*end_of(s, u, b))

                def maxima(U, half, g):
                    waits(pool, (mx_red, 32 * U + 16 * (g + 1)),
                          (mt_full, 2 * (U - 2) + g + 1), apart=True)
                    split_max(half, g, max_hi, max_split, 2 * U + g)

                run_slots(pool, s, slot)

            def mlp(s):
                m = MLP_NO[s]

                def batch(b, more):
                    if more:
                        layer_norm(NB * s + b + 1, xt(b + 1, 0, NT), ml_full, 2 * (NB * m + b + 1))
                    pool.wait_ge(pr_evac, 2 * (NB * m + b + 1))
                    add_bias(s, b)

                layer_norm(NB * s, xt(0, 0, NT))
                batch(0, True)
                with pool.Fori(1, NB - 1) as b:
                    batch(b, True)
                batch(NB - 1, False)

            def layer3(s):
                def slot(v, r, b, on):
                    par = r % 2
                    if r == 2 and on["a"]:
                        layer_norm(norm3(b + 1, 1), xt(b + 1, 0, NT), la3_full, job3(v, r, b, "tc", 1) + 1)
                    if on["tail"]:
                        normalize(v - 1, (r - 1) % R3, 1)
                    if on["m"]:
                        waits(pool, (mx3_red, 16 * (v + 2)),
                              (mt3_full, v), apart=True)
                        split_max(1 - par, 0, max3_hi, max3_split, v + 1)
                    if r == 1 and on["ln"]:
                        layer_norm(norm3(b + 1, 0), XH[:, :, :])
                    if r == 0 and on["op"]:
                        pool.wait_ge(op3_evac, BASE + 2 * b)
                        add_bias(s, b - 1)
                    if on["b"]:
                        normalize(v, r, 0)

                def normalize(v, r, j):
                    pool.wait_ge(rc3_done, 8 * v + 4 * (j + 1))
                    pair = AT3[:, 2 * r + j, :]
                    nc.gpsimd.tensor_tensor(pair, pair, sums[:, j, :], ALU.mult).then_inc(at3_ready, 1)

                nc.gpsimd.memset(ones3, 1.0).then_inc(stack3_ones, 1)
                for par in range(2):
                    pool.wait_ge(stack3_ones, par + 1)
                    nc.gpsimd.memset(stk[HS:P, 16 * par + 12:16 * par + 16, :].bitcast(F32), -1.0).then_inc(stack3_ones, 1)
                pool.wait_ge(stack3_ones, 3)
                layer_norm(norm3(0, 0), XH[:, :, :])
                pool.wait_ge(bias3, 3)
                run_slots3(pool, slot)

            def columns_of_one():
                ones_at = Vh[:, :, :, :, :].rearrange("p a t h (d two) -> p (a t h) d two", two=2)[:, :, :, 1]
                nc.gpsimd.memset(ones_at, 1.0).then_inc(v_ones, 1)

            nc.gpsimd.memset(mhalf[:, :], -0.5).then_inc(pool_init, 1)
            for half in range(2):
                lo_p = 64 * half + 32
                pool.wait_ge(pool_init, half + 1)
                nc.gpsimd.memset(stk[lo_p:lo_p + 32, 8:16, :].bitcast(F32), -1.0).then_inc(pool_init, 1)
            pool.wait_ge(pool_init, 3)
            columns_of_one()
            pool.wait_ge(v_ones, 1)
            pool.wait_ge(consts_in, 48)
            nc.gpsimd.tensor_scalar(cols[:, C_Q:C_Q + 10], cols[:, C_Q:C_Q + 10], HD ** -0.5, None, ALU.mult).then_inc(pool_init, 1)
            pool.wait_ge(pool_init, 4)
            nc.gpsimd.tensor_scalar(cols[:, C_Q3:C_Q3 + 8], cols[:, C_Q3:C_Q3 + 8], HS ** -0.5, None, ALU.mult).then_inc(pool_init, 1)
            pool.wait_ge(pool_init, 5)
            pool.wait_ge(x_loaded, 32)
            nc.gpsimd.memset(qst[:, 12:16], 0.0).then_inc(pool_ready, 1)
            for s in range(8):
                if s not in JOINED:
                    wait(pool, x_done, NB * s)
                if s in ATTN:
                    if s == CROSS1:
                        nc.gpsimd.memset(ones, 1.0).then_inc(ones_set, 1)
                        pool.wait_ge(ones_set, 1)
                        columns_of_one()
                        pool.wait_ge(v_ones, 2)
                    attention(s)
                elif s in MLP_NO:
                    mlp(s)
                else:
                    layer3(s)


ATTN_NAMES = {SELF0: ("L0_xattn_ln1_g", "L0_xattn_ln1_b", None, "L0_xattn_attn_proj_w", None, "L0_xattn_attn_proj_b"),
              CROSS0: ("L0_xattn_ln2_g", "L0_xattn_ln2_b", ("L0_xattn_q_w", "L0_xattn_k_w", "L0_xattn_v_w"),
                       "L0_xattn_ca_proj_w", ("L0_xattn_q_b", "L0_xattn_k_b", "L0_xattn_v_b"), "L0_xattn_ca_proj_b"),
              CROSS1: ("L1_xattn_ln_gamma", "L1_xattn_ln_beta", ("L1_xattn_Wq", "L1_xattn_Wk", "L1_xattn_Wv"),
                       "L1_xattn_Wo", ("L1_xattn_bq", "L1_xattn_bk", "L1_xattn_bv"), "L1_xattn_bo"),
              SELF2: ("L2_xattn_attn_ln_w", "L2_xattn_attn_ln_b", ("L2_xattn_q_w", "L2_xattn_k_w", "L2_xattn_v_w"),
                      "L2_xattn_o_w", ("L2_xattn_q_b", None, "L2_xattn_v_b"), "L2_xattn_o_b"),
              CROSS2: ("L2_xattn_cross_ln_w", "L2_xattn_cross_ln_b", ("L2_xattn_cq_w", "L2_xattn_ck_w", "L2_xattn_cv_w"),
                       "L2_xattn_co_w", ("L2_xattn_cq_b", None, "L2_xattn_cv_b"), "L2_xattn_co_b")}
MLP_NAMES = {MLP0: ("L0_xattn_ln3_g", "L0_xattn_ln3_b", "L0_xattn_fc_w", "L0_xattn_fc_b", "L0_xattn_proj_w", "L0_xattn_proj_b"),
             MLP2: ("L2_xattn_mlp_ln_w", "L2_xattn_mlp_ln_b", "L2_xattn_fc1_w", "L2_xattn_fc1_b", "L2_xattn_fc2_w",
                    "L2_xattn_fc2_b")}


def by_partition(w):
    return w.reshape(-1, P, w.shape[1]).transpose(1, 0, 2).reshape(P, -1)


def head_order():
    return np.arange(E).reshape(2, 2, G, HD).transpose(0, 1, 3, 2).reshape(-1)


def head_order3():
    return np.arange(H * HS).reshape(H // 2, 2, HS).transpose(0, 2, 1).reshape(-1)


def kernel(**inputs):
    import concourse.bacc as bacc
    from concourse.bass_utils import run_bass_kernel_spmd

    a = {k: np.asarray(v) for k, v in inputs.items()}
    zero = np.zeros(E, np.float32)
    order, order3 = head_order(), head_order3()
    weights, cols, rows = [None] * 8, np.zeros((P, N_COLS), np.float32), np.zeros((N_ROWS, E), np.float32)

    def put(at, vector):
        cols[:, at:at + vector.size // P] = vector.reshape(-1, P).T

    for s, (g, o, qkv, wo, qkv_b, bo) in ATTN_NAMES.items():
        if qkv is None:
            q_w, k_w, v_w = np.split(a["L0_xattn_attn_qkv_w"], 3)
            q_b, k_b, v_b = np.split(a["L0_xattn_attn_qkv_b"], 3)
        else:
            q_w, k_w, v_w = (a[x] for x in qkv)
            q_b, k_b, v_b = (zero if x is None else a[x] for x in qkv_b)
        weights[s] = np.concatenate([by_partition(q_w[order].T), by_partition(k_w[order].T), by_partition(v_w.T),
                                     by_partition(a[wo].T)], axis=1)
        put(C_Q + 2 * ATTN_NO[s], q_b[order])
        put(C_K + 2 * ATTN_NO[s], k_b[order])
        rows[R_V + ATTN_NO[s]], rows[R_O + s] = v_b, a[bo]
        put(C_G + 2 * s, a[g])
        put(C_B + 2 * s, a[o])
    for s, (g, o, fw, fb, pw, pb_) in MLP_NAMES.items():
        weights[s] = np.concatenate([by_partition(a[fw].T), by_partition(a[pw].T)], axis=1)
        put(C_F + NF * MLP_NO[s], a[fb])
        rows[R_O + s] = a[pb_]
        put(C_G + 2 * s, a[g])
        put(C_B + 2 * s, a[o])
    k3, v3 = np.split(a["L3_xattn_wkv"], 2, axis=1)
    kb3, vb3 = np.split(a["L3_xattn_bkv"], 2)
    weights[SELF3] = np.concatenate([by_partition(a["L3_xattn_wq"][:, order3]), by_partition(k3[:, order3]),
                                     by_partition(v3), by_partition(a["L3_xattn_wo"])], axis=1)
    put(C_Q3, a["L3_xattn_bq"][order3])
    put(C_K3, kb3[order3])
    put(C_V, vb3)
    rows[R_O + SELF3] = a["L3_xattn_bo"]
    put(C_G + 2 * SELF3, a["L3_xattn_ln_g"])
    put(C_B + 2 * SELF3, a["L3_xattn_ln_b"])

    later = np.triu(np.full((P, P), NEG, np.float32), 1)
    arrays = {
        "x_t": a["x"].reshape(NB * NT, P, E).transpose(1, 0, 2),
        "ctx_t": a["ctx_1024"].transpose(2, 0, 1).reshape(NC, P, NB, S).transpose(1, 2, 0, 3).reshape(P, NB * NC, S),
        "ctx_rows": a["ctx_1024"].reshape(NB * NT, P, E).transpose(1, 0, 2),
        "masks": np.concatenate([m.reshape(NT, P, S).transpose(1, 0, 2) for m in (a["mask_SxS_fc0"], a["mask_SxS_fc0"].T)], axis=1),
        "shapes": np.concatenate([np.eye(P, dtype=np.float32), later, later.T], axis=1),
        "cols": cols,
        "rows": rows,
        **{f"w{s}": w for s, w in enumerate(weights)},
    }
    arrays = {k: np.ascontiguousarray(v) for k, v in arrays.items()}
    nc = bacc.Bacc("TRN2", target_bir_lowering=False, num_devices=1)
    aps = {k: nc.dram_tensor("in_" + k, v.shape, F32, kind="ExternalInput").ap() for k, v in arrays.items()}
    out = nc.dram_tensor("out_x", (P, NB * NT, E), F32, kind="ExternalOutput").ap()
    program(nc, aps["x_t"], aps["ctx_t"], aps["ctx_rows"], aps["masks"], aps["shapes"], aps["cols"], aps["rows"],
            [aps[f"w{s}"] for s in range(8)], out)
    r = run_bass_kernel_spmd(nc, [{"in_" + k: v for k, v in arrays.items()}], core_ids=[0])
    return r.results[0]["out_x"].transpose(1, 0, 2).reshape(NB, S, E)
```
